# Optimizing a Trainium2 kernel written in Bass

```python
import numpy as np
import jax
import jax.numpy as jnp

def _softmax(x, axis=-1):
    return jax.nn.softmax(x, axis=axis)

def _gelu(x):
    return jax.nn.gelu(x, approximate=True)

def _silu(x):
    return jax.nn.silu(x)

def _sigmoid(x):
    return jax.nn.sigmoid(x)

def _layernorm(x, axis=-1, eps=1e-05):
    m = jnp.mean(x, axis=axis, keepdims=True)
    v = jnp.var(x, axis=axis, keepdims=True)
    return (x - m) / jnp.sqrt(v + eps)

def _scatter_add(tgt, idx, src, axis=0):
    return tgt.at[idx].add(src)

def _segment_sum(src, seg, n):
    return jax.ops.segment_sum(src, seg, n)
kernel_name = 'mk_decoder_preln_d2_seqx_r4_569f78'

def setup_inputs(seed: int=0):
    np.random.seed(seed)
    _w = jnp.asarray

    def _rec_inputs():
        import jax
        import jax.numpy as jnp
        _rk = jax.random.key(seed)
        x = 2.818e-05 + 1 * jax.random.normal(jax.random.fold_in(_rk, 1), (8, 256, 256), jnp.float32)
        _lenS = 256 - jax.random.randint(jax.random.fold_in(_rk, 7), (8,), 0, max(1, 256 // 4) + 1, jnp.int32)
        _lenS2 = 256 - jax.random.randint(jax.random.fold_in(_rk, 8), (8,), 0, max(1, 256 // 4) + 1, jnp.int32)
        _ctx_2048P = jax.random.normal(jax.random.fold_in(_rk, 11), (8, 16, 512), jnp.float32)
        _ctx_2048c = jax.random.dirichlet(jax.random.fold_in(_rk, 511), 0.3 * jnp.ones((16,), jnp.float32), (8, 256))
        _ctx_2048t = jnp.einsum('bsk,bkd->bsd', _ctx_2048c, _ctx_2048P)
        _ctx_2048t = _ctx_2048t * jax.lax.rsqrt(jnp.mean(jnp.square(_ctx_2048t)) + 1e-12) * 0.953939
        ctx_2048 = -0.000125008 + 0.999885 * (_ctx_2048t + 0.3 * jax.random.normal(jax.random.fold_in(_rk, 611), (8, 256, 512), jnp.float32))
        _validS = jnp.arange(256)[None, :] < _lenS[:, None]
        _validS2 = jnp.arange(256)[None, :] < _lenS2[:, None]
        _causal = jnp.tril(jnp.ones((256, 256), dtype=bool))
        mask_BxS2_fk1 = jnp.where(jnp.broadcast_to(_validS2[:, :], (8, 256)), 1.0, 0.0).astype(jnp.float32)
        mask_BxS2_if0 = jnp.where(jnp.ones((8, 256), dtype=bool), 4, 0).astype(jnp.int32)
        return (x, ctx_2048, mask_BxS2_fk1, mask_BxS2_if0)
    x, ctx_2048, mask_BxS2_fk1, mask_BxS2_if0 = _rec_inputs()

    def _L0_attn_setup():
        import jax, jax.numpy as jnp
        import numpy as np
        D_MODEL = 256
        STATE_DIM = 256
        LN_EPS = 1e-05

        def _layernorm(x, w, b):
            mu = jnp.mean(x, axis=-1, keepdims=True)
            var = jnp.mean(jnp.square(x - mu), axis=-1, keepdims=True)
            return (x - mu) * jax.lax.rsqrt(var + LN_EPS) * w + b

        def _diag_scan(alpha, u):

            def combine(e1, e2):
                a1, b1 = e1
                a2, b2 = e2
                return (a2 * a1, a2 * b1 + b2)
            _, h = jax.lax.associative_scan(combine, (alpha, u), axis=1)
            return h
        key = jax.random.key(seed)
        ks = jax.random.split(key, 8)
        x = jax.random.normal(ks[0], (4, 1024, D_MODEL), dtype=jnp.float32)
        W_alpha_w = jax.random.normal(ks[1], (STATE_DIM, D_MODEL), dtype=jnp.float32) * 0.01
        W_alpha_b = jnp.full((STATE_DIM,), 2.0, dtype=jnp.float32)
        W_B_w = jax.random.normal(ks[2], (STATE_DIM, D_MODEL), dtype=jnp.float32) * 0.02
        W_B_b = jnp.zeros((STATE_DIM,), dtype=jnp.float32)
        W_C_w = jax.random.normal(ks[3], (D_MODEL, STATE_DIM), dtype=jnp.float32) * 0.02
        W_C_b = jnp.zeros((D_MODEL,), dtype=jnp.float32)
        D_param = jax.random.normal(ks[4], (D_MODEL,), dtype=jnp.float32) * 0.01
        ln_w = jnp.ones((D_MODEL,), dtype=jnp.float32)
        ln_b = jnp.zeros((D_MODEL,), dtype=jnp.float32)
        return {'x': x, 'W_alpha_w': W_alpha_w, 'W_alpha_b': W_alpha_b, 'W_B_w': W_B_w, 'W_B_b': W_B_b, 'W_C_w': W_C_w, 'W_C_b': W_C_b, 'D_param': D_param, 'ln_w': ln_w, 'ln_b': ln_b}
    _L0_attn_all = _L0_attn_setup()
    _L0_attn_in = {k: v for k, v in _L0_attn_all.items() if k in ('W_alpha_w', 'W_alpha_b', 'W_B_w', 'W_B_b', 'W_C_w', 'W_C_b', 'D_param', 'ln_w', 'ln_b')}
    del _L0_attn_all

    def _L0_xattn_setup():
        import jax, jax.numpy as jnp
        import numpy as np
        B, S, T = (32, 128, 128)
        SRC_SIZE, TGT_SIZE, OUT_SIZE, NUM_HEAD = (512, 256, 256, 8)
        HEAD_DIM = OUT_SIZE // NUM_HEAD
        key = jax.random.key(seed)
        ks = jax.random.split(key, 12)
        src = jax.random.normal(ks[0], (B, S, SRC_SIZE), dtype=jnp.float32)
        tgt = jax.random.normal(ks[1], (B, T, TGT_SIZE), dtype=jnp.float32)
        src_mask = (jax.random.uniform(ks[2], (B, S)) > 0.3).astype(jnp.float32)
        src_mask = src_mask.at[:, 0].set(1.0)
        tgt_mask = (jax.random.uniform(ks[3], (B, T)) > 0.3).astype(jnp.float32)
        tgt_mask = tgt_mask.at[:, 0].set(1.0)

        def lin(k, out_f, in_f):
            return jax.random.normal(k, (out_f, in_f), dtype=jnp.float32) / np.sqrt(in_f)
        W_src = lin(ks[4], 2 * OUT_SIZE, SRC_SIZE)
        b_src = jnp.zeros((2 * OUT_SIZE,), jnp.float32)
        W_tgt = lin(ks[5], OUT_SIZE, TGT_SIZE)
        b_tgt = jnp.zeros((OUT_SIZE,), jnp.float32)
        W_out = lin(ks[6], OUT_SIZE, OUT_SIZE + TGT_SIZE)
        b_out = jnp.zeros((OUT_SIZE,), jnp.float32)
        return {'src': src, 'tgt': tgt, 'src_mask': src_mask, 'tgt_mask': tgt_mask, 'W_src': W_src, 'b_src': b_src, 'W_tgt': W_tgt, 'b_tgt': b_tgt, 'W_out': W_out, 'b_out': b_out}
    _L0_xattn_all = _L0_xattn_setup()
    _L0_xattn_in = {k: v for k, v in _L0_xattn_all.items() if k in ('W_src', 'b_src', 'W_tgt', 'b_tgt', 'W_out', 'b_out')}
    del _L0_xattn_all

    def _L0_ffn_setup():
        import jax, jax.numpy as jnp
        import numpy as np
        B, T, C = (4, 512, 256)
        E = 8
        K = 2
        H = 352
        HS = 352 * 2
        key = jax.random.key(seed)
        k = jax.random.split(key, 8)
        s = 0.02
        return {'x': jax.random.normal(k[0], (B, T, C), jnp.float32), 'Wg': jax.random.normal(k[1], (C, E), jnp.float32) * s, 'W1': jax.random.normal(k[2], (E, C, H), jnp.float32) * s, 'W2': jax.random.normal(k[3], (E, C, H), jnp.float32) * s, 'W3': jax.random.normal(k[4], (E, H, C), jnp.float32) * s, 'Ws1': jax.random.normal(k[5], (C, HS), jnp.float32) * s, 'Ws2': jax.random.normal(k[6], (C, HS), jnp.float32) * s, 'Ws3': jax.random.normal(k[7], (HS, C), jnp.float32) * s}
    _L0_ffn_all = _L0_ffn_setup()
    _L0_ffn_in = {k: v for k, v in _L0_ffn_all.items() if k in ('Wg', 'W1', 'W2', 'W3', 'Ws1', 'Ws2', 'Ws3')}
    del _L0_ffn_all

    def _L1_attn_setup():
        import jax, jax.numpy as jnp
        import numpy as np
        N_HEADS = 16
        INPUT_DIM = 256
        EMBED_DIM = 256
        KEY_DIM = EMBED_DIM // N_HEADS
        BATCH = 4
        SEQ = 512

        def _uniform(key, shape, bound):
            return jax.random.uniform(key, shape, jnp.float32, -bound, bound)
        key = jax.random.key(seed)
        kq, k1, k2, k3, k4 = jax.random.split(key, 5)
        stdv_k = 1.0 / np.sqrt(KEY_DIM)
        stdv_e = 1.0 / np.sqrt(EMBED_DIM)
        return {'q': jax.random.normal(kq, (BATCH, SEQ, INPUT_DIM), jnp.float32), 'W_query': _uniform(k1, (N_HEADS, INPUT_DIM, KEY_DIM), stdv_k), 'W_key': _uniform(k2, (N_HEADS, INPUT_DIM, KEY_DIM), stdv_k), 'W_val': _uniform(k3, (N_HEADS, INPUT_DIM, KEY_DIM), stdv_k), 'W_out': _uniform(k4, (N_HEADS, KEY_DIM, EMBED_DIM), stdv_e)}
    _L1_attn_all = _L1_attn_setup()
    _L1_attn_in = {k: v for k, v in _L1_attn_all.items() if k in ('W_query', 'W_key', 'W_val', 'W_out')}
    del _L1_attn_all

    def _L1_xattn_setup():
        import jax, jax.numpy as jnp
        import numpy as np
        B, L, P = (4, 1024, 256)
        D_MODEL = 256
        D_GLOBAL = 512
        HEADDIM = 32
        EPSILON = 0.001
        RMS_EPS = 1e-05

        def rmsnorm(x, g, eps=RMS_EPS):
            var = jnp.mean(jnp.square(x), axis=-1, keepdims=True)
            return x * jax.lax.rsqrt(var + eps) * g

        def _hnet_depool(h, h_patch_full, patch_lens):
            h_patch = h_patch_full[..., :D_MODEL]
            bsz, plen = (h_patch.shape[0], h_patch.shape[1])
            seqlen = h.shape[1]
            logp = jnp.full((bsz, plen), -EPSILON, dtype=jnp.float32)
            bidx = jnp.cumsum(patch_lens, axis=1) - 1
            boundary_mask = jnp.zeros((bsz, seqlen), dtype=jnp.int32)
            boundary_mask = boundary_mask.at[jnp.arange(bsz)[:, None], bidx].set(1)
            dt = (-jnp.log(-jnp.expm1(logp))).astype(h_patch.dtype)
            x = h_patch / dt[..., None]
            n_heads = D_MODEL // HEADDIM
            A = -jnp.ones((n_heads,), dtype=jnp.float32)
            bcoef = jnp.exp(logp).astype(h_patch.dtype)
            x4 = x.reshape(bsz, plen, n_heads, HEADDIM)
            a = jnp.exp(dt[:, :, None] * A[None, None, :])
            u = (dt * bcoef)[:, :, None, None] * x4
            a_b = jnp.broadcast_to(a[..., None], u.shape)

            def comb(lft, rgt):
                aL, uL = lft
                aR, uR = rgt
                return (aL * aR, uL * aR + uR)
            _, s = jax.lax.associative_scan(comb, (a_b, u), axis=1)
            depool = s.reshape(bsz, plen, D_MODEL)
            plug = jnp.clip(jnp.cumsum(boundary_mask, axis=1) - 1, 0, plen - 1)
            depool_out = depool[jnp.arange(bsz)[:, None], plug]
            return depool_out + h
        key = jax.random.key(seed)
        k1, k2, k3, k4 = jax.random.split(key, 4)
        embeds = jax.random.normal(k1, (B, L, D_MODEL), dtype=jnp.float32)
        patch_embeds = jax.random.normal(k2, (B, P, D_GLOBAL), dtype=jnp.float32)
        patch_lens = jnp.full((B, P), L // P, dtype=jnp.int64)
        W_in = jax.random.normal(k3, (D_MODEL, D_MODEL), dtype=jnp.float32) * 0.02
        b_in = jnp.zeros((D_MODEL,), dtype=jnp.float32)
        g_res = jnp.ones((D_MODEL,), dtype=jnp.float32)
        g_init = jnp.ones((D_GLOBAL,), dtype=jnp.float32)
        return {'embeds': embeds, 'patch_embeds': patch_embeds, 'patch_lens': patch_lens, 'W_in': W_in, 'b_in': b_in, 'g_res': g_res, 'g_init': g_init}
    _L1_xattn_all = _L1_xattn_setup()
    _L1_xattn_in = {k: v for k, v in _L1_xattn_all.items() if k in ('W_in', 'b_in', 'g_res', 'g_init')}
    del _L1_xattn_all

    def _L1_ffn_setup():
        import jax, jax.numpy as jnp
        import numpy as np
        QMAX = 127.0

        def _ste_round(v):
            return v + jax.lax.stop_gradient(jnp.round(v) - v)

        def _act_fake_quant(x, clip_factor):
            scale = jax.nn.sigmoid(clip_factor) * jnp.max(jnp.abs(x)) / QMAX
            return jnp.clip(_ste_round(x / scale), -QMAX - 1.0, QMAX) * scale

        def _weight_fake_quant(w):
            scale = jnp.max(jnp.abs(w), axis=1, keepdims=True) / QMAX
            return jnp.clip(_ste_round(w / scale), -QMAX - 1.0, QMAX) * scale
        key = jax.random.key(seed)
        k1, k2, k3, k4 = jax.random.split(key, 4)
        B, S, H, I = (8, 2048, 256, 704)
        return {'x': jax.random.normal(k1, (B, S, H), dtype=jnp.float32), 'clip_x': jnp.full((1,), 4.0, dtype=jnp.float32), 'clip_down': jnp.full((1,), 4.0, dtype=jnp.float32), 'w_gate': jax.random.normal(k2, (I, H), dtype=jnp.float32) * 0.02, 'w_up': jax.random.normal(k3, (I, H), dtype=jnp.float32) * 0.02, 'w_down': jax.random.normal(k4, (H, I), dtype=jnp.float32) * 0.02}
    _L1_ffn_all = _L1_ffn_setup()
    _L1_ffn_in = {k: v for k, v in _L1_ffn_all.items() if k in ('clip_x', 'clip_down', 'w_gate', 'w_up', 'w_down')}
    del _L1_ffn_all
    return {'x': x, 'ctx_2048': ctx_2048, 'mask_BxS2_fk1': mask_BxS2_fk1, 'mask_BxS2_if0': mask_BxS2_if0, 'L0_attn_W_alpha_w': _L0_attn_in['W_alpha_w'], 'L0_attn_W_alpha_b': _L0_attn_in['W_alpha_b'], 'L0_attn_W_B_w': _L0_attn_in['W_B_w'], 'L0_attn_W_B_b': _L0_attn_in['W_B_b'], 'L0_attn_W_C_w': _L0_attn_in['W_C_w'], 'L0_attn_W_C_b': _L0_attn_in['W_C_b'], 'L0_attn_D_param': _L0_attn_in['D_param'], 'L0_attn_ln_w': _L0_attn_in['ln_w'], 'L0_attn_ln_b': _L0_attn_in['ln_b'], 'L0_xattn_W_src': _L0_xattn_in['W_src'], 'L0_xattn_b_src': _L0_xattn_in['b_src'], 'L0_xattn_W_tgt': _L0_xattn_in['W_tgt'], 'L0_xattn_b_tgt': _L0_xattn_in['b_tgt'], 'L0_xattn_W_out': _L0_xattn_in['W_out'], 'L0_xattn_b_out': _L0_xattn_in['b_out'], 'L0_ffn_Wg': _L0_ffn_in['Wg'], 'L0_ffn_W1': _L0_ffn_in['W1'], 'L0_ffn_W2': _L0_ffn_in['W2'], 'L0_ffn_W3': _L0_ffn_in['W3'], 'L0_ffn_Ws1': _L0_ffn_in['Ws1'], 'L0_ffn_Ws2': _L0_ffn_in['Ws2'], 'L0_ffn_Ws3': _L0_ffn_in['Ws3'], 'L1_attn_W_query': _L1_attn_in['W_query'], 'L1_attn_W_key': _L1_attn_in['W_key'], 'L1_attn_W_val': _L1_attn_in['W_val'], 'L1_attn_W_out': _L1_attn_in['W_out'], 'L1_xattn_W_in': _L1_xattn_in['W_in'], 'L1_xattn_b_in': _L1_xattn_in['b_in'], 'L1_xattn_g_res': _L1_xattn_in['g_res'], 'L1_xattn_g_init': _L1_xattn_in['g_init'], 'L1_ffn_clip_x': _L1_ffn_in['clip_x'], 'L1_ffn_clip_down': _L1_ffn_in['clip_down'], 'L1_ffn_w_gate': _L1_ffn_in['w_gate'], 'L1_ffn_w_up': _L1_ffn_in['w_up'], 'L1_ffn_w_down': _L1_ffn_in['w_down']}

def reference(x, ctx_2048, mask_BxS2_fk1, mask_BxS2_if0, L0_attn_W_alpha_w, L0_attn_W_alpha_b, L0_attn_W_B_w, L0_attn_W_B_b, L0_attn_W_C_w, L0_attn_W_C_b, L0_attn_D_param, L0_attn_ln_w, L0_attn_ln_b, L0_xattn_W_src, L0_xattn_b_src, L0_xattn_W_tgt, L0_xattn_b_tgt, L0_xattn_W_out, L0_xattn_b_out, L0_ffn_Wg, L0_ffn_W1, L0_ffn_W2, L0_ffn_W3, L0_ffn_Ws1, L0_ffn_Ws2, L0_ffn_Ws3, L1_attn_W_query, L1_attn_W_key, L1_attn_W_val, L1_attn_W_out, L1_xattn_W_in, L1_xattn_b_in, L1_xattn_g_res, L1_xattn_g_init, L1_ffn_clip_x, L1_ffn_clip_down, L1_ffn_w_gate, L1_ffn_w_up, L1_ffn_w_down):
    import jax
    import jax.numpy as jnp

    def _L0_attn_ref(x, W_alpha_w, W_alpha_b, W_B_w, W_B_b, W_C_w, W_C_b, D_param, ln_w, ln_b):
        import jax, jax.numpy as jnp
        import numpy as np
        D_MODEL = 256
        STATE_DIM = 256
        LN_EPS = 1e-05

        def _layernorm(x, w, b):
            mu = jnp.mean(x, axis=-1, keepdims=True)
            var = jnp.mean(jnp.square(x - mu), axis=-1, keepdims=True)
            return (x - mu) * jax.lax.rsqrt(var + LN_EPS) * w + b

        def _diag_scan(alpha, u):

            def combine(e1, e2):
                a1, b1 = e1
                a2, b2 = e2
                return (a2 * a1, a2 * b1 + b2)
            _, h = jax.lax.associative_scan(combine, (alpha, u), axis=1)
            return h
        residual = x
        xn = _layernorm(x, ln_w, ln_b)
        alpha = jax.nn.sigmoid(jnp.einsum('btd,nd->btn', xn, W_alpha_w) + W_alpha_b)
        u = jnp.einsum('btd,nd->btn', xn, W_B_w) + W_B_b
        h_all = _diag_scan(alpha, u)
        y = jnp.einsum('btn,dn->btd', h_all, W_C_w) + W_C_b + D_param * residual
        return y

    def _L0_xattn_ref(src, tgt, src_mask, tgt_mask, W_src, b_src, W_tgt, b_tgt, W_out, b_out):
        import jax, jax.numpy as jnp
        import numpy as np
        B, S, T = (32, 128, 128)
        SRC_SIZE, TGT_SIZE, OUT_SIZE, NUM_HEAD = (512, 256, 256, 8)
        HEAD_DIM = OUT_SIZE // NUM_HEAD
        b, s, _ = src.shape
        t = tgt.shape[1]
        src_trans = jnp.einsum('bsf,of->bso', src, W_src) + b_src
        tgt_trans = jnp.einsum('btf,of->bto', tgt, W_tgt) + b_tgt
        src_trans = src_trans * src_mask[:, :, None]
        tgt_trans = tgt_trans * tgt_mask[:, :, None]
        src_key, src_val = jnp.split(src_trans, 2, axis=2)
        k = src_key.reshape(b, s, NUM_HEAD, HEAD_DIM)
        v = src_val.reshape(b, s, NUM_HEAD, HEAD_DIM)
        q = tgt_trans.reshape(b, t, NUM_HEAD, HEAD_DIM)
        scores = jnp.einsum('bthd,bshd->bhts', q, k) / np.sqrt(HEAD_DIM)
        scores = jnp.where(src_mask[:, None, None, :] == 0, -jnp.inf, scores)
        attn = jax.nn.softmax(scores, axis=-1)
        tgt_update = jnp.einsum('bhts,bshd->bthd', attn, v).reshape(b, t, OUT_SIZE)
        cat_tgt = jnp.concatenate([tgt, tgt_update], axis=2)
        return jnp.einsum('btf,of->bto', cat_tgt, W_out) + b_out

    def _L0_ffn_ref(x, Wg, W1, W2, W3, Ws1, Ws2, Ws3):
        import jax, jax.numpy as jnp
        import numpy as np
        B, T, C = (4, 512, 256)
        E = 8
        K = 2
        H = 352
        HS = 352 * 2
        b, t, c = x.shape
        xf = x.reshape(-1, c)
        n = xf.shape[0]
        router = xf @ Wg
        top_logits, idx = jax.lax.top_k(router, K)
        probs = jax.nn.softmax(top_logits.astype(jnp.float32), axis=-1).astype(x.dtype)
        w = jnp.zeros((n, E), x.dtype).at[jnp.arange(n)[:, None], idx].add(probs)
        h = jax.nn.silu(jnp.einsum('tc,ech->eth', xf, W1)) * jnp.einsum('tc,ech->eth', xf, W2)
        y = jnp.einsum('eth,ehc,te->tc', h, W3, w)
        y = y.reshape(b, t, c)
        hs = jax.nn.silu(xf @ Ws1) * (xf @ Ws2)
        y = y + (hs @ Ws3).reshape(b, t, c)
        return y

    def _L1_attn_ref(q, W_query, W_key, W_val, W_out):
        import jax, jax.numpy as jnp
        import numpy as np
        N_HEADS = 16
        INPUT_DIM = 256
        EMBED_DIM = 256
        KEY_DIM = EMBED_DIM // N_HEADS
        BATCH = 4
        SEQ = 512

        def _uniform(key, shape, bound):
            return jax.random.uniform(key, shape, jnp.float32, -bound, bound)
        norm = 1.0 / np.sqrt(KEY_DIM)
        Q = jnp.einsum('bsd,hdk->hbsk', q, W_query)
        K = jnp.einsum('bsd,hdk->hbsk', q, W_key)
        V = jnp.einsum('bsd,hdv->hbsv', q, W_val)
        scores = norm * jnp.einsum('hbqk,hbnk->hbqn', Q, K)
        attn = jax.nn.softmax(scores, axis=-1)
        heads = jnp.einsum('hbqn,hbnv->hbqv', attn, V)
        out = jnp.einsum('hbqv,hve->bqe', heads, W_out)
        return out

    def _L1_xattn_ref(embeds, patch_embeds, patch_lens, W_in, b_in, g_res, g_init):
        import jax, jax.numpy as jnp
        import numpy as np
        B, L, P = (4, 1024, 256)
        D_MODEL = 256
        D_GLOBAL = 512
        HEADDIM = 32
        EPSILON = 0.001
        RMS_EPS = 1e-05

        def rmsnorm(x, g, eps=RMS_EPS):
            var = jnp.mean(jnp.square(x), axis=-1, keepdims=True)
            return x * jax.lax.rsqrt(var + eps) * g

        def _hnet_depool(h, h_patch_full, patch_lens):
            h_patch = h_patch_full[..., :D_MODEL]
            bsz, plen = (h_patch.shape[0], h_patch.shape[1])
            seqlen = h.shape[1]
            logp = jnp.full((bsz, plen), -EPSILON, dtype=jnp.float32)
            bidx = jnp.cumsum(patch_lens, axis=1) - 1
            boundary_mask = jnp.zeros((bsz, seqlen), dtype=jnp.int32)
            boundary_mask = boundary_mask.at[jnp.arange(bsz)[:, None], bidx].set(1)
            dt = (-jnp.log(-jnp.expm1(logp))).astype(h_patch.dtype)
            x = h_patch / dt[..., None]
            n_heads = D_MODEL // HEADDIM
            A = -jnp.ones((n_heads,), dtype=jnp.float32)
            bcoef = jnp.exp(logp).astype(h_patch.dtype)
            x4 = x.reshape(bsz, plen, n_heads, HEADDIM)
            a = jnp.exp(dt[:, :, None] * A[None, None, :])
            u = (dt * bcoef)[:, :, None, None] * x4
            a_b = jnp.broadcast_to(a[..., None], u.shape)

            def comb(lft, rgt):
                aL, uL = lft
                aR, uR = rgt
                return (aL * aR, uL * aR + uR)
            _, s = jax.lax.associative_scan(comb, (a_b, u), axis=1)
            depool = s.reshape(bsz, plen, D_MODEL)
            plug = jnp.clip(jnp.cumsum(boundary_mask, axis=1) - 1, 0, plen - 1)
            depool_out = depool[jnp.arange(bsz)[:, None], plug]
            return depool_out + h
        h = rmsnorm(embeds, g_res)
        h = jnp.einsum('bld,ed->ble', h, W_in) + b_in
        h_patch = rmsnorm(patch_embeds, g_init)
        return _hnet_depool(h, h_patch, patch_lens)

    def _L1_ffn_ref(x, clip_x, clip_down, w_gate, w_up, w_down):
        import jax, jax.numpy as jnp
        import numpy as np
        QMAX = 127.0

        def _ste_round(v):
            return v + jax.lax.stop_gradient(jnp.round(v) - v)

        def _act_fake_quant(x, clip_factor):
            scale = jax.nn.sigmoid(clip_factor) * jnp.max(jnp.abs(x)) / QMAX
            return jnp.clip(_ste_round(x / scale), -QMAX - 1.0, QMAX) * scale

        def _weight_fake_quant(w):
            scale = jnp.max(jnp.abs(w), axis=1, keepdims=True) / QMAX
            return jnp.clip(_ste_round(w / scale), -QMAX - 1.0, QMAX) * scale
        xq = _act_fake_quant(x, clip_x[0])
        gate = jnp.einsum('bsh,ih->bsi', xq, _weight_fake_quant(w_gate))
        up = jnp.einsum('bsh,ih->bsi', xq, _weight_fake_quant(w_up))
        h = _act_fake_quant(jax.nn.silu(gate) * up, clip_down[0])
        return jnp.einsum('bsi,hi->bsh', h, _weight_fake_quant(w_down))
    x = x + _L0_attn_ref(_layernorm(x, axis=-1), L0_attn_W_alpha_w, L0_attn_W_alpha_b, L0_attn_W_B_w, L0_attn_W_B_b, L0_attn_W_C_w, L0_attn_W_C_b, L0_attn_D_param, L0_attn_ln_w, L0_attn_ln_b)
    x = x + _L0_xattn_ref(ctx_2048, _layernorm(x, axis=-1), mask_BxS2_fk1, mask_BxS2_fk1, L0_xattn_W_src, L0_xattn_b_src, L0_xattn_W_tgt, L0_xattn_b_tgt, L0_xattn_W_out, L0_xattn_b_out)
    x = x + _L0_ffn_ref(_layernorm(x, axis=-1), L0_ffn_Wg, L0_ffn_W1, L0_ffn_W2, L0_ffn_W3, L0_ffn_Ws1, L0_ffn_Ws2, L0_ffn_Ws3)
    x = x + _L1_attn_ref(_layernorm(x, axis=-1), L1_attn_W_query, L1_attn_W_key, L1_attn_W_val, L1_attn_W_out)
    x = x + _L1_xattn_ref(_layernorm(x, axis=-1), ctx_2048, mask_BxS2_if0, L1_xattn_W_in, L1_xattn_b_in, L1_xattn_g_res, L1_xattn_g_init)
    x = x + _L1_ffn_ref(_layernorm(x, axis=-1), L1_ffn_clip_x, L1_ffn_clip_down, L1_ffn_w_gate, L1_ffn_w_up, L1_ffn_w_down)
    return x

_drawn_inputs = setup_inputs


def setup_inputs(seed=0):
    import zlib

    import numpy as np

    out = dict(_drawn_inputs(seed))
    spreads = {'L0_attn_W_alpha_b': (2.0, 0.2),
     'L0_attn_W_B_b': (0.0, 0.1),
     'L0_attn_W_C_b': (0.0, 0.1),
     'L0_attn_ln_w': (1.0, 0.2),
     'L0_attn_ln_b': (0.0, 0.1),
     'L0_xattn_b_src': (0.0, 0.1),
     'L0_xattn_b_tgt': (0.0, 0.52),
     'L0_xattn_b_out': (0.0, 0.1),
     'L1_xattn_b_in': (0.0, 0.1),
     'L1_xattn_g_res': (1.0, 0.2),
     'L1_xattn_g_init': (1.0, 0.2)}
    factors = {'L0_attn_W_alpha_w': 2.979,
     'L0_attn_D_param': 4.12,
     'L0_ffn_Wg': 3.924,
     'L0_ffn_W1': 3.432,
     'L0_ffn_W2': 3.427,
     'L0_ffn_W3': 3.405,
     'L1_ffn_w_gate': 3.948,
     'L1_ffn_w_up': 3.812,
     'L1_ffn_w_down': 3.822}
    for name, (base, spread) in spreads.items():
        noise = np.random.default_rng([zlib.crc32(name.encode()), seed]).standard_normal(out[name].shape)
        drawn = base * np.exp(spread * noise) if base else spread * noise
        out[name] = jnp.asarray(drawn.astype(out[name].dtype))
    for name, factor in factors.items():
        out[name] = (out[name] * factor).astype(out[name].dtype)
    return out
```

```python
from contextlib import ExitStack

import numpy as np
import concourse.bass as bass
from concourse import mybir

F32, F16, BF16, I32 = mybir.dt.float32, mybir.dt.float16, mybir.dt.bfloat16, mybir.dt.int32
ALU = mybir.AluOpType
ACT = mybir.ActivationFunctionType
AX = mybir.AxisListType.X
ds = bass.ds

P = 128
B, S, D, CD = 8, 256, 256, 512
T = B * S
NT = T // P
BLK = 512
NB = T // BLK
TB = BLK // P
KD, KC = D // P, CD // P
E, H = 8, 352
EA = E + 2
HCH = [(0, 128), (128, 128), (256, 96)]
NHC = len(HCH)
HS = 2 * H
QCH = [(0, 128), (128, 128), (256, 128), (384, 128), (512, 96), (608, 96)]
EPS = 1e-5
WS = 64.0
NEG = -60000.0
QMAX = 127.0
MAGIC = 1.5 * 2.0 ** 23

SW = {}
for _n, _k, _m in (("a", KD, D), ("b", KD, D), ("c", KD, D), ("src", KC, 2 * D), ("tgt", KD, D),
                   ("o", 2 * KD, D), ("q", KD, D), ("k", KD, D), ("v", KD, D), ("mo", 4, D),
                   ("in", KD, D), ("g", KD, E)):
    SW[_n] = (sum(k * m for _, k, m in SW.values()), _k, _m)
NSW = sum(k * m for _, k, m in SW.values())
NEW = 2 * KD * H + NHC * D

V_LNW, V_LNB, V_BA, V_BB, V_BTGT, V_BSRC, V_GRES = 0, 2, 4, 6, 8, 10, 12
R_BC, R_D, R_BV, R_BO, R_BIN, R_GI = range(6)

LOGP = np.float32(-0.001)
DT = float(-np.log(-np.expm1(LOGP)))


def weight(k, name, kc, part):
    off, _, m = SW[name]
    return k.sw[part][:, off + kc * m:off + (kc + 1) * m]


class Shared:
    pass


def wait(eng, sem, count):
    if not (isinstance(count, int) and count <= 0):
        eng.wait_ge(sem, count)


def peeled(eng, n, step):
    step(0)
    with eng.Fori(1, n) as i:
        step(i)


PASSES = ((0, 0), (0, 1), (1, 0))


def prepare(nc, k, a):
    with ExitStack() as ctx:
        stage = ctx.enter_context(nc.sbuf_tensor("stage", [P, NSW], F32))
        x_in, rest_in, stats = (ctx.enter_context(nc.semaphore(n)) for n in ("x_in", "rest_in", "stats"))
        w_in = [ctx.enter_context(nc.semaphore(f"w_in{i}")) for i in range(8)]
        high = ctx.enter_context(nc.semaphore("w_high"))
        low = ctx.enter_context(nc.semaphore("w_low"))
        made = ctx.enter_context(nc.semaphore("const_made"))
        block = ctx.enter_context(nc.Block())
        n = 8
        cuts = [NSW * i // n for i in range(n + 1)]

        @block.sync
        def _(sp):
            sp.dma_start(k.X[:], a["x"].rearrange("(n p) d -> p n d", p=P)).then_inc(x_in, 16)
            for lo, hi, piece_in in zip(cuts, cuts[1:], w_in):
                sp.dma_start(stage[:, lo:hi], a["sw"][:, lo:hi]).then_inc(piece_in, 16)
            sp.dma_start(k.vec[:], a["vec"]).then_inc(rest_in, 16)
            for r in range(6):
                sp.dma_start(k.rows[:, r, :], a["rows"][r:r + 1, :].to_broadcast([P, D])).then_inc(rest_in, 16)
            sp.wait_ge(rest_in, 16 * 7)

        @block.scalar
        def _(act):
            for i, (lo, hi) in enumerate(zip(cuts, cuts[1:])):
                act.wait_ge(w_in[i], 16)
                nc.scalar.activation(k.sw[0][:, lo:hi], stage[:, lo:hi], ACT.Copy, scale=WS).then_inc(high, 1)

        @block.vector
        def _(dve):
            nc.vector.memset(k.ones[:], 1.0)
            nc.vector.memset(k.ones16[:], 1.0)
            dve.wait_ge(x_in, 16)
            for t in range(NT):
                tile_stats(nc, k, t).then_inc(stats, 1)
            for i, (lo, hi) in enumerate(zip(cuts, cuts[1:])):
                dve.wait_ge(high, i + 1)
                nc.vector.scalar_tensor_tensor(k.sw[1][:, lo:hi], stage[:, lo:hi], WS, k.sw[0][:, lo:hi],
                                               ALU.mult, ALU.subtract).then_inc(low, 1)

        @block.gpsimd
        def _(pool):
            nc.gpsimd.memset(k.ident[:], 0.0).then_inc(made, 1)
            nc.gpsimd.memset(k.half[:], -0.5).then_inc(made, 1)
            pool.wait_ge(made, 1)
            nc.gpsimd.affine_select(out=k.ident[:], in_=k.ident[:], compare_op=ALU.not_equal, fill=1.0,
                                    base=0, pattern=[[-1, P]], channel_multiplier=1).then_inc(made, 1)
            pool.wait_ge(made, 3)
            nc.gpsimd.tensor_copy(k.identb[:], k.ident[:]).then_inc(made, 1)


def tile_stats(nc, k, t):
    return nc.vector.bn_stats(k.st[:, ds(t, 1), :], k.X[:, ds(t, 1), :])


def layer_stats(nc, k, tag, ctx, second):
    sem = lambda n: ctx.enter_context(nc.semaphore(f"{tag}_{n}"))
    s_aggr, k.s_rstd, k.s_fac = sem("aggr"), sem("rstd"), sem("fac")
    parts = (slice(0, TB), slice(TB, NT))

    def dve_part(dve):
        for t in range(NT):
            nc.vector.bn_aggr(k.mv[:, t, :], k.st[:, t, :]).then_inc(s_aggr, 1)

    def pool_part(pool):
        step = [0]

        def then(ins):
            step[0] += 1
            ins.then_inc(k.s_rstd, 1)
            pool.wait_ge(k.s_rstd, step[0])

        for ts in parts:
            r1, fac, var, half = k.r1[:, ts], k.fac[:, ts], k.mv[:, ts, 1], k.half[:, ts]
            pool.wait_ge(s_aggr, ts.stop)
            then(nc.gpsimd.tensor_scalar(r1, var, EPS, None, ALU.add))
            then(nc.gpsimd.tensor_tensor(r1, r1, half, ALU.pow))
            if not second:
                nc.gpsimd.tensor_copy(fac, r1).then_inc(k.s_fac, 1)
                continue
            then(nc.gpsimd.tensor_tensor(fac, r1, r1, ALU.mult))
            then(nc.gpsimd.tensor_tensor(fac, fac, var, ALU.mult))
            then(nc.gpsimd.tensor_scalar(fac, fac, EPS, None, ALU.add))
            then(nc.gpsimd.tensor_tensor(fac, fac, half, ALU.pow))
            nc.gpsimd.tensor_tensor(fac, fac, r1, ALU.mult).then_inc(k.s_fac, 1)

    return dve_part, pool_part


def normalise(nc, k, tag, second=False, w=None, b=None):
    with ExitStack() as ctx:
        sem = lambda n: ctx.enter_context(nc.semaphore(f"{tag}_{n}"))
        xn = ctx.enter_context(nc.sbuf_tensor(f"{tag}_xn", [P, NT, D], F32))
        full = ctx.enter_context(nc.sbuf_tensor(f"{tag}_full", [P, 2, KD, BLK], F32)) if b is not None else None
        dve_stats, pool_stats = layer_stats(nc, k, tag, ctx, second)
        s_xn, s_turned, s_full, s_high, s_low = sem("xn"), sem("turned"), sem("full"), sem("high"), sem("low")
        block = ctx.enter_context(nc.Block())
        high, low = ([part[:, :, i * BLK:(i + 1) * BLK] for i in range(NB)] for part in k.nT)

        def banks(i):
            return k.ps[:, 2 * (i % 2):2 * (i % 2) + KD, :]

        @block.vector
        def _(dve):
            def scaled(i):
                dve.wait_ge(k.s_fac, min(i, 1) + 1)
                for t in range(i * TB, (i + 1) * TB):
                    nc.vector.tensor_scalar(xn[:, t, :], k.X[:, t, :], k.mv[:, t, 0:1], k.fac[:, t:t + 1],
                                            ALU.subtract, ALU.mult).then_inc(s_xn, 1)

            def low_part(i):
                dve.wait_ge(s_high, KD * (i + 1))
                if b is not None:
                    nc.vector.tensor_tensor(low[i], full[:, i % 2], high[i], ALU.subtract).then_inc(s_low, KD)
                elif w is not None:
                    for c in range(KD):
                        nc.vector.scalar_tensor_tensor(low[i][:, c], banks(i)[:, c], k.vec[:, w + c:w + c + 1], high[i][:, c],
                                                       ALU.mult, ALU.subtract).then_inc(s_low, 1)
                else:
                    nc.vector.tensor_tensor(low[i], banks(i), high[i], ALU.subtract).then_inc(s_low, KD)

            dve_stats(dve)
            scaled(0)
            scaled(1)
            for i in range(2, NB):
                low_part(i - 2)
                scaled(i)
            low_part(NB - 2)
            low_part(NB - 1)

        @block.gpsimd
        def _(pool):
            pool_stats(pool)

        @block.tensor
        def _(pe):
            for i in range(NB):
                if i >= 2:
                    pe.wait_ge(s_low, KD * (i - 1))
                pe.wait_ge(s_xn, TB * (i + 1))
                for c in range(KD):
                    for j in range(TB):
                        t = nc.tensor.transpose(k.ps[:, 2 * (i % 2) + c, j * P:(j + 1) * P],
                                                xn[:, i * TB + j, c * P:(c + 1) * P], k.ident[:])
                    t.then_inc(s_turned, 1)

        @block.scalar
        def _(act):
            for i in range(NB):
                act.wait_ge(s_turned, KD * (i + 1))
                if b is not None:
                    for c in range(KD):
                        nc.scalar.activation(full[:, i % 2, c, :], banks(i)[:, c], ACT.Identity, scale=k.vec[:, w + c:w + c + 1],
                                             bias=k.vec[:, b + c:b + c + 1]).then_inc(s_full, 1)
                    act.wait_ge(s_full, KD * (i + 1))
                    nc.scalar.activation(high[i], full[:, i % 2], ACT.Copy).then_inc(s_high, KD)
                elif w is not None:
                    for c in range(KD):
                        nc.scalar.activation(high[i][:, c], banks(i)[:, c], ACT.Copy, scale=k.vec[:, w + c:w + c + 1]).then_inc(s_high, 1)
                else:
                    nc.scalar.activation(high[i], banks(i), ACT.Copy).then_inc(s_high, KD)


def ssm(nc, k):
    with ExitStack() as ctx:
        sb = lambda n, s, d=F32: ctx.enter_context(nc.sbuf_tensor("ssm_" + n, s, d))
        sem = lambda n: ctx.enter_context(nc.semaphore("ssm_" + n))
        alpha, u, h = sb("alpha", [P, KD, T]), sb("u", [P, KD, T]), sb("h", [P, KD, T])
        h_split = [sb("hh", [P, KD, T], F16), sb("hl", [P, KD, T], F16)]
        res = sb("res", [P, 2, D])
        s_au, s_evac, s_scan, s_high, s_low = sem("au"), sem("evac"), sem("scan"), sem("high"), sem("low")
        s_y, s_x, s_res, s_st = sem("y"), sem("x"), sem("res"), sem("st")
        block = ctx.enter_context(nc.Block())
        AU = (("a", V_BA, ACT.Sigmoid, alpha), ("b", V_BB, ACT.Identity, u))

        @block.tensor
        def _(pe):
            def alpha_u(i):
                wait(pe, s_evac, 4 * i)
                for m, (name, _, _, _) in enumerate(AU):
                    for c in range(KD):
                        n = 0
                        for kc in range(KD):
                            for pw, px in PASSES:
                                mm = nc.tensor.matmul(k.ps[:, 2 * m + c, :],
                                                      weight(k, name, kc, pw)[:, c * P:(c + 1) * P],
                                                      k.nT[px][:, kc, ds(i * BLK, BLK)],
                                                      start=n == 0, stop=n == 5)
                                n += 1
                        mm.then_inc(s_au, 1)

            def y(i):
                pe.wait_ge(s_low, i + 1)
                wait(pe, s_x, TB * i)
                for j in range(TB):
                    n = 0
                    for kc in range(KD):
                        for ph, pw in PASSES:
                            mm = nc.tensor.matmul(k.ps[:, 4 + j, 0:D], h_split[ph][:, kc, ds(i * BLK + j * P, P)],
                                                  weight(k, "c", kc, pw), start=n == 0, stop=n == 5)
                            n += 1
                    mm.then_inc(s_y, 1)

            alpha_u(0)
            alpha_u(1)
            y(0)
            with pe.Fori(2, NB) as i:
                alpha_u(i)
                y(i - 1)
            y(NB - 1)

        @block.scalar
        def _(act):
            with act.Fori(0, NB) as i:
                for m, (_, bias, fn, dst) in enumerate(AU):
                    for c in range(KD):
                        act.wait_ge(s_au, 4 * i + 2 * m + c + 1)
                        nc.scalar.activation(dst[:, c, ds(i * BLK, BLK)], k.ps[:, 2 * m + c, :], fn,
                                             scale=1.0 / WS, bias=k.vec[:, bias + c:bias + c + 1]).then_inc(s_evac, 1)

        @block.gpsimd
        def _(pool):
            with pool.Fori(0, NB) as i:
                cols = ds(i * BLK, BLK)
                pool.wait_ge(s_scan, 4 * i + 4)
                nc.gpsimd.tensor_copy(h_split[0][:, :, cols], h[:, :, cols]).then_inc(s_high, 1)
                pool.wait_ge(s_high, i + 1)
                nc.gpsimd.tensor_tensor(h_split[1][:, :, cols], h[:, :, cols], h_split[0][:, :, cols],
                                        ALU.subtract).then_inc(s_low, 1)

        @block.vector
        def _(dve):
            def scans(i):
                dve.wait_ge(s_evac, 4 * i + 4)
                for c in range(KD):
                    for b in range(BLK // S):
                        cols = ds(i * BLK + b * S, S)
                        nc.vector.tensor_tensor_scan(h[:, c, cols], alpha[:, c, cols], u[:, c, cols], 0.0,
                                                     ALU.mult, ALU.add).then_inc(s_scan, 1)

            def residual(i):
                for j in range(TB):
                    t = ds(i * TB + j, 1)
                    n = i * TB + j
                    nc.vector.tensor_scalar(res[:, 0, :], k.X[:, t, :], k.mv[:, t, 0], k.r1[:, t],
                                            ALU.subtract, ALU.mult).then_inc(s_res, 1)
                    dve.wait_ge(s_res, 4 * n + 1)
                    nc.vector.tensor_tensor(res[:, 1, :], res[:, 0, :], k.rows[:, R_D, :], ALU.mult).then_inc(s_res, 1)
                    dve.wait_ge(s_res, 4 * n + 2)
                    nc.vector.tensor_tensor(res[:, 0, :], res[:, 1, :], k.X[:, ds(n, 1), :], ALU.add).then_inc(s_res, 1)
                    dve.wait_ge(s_res, 4 * n + 3)
                    nc.vector.tensor_tensor(res[:, 1, :], res[:, 0, :], k.rows[:, R_BC, :], ALU.add).then_inc(s_res, 1)
                    dve.wait_ge(s_res, 4 * n + 4)
                    dve.wait_ge(s_y, n + 1)
                    nc.vector.scalar_tensor_tensor(k.X[:, ds(n, 1), :], k.ps[:, 4 + j, 0:D], 1.0 / WS, res[:, 1, :],
                                                   ALU.mult, ALU.add).then_inc(s_x, 1)
                    dve.wait_ge(s_x, n + 1)
                    tile_stats(nc, k, n).then_inc(s_st, 1)

            scans(0)
            with dve.Fori(1, NB) as i:
                scans(i)
                residual(i - 1)
            residual(NB - 1)


def three_pass(nc, out, stationary, moving, first=True, last=True):
    for n, (ps, pm) in enumerate(PASSES):
        mm = nc.tensor.matmul(out, stationary(ps), moving(pm), start=first and n == 0,
                              stop=last and n == len(PASSES) - 1)
    return mm


def cross_project(nc, k, a, A):
    with ExitStack() as ctx:
        sb = lambda n, s, d=F32: ctx.enter_context(nc.sbuf_tensor("xp_" + n, s, d))
        sem = lambda n: ctx.enter_context(nc.semaphore("xp_" + n))
        ctx_in = sb("ctx_in", [P, 2, KC, BLK])
        ctx_h, ctx_l = sb("ctx_h", [P, 2, KC, BLK], F16), sb("ctx_l", [P, 2, KC, BLK], F16)
        mask_row = sb("mask_row", [P, T])
        biased = sb("biased", [P, 2, BLK])
        masked = sb("masked", [P, 2, BLK])
        qk_h, qk_l = sb("qk_h", [P, 4, BLK], F16), sb("qk_l", [P, 4, BLK], F16)
        vtmp = sb("vtmp", [P, 2, D])
        negm = sb("negm", [B, S])
        negh = sb("negh", [B, S], F16)
        s_ctx = [sem("ctx0"), sem("ctx1")]
        s_mask, s_ch, s_cl, s_qk, s_biased, s_masked = sem("mask"), sem("ch"), sem("cl"), sem("qk"), sem("biased"), sem("masked")
        s_high, s_low, s_v, s_vt, s_vm, s_o, s_x = (sem(n) for n in ("high", "low", "v", "vt", "vm", "o", "x"))
        s_out = [sem(f"out{m}") for m in range(4)]
        s_neg, s_negout, s_xb, s_fill = sem("neg"), sem("negout"), sem("xb"), sem("fill")
        block = ctx.enter_context(nc.Block())
        UNITS = (("tgt", 0, V_BTGT), ("tgt", 1, V_BTGT + 1), ("src", 0, V_BSRC), ("src", 1, V_BSRC + 1))

        @block.sync
        def _(sp):
            sp.dma_start(negm[:], a["mask"]).then_inc(s_mask, 16)
            sp.dma_start(k.mask_col[:], a["maskT"]).then_inc(s_mask, 16)
            sp.dma_start(mask_row[:], a["mask"].rearrange("(o b) s -> o (b s)", o=1).to_broadcast([P, T])).then_inc(s_mask, 16)
            for i in range(2):
                sp.dma_start(ctx_in[:, i], a["ctxT"][:, :, i * BLK:(i + 1) * BLK]).then_inc(s_ctx[i], 16)
            for i in range(2, NB):
                sp.wait_ge(s_cl, i - 1)
                sp.dma_start(ctx_in[:, i % 2], a["ctxT"][:, :, i * BLK:(i + 1) * BLK]).then_inc(s_ctx[i % 2], 16)
            sp.wait_ge(s_neg, 2)
            sp.dma_start(k.negmask, negh[:]).then_inc(s_negout, 16)
            sp.wait_ge(s_negout, 16)

        @block.tensor
        def _(pe):
            def two_blocks(ii):
                for s in range(2):
                    i = 2 * ii + s
                    for m, (name, c, _) in enumerate(UNITS):
                        if m == 2:
                            pe.wait_ge(s_cl, i + 1)
                        wait(pe, s_biased, 4 * i + m - 1)
                        for kc in range(KD if name == "tgt" else KC):
                            src = (lambda p: k.nT[p][:, kc, ds(i * BLK, BLK)]) if name == "tgt" else \
                                  (lambda p: (ctx_h, ctx_l)[p][:, s, kc, :])
                            mm = three_pass(nc, k.ps[:, m % 2, :], lambda p: weight(k, name, kc, p)[:, c * P:(c + 1) * P],
                                            src, kc == 0, kc == (KD if name == "tgt" else KC) - 1)
                        mm.then_inc(s_qk, 1)
                    for j in range(TB):
                        wait(pe, s_vt, TB * i + j - 1)
                        for kc in range(KC):
                            mm = three_pass(nc, k.ps[:, 2 + j % 2, 0:D], lambda p: (ctx_h, ctx_l)[p][:, s, kc, j * P:(j + 1) * P],
                                            lambda p: weight(k, "src", kc, p)[:, D:2 * D], kc == 0, kc == KC - 1)
                        mm.then_inc(s_v, 1)
                        wait(pe, s_x, TB * i + j - 1)
                        for kc in range(KD):
                            mm = three_pass(nc, k.ps[:, 4 + j % 2, 0:D], lambda p: k.nT[p][:, kc, ds(i * BLK + j * P, P)],
                                            lambda p: weight(k, "o", kc, p), kc == 0, kc == KD - 1)
                        mm.then_inc(s_o, 1)

            peeled(pe, NB // 2, two_blocks)

        @block.scalar
        def _(act):
            for i in range(NB):
                act.wait_ge(s_ctx[i % 2], 16 * (i // 2 + 1))
                if i >= 2:
                    act.wait_ge(s_v, TB * (i - 1))
                nc.scalar.activation(ctx_h[:, i % 2], ctx_in[:, i % 2], ACT.Copy).then_inc(s_ch, 1)
                for m, (_, _, v) in enumerate(UNITS):
                    n = 4 * i + m
                    act.wait_ge(s_qk, n + 1)
                    if n >= 2:
                        act.wait_ge(s_masked, n - 1)
                    nc.scalar.activation(biased[:, n % 2, :], k.ps[:, m % 2, :], ACT.Identity, scale=1.0 / WS,
                                         bias=k.vec[:, v:v + 1]).then_inc(s_biased, 1)
                    act.wait_ge(s_masked, n + 1)
                    if n >= 4:
                        act.wait_ge(s_out[m], 32 * i)
                    nc.scalar.activation(qk_h[:, m, :], masked[:, n % 2, :], ACT.Copy).then_inc(s_high, 1)
                for m in range(4):
                    act.wait_ge(s_low, 4 * i + m + 1)
                    for p, part in enumerate((qk_h, qk_l)):
                        act.dma_start(A.rows_of(k.xqk, m, p)[:, :, i * BLK:(i + 1) * BLK], part[:, m, :]).then_inc(s_out[m], 16)
            for m in range(4):
                act.wait_ge(s_out[m], 32 * NB)

        @block.vector
        def _(dve):
            dve.wait_ge(s_mask, 48)
            nc.vector.tensor_scalar(negm[:], negm[:], 0.0, NEG, ALU.is_equal, ALU.mult).then_inc(s_neg, 1)
            dve.wait_ge(s_neg, 1)
            nc.vector.tensor_copy(negh[:], negm[:]).then_inc(s_neg, 1)
            for i in range(NB):
                for m in range(4):
                    n = 4 * i + m
                    dve.wait_ge(s_biased, n + 1)
                    if n >= 2:
                        dve.wait_ge(s_low, n - 1)
                    nc.vector.tensor_tensor(masked[:, n % 2, :], biased[:, n % 2, :], mask_row[:, i * BLK:(i + 1) * BLK],
                                            ALU.mult).then_inc(s_masked, 1)
                for j in range(TB):
                    n = TB * i + j
                    dve.wait_ge(s_v, n + 1)
                    if n >= 2:
                        dve.wait_ge(s_vm, n - 1)
                    nc.vector.scalar_tensor_tensor(vtmp[:, n % 2, :], k.ps[:, 2 + j % 2, 0:D], 1.0 / WS, k.rows[:, R_BV, :],
                                                   ALU.mult, ALU.add).then_inc(s_vt, 1)
                    dve.wait_ge(s_xb, n + 1)
                    dve.wait_ge(s_o, n + 1)
                    nc.vector.scalar_tensor_tensor(k.X[:, n, :], k.ps[:, 4 + j % 2, 0:D], 1.0 / WS, k.X[:, n, :],
                                                   ALU.mult, ALU.add).then_inc(s_x, 1)

        @block.gpsimd
        def _(pool):
            A.fill(nc, pool, s_fill)
            for i in range(NB):
                pool.wait_ge(s_ch, i + 1)
                nc.gpsimd.tensor_tensor(ctx_l[:, i % 2], ctx_in[:, i % 2], ctx_h[:, i % 2], ALU.subtract).then_inc(s_cl, 1)
                for j in range(TB):
                    n = TB * i + j
                    nc.gpsimd.tensor_tensor(k.X[:, n, :], k.X[:, n, :], k.rows[:, R_BO, :], ALU.add).then_inc(s_xb, 1)
                for m in range(4):
                    n = 4 * i + m
                    pool.wait_ge(s_high, n + 1)
                    nc.gpsimd.tensor_tensor(qk_l[:, m, :], masked[:, n % 2, :], qk_h[:, m, :], ALU.subtract).then_inc(s_low, 1)
                for j in range(TB):
                    n = TB * i + j
                    pool.wait_ge(s_vt, n + 1)
                    nc.gpsimd.tensor_scalar(k.V[:, n, :], vtmp[:, n % 2, :], k.mask_col[:, n:n + 1], None, ALU.mult).then_inc(s_vm, 1)


class Heads:

    def __init__(self, nc, k, ctx, tag, heads, dim, masked):
        sb = lambda n, s, d=F32: ctx.enter_context(nc.sbuf_tensor(tag + n, s, d))
        self.tag, self.heads, self.dim, self.masked = tag, heads, dim, masked
        self.top = 96 if masked else 64
        self.shift = self.top + 1
        self.groups = heads // 4
        self.units = 2 * self.groups
        self.wide = S if dim < 32 else 2 * S
        self.Q, self.K = sb("Q", [P, NSLOT * heads, S], F16), sb("K", [P, NSLOT * heads, S], F16)
        self.V = sb("Vb", [P, 2, 2, heads * 32])

    def rows_of(self, qk, m, part):
        n = P // self.dim
        return qk[m // 2, (m % 2) * n:(m % 2 + 1) * n, part * self.dim:(part + 1) * self.dim, :]

    def fill(self, nc, pool, filled):
        two_ones = float(np.array([1.0, 1.0], np.float16).view(np.float32)[0])
        rows = [(self.Q[96:P], two_ones), (self.K[96:P], two_ones)] if self.masked else \
               [(self.Q[:], 0.0), (self.K[0:64], 0.0), (self.K[64:P], two_ones)]
        fills = [(where.bitcast(F32), value) for where, value in rows]
        if not self.masked:
            fills.append((self.V[:], 1.0))
        for n, (where, value) in enumerate(fills):
            nc.gpsimd.memset(where, value).then_inc(filled, 1)
            pool.wait_ge(filled, n + 1)


NSLOT = 4


def has(b, before=0, after=0):
    return not isinstance(b, int) or (b >= before and b + after < B)


def over_batches(eng, step):
    step(0, 0)
    step(1, 1)
    with eng.Fori(1, B // 2 - 1) as i:
        step(2 * i, 0)
        step(2 * i + 1, 1)
    step(B - 2, 0)
    step(B - 1, 1)


def attention(nc, k, A, qk, wname, wk0, negmask):
    tag, heads, dim, top, shift = A.tag, A.heads, A.dim, A.top, A.shift
    Q, K, V, G, UN = A.Q, A.K, A.V, A.groups, A.units
    MU = 2 * UN
    HALF = UN // 2
    NC = G * S
    scale = float(dim) ** -0.5
    loads = 5 if negmask is not None else 4
    den_row = 0 if dim == 32 else dim
    with ExitStack() as ctx:
        sb = lambda n, s, d=F32: ctx.enter_context(nc.sbuf_tensor(tag + n, s, d))
        sem = lambda n: ctx.enter_context(nc.semaphore(tag + n))
        pT = sb("pT", [P, 2, 4 * S])
        nmx = sb("nmx", [P, 2, 2, heads])
        nmT = sb("nmT", [heads, 2, S], F16)
        sums = sb("sums", [P, 2, A.wide // S, NC])
        den, rec = sb("den", [P, heads * S // P]), sb("rec", [P, heads * S // P])
        rec_d = nc.dram_tensor(tag + "rec_d", (4, NC), F32, kind="Internal").ap()
        recb = sb("recb", [P, NC])
        last_rec = sb("last_rec", [P, NC])
        o = sb("o", [P, 2, NC])
        oh, ol = sb("oh", [P, 2, NC], F16), sb("ol", [P, 2, NC], F16)
        s_load, s_nmin = [sem("load0"), sem("load1")], [sem("nmin0"), sem("nmin1")]
        s_v, s_mx, s_red, s_turn, s_nmT = (sem(n) for n in ("v", "mx", "red", "turn", "nmT"))
        s_st, s_exp, s_pv, s_sum, s_rec, s_o, s_oh, s_ol, s_out, s_x = (sem(n) for n in ("st", "exp", "pv", "sum", "rec", "o", "oh", "ol", "out", "x"))
        s_den, s_recw, s_recr, s_last, s_stats = (sem(n) for n in ("den", "recw", "recr", "last", "stats"))
        block = ctx.enter_context(nc.Block())

        @block.sync
        def _(sp):
            def load(b, s):
                sl = (b % NSLOT) * heads
                cols = b * S
                if not isinstance(b, int):
                    sl, cols = sp.snap(sl), sp.snap(cols)
                wait(sp, s_pv, UN * (b - NSLOT + 1))
                for dst, row, src, lo, hi in ((Q, 0, 0, 0, 2), (Q, 2 * dim, 0, 0, 1), (K, 0, 1, 0, 1), (K, dim, 1, 0, 2)):
                    sp.dma_start(dst[row:row + (hi - lo) * dim, ds(sl, heads), :],
                                 qk[src, :, lo * dim:hi * dim, ds(cols, S)].rearrange("h r t -> r h t")).then_inc(s_load[s], 16)
                if negmask is not None:
                    sp.dma_start(K[top:top + 1, ds(sl, heads), :],
                                 negmask[ds(b, 1), :].rearrange("o (h s) -> o h s", h=1).to_broadcast([1, heads, S])).then_inc(s_load[s], 16)

            def maxima(b, s):
                sl = (b % NSLOT) * heads
                if not isinstance(b, int):
                    sl = sp.snap(sl)
                sp.wait_ge(s_nmT, b + 1)
                sp.dma_start(Q[shift:shift + 1, ds(sl, heads), :], nmT[:, s, :]).then_inc(s_nmin[s], 16)

            def gather(b, s):
                sp.wait_ge(s_sum, G * b + G)
                sp.dma_start(den[:], sums[den_row:P:32, s, A.wide // S - 1, :].rearrange("j (a e) -> j a e", a=32)).then_inc(s_den, 16)

            def scatter(b):
                sp.wait_ge(s_rec, b + 1)
                wait(sp, s_o, b)
                sp.dma_start(rec_d.rearrange("j (a e) -> (j a) e", a=32), rec[:]).then_inc(s_recw, 16)
                sp.wait_ge(s_recw, 16 * b + 16)
                sp.dma_start(recb[:], rec_d.rearrange("j (o c) -> j o c", o=1).to_broadcast([4, 32, NC])).then_inc(s_recr, 16)

            def step(b, s):
                if has(b, after=2):
                    load(b + 2, s)
                if has(b, before=1):
                    gather(b - 1, 1 - s)
                if has(b, after=1):
                    maxima(b + 1, 1 - s)
                if has(b, before=1):
                    scatter(b - 1)
                    if not has(b, after=1):
                        sp.wait_ge(s_recr, 16 * b)

            load(0, 0)
            load(1, 1)
            maxima(0, 0)
            over_batches(sp, step)

        @block.gpsimd
        def _(pool):
            def values(b, s):
                wait(pool, s_pv, UN * (b - 1))
                nc.gpsimd.tensor_copy(V[:, s].rearrange("p c (h d) -> p c h d", d=32)[:, :, :, 0:dim],
                                      k.V[:, ds(2 * b, 2), :].rearrange("p c (h d) -> p c h d", d=dim)).then_inc(s_v, 1)

            def low(b, s):
                pool.wait_ge(s_oh, b + 1)
                nc.gpsimd.tensor_tensor(ol[:, s], o[:, s], oh[:, s], ALU.subtract).then_inc(s_ol, 1)

            def step(b, s):
                if has(b, after=1):
                    values(b + 1, 1 - s)
                if has(b, before=2):
                    low(b - 2, s)

            values(0, 0)
            over_batches(pool, step)
            low(B - 2, 0)
            low(B - 1, 1)

        @block.tensor
        def _(pe):
            slot_regs = [pe.alloc_register(f"{tag}slot{r}") for r in range(3)]

            def slot_of(b, r):
                sl = (b % NSLOT) * heads
                if isinstance(b, int):
                    return sl
                pe.reg_mov(slot_regs[r], sl)
                return pe.snap(slot_regs[r], min_val=0, max_val=(NSLOT - 1) * heads)

            def max_unit(b, sl, m):
                tc, hp = m // (heads // 2), m % (heads // 2)
                wait(pe, s_red, MU * b + m - 1)
                for e in range(2):
                    mm = nc.tensor.matmul(k.ps[:, m % 2, e * S:(e + 1) * S], Q[0:top + 1, ds(sl + (2 * hp + e), 1), tc * P:(tc + 1) * P],
                                          K[0:top + 1, ds(sl + (2 * hp + e), 1), :], start=True, stop=True)
                mm.then_inc(s_mx, 1)

            def turn(b, s):
                pe.wait_ge(s_red, MU * b + MU)
                wait(pe, s_x, b - 3)
                for tc in range(2):
                    mm = nc.tensor.transpose(k.ps[0:heads, 7, tc * P:(tc + 1) * P], nmx[:, s, tc, :], k.ident[:])
                mm.then_inc(s_turn, 1)

            def scores(b, sl, u):
                g, c = u // 2, u % 2
                wait(pe, s_exp, UN * b + u - 1)
                for j in range(4):
                    mm = nc.tensor.matmul(k.ps[:, 2 + 2 * (u % 2) + j // 2, (j % 2) * S:(j % 2 + 1) * S],
                                          K[0:shift + 1, ds(sl + (4 * g + j), 1), c * P:(c + 1) * P], Q[0:shift + 1, ds(sl + (4 * g + j), 1), :], start=True, stop=True)
                mm.then_inc(s_st, 1)

            def weigh(b, s, u):
                g, c = u // 2, u % 2
                pe.wait_ge(s_exp, UN * b + u + 1)
                if c == 0:
                    wait(pe, s_sum, G * b + g)
                for what in range(A.wide // S):
                    for j in range(4):
                        h = 4 * g + j
                        lhs = V[:, s, c, 32 * h:32 * h + 32] if what == 0 else k.ones[:, :]
                        mm = nc.tensor.matmul(k.ps[32 * j:32 * j + 32, 6, what * S:(what + 1) * S], lhs,
                                              pT[:, u % 2, j * S:(j + 1) * S], start=c == 0 and what == 0, stop=c == 1,
                                              skip_group_check=True)
                mm.then_inc(s_pv, 1)

            def output(b, s, part):
                if part == 0:
                    pe.wait_ge(s_ol, b + 1)
                    pe.wait_ge(s_nmT, min(b + 4, B) if isinstance(b, int) else b + 4)
                for piece in (2 * part, 2 * part + 1):
                    tc, g = piece // G, piece % G
                    mm = three_pass(nc, k.ps[:, 7, tc * D:(tc + 1) * D],
                                    lambda p: (oh, ol)[p][:, s, g * S + tc * P:g * S + (tc + 1) * P],
                                    lambda p: weight(k, wname, wk0 + g, p), g == 0, g == G - 1)
                if part == HALF - 1:
                    mm.then_inc(s_out, 1)

            def step(b, s):
                pe.wait_ge(s_nmin[s], 8 * b + 16 - 8 * s)
                pe.wait_ge(s_v, b + 1)
                sl, sl1, sl2 = slot_of(b, 0), slot_of(b + 1, 1), slot_of(b + 2, 2)
                scores(b, sl, 0)
                for u in range(UN):
                    if u + 1 < UN:
                        scores(b, sl, u + 1)
                    if u < HALF and has(b, after=1):
                        for e in range(2):
                            max_unit(b + 1, sl1, UN + 2 * u + e)
                    if u == HALF and has(b, after=1):
                        turn(b + 1, 1 - s)
                    if u == HALF and has(b, after=2):
                        pe.wait_ge(s_load[s], loads * (8 * b + 32 - 8 * s))
                    if u >= HALF and has(b, after=2):
                        for e in range(2):
                            max_unit(b + 2, sl2, 2 * (u - HALF) + e)
                    if u >= HALF and has(b, before=2):
                        output(b - 2, s, u - HALF)
                    weigh(b, s, u)

            pe.wait_ge(s_load[0], 16 * loads)
            for m in range(MU):
                max_unit(0, 0, m)
            turn(0, 0)
            pe.wait_ge(s_load[1], 16 * loads)
            for m in range(UN):
                max_unit(1, heads, m)
            over_batches(pe, step)
            for b in (B - 2, B - 1):
                if b == B - 1:
                    pe.wait_ge(s_x, B - 1)
                for part in range(HALF):
                    output(b, b % 2, part)

        @block.scalar
        def _(act):
            def turned(b, s):
                act.wait_ge(s_turn, b + 1)
                if has(b, before=2):
                    act.wait_ge(s_nmin[s], 8 * b - 8 * s)
                nc.scalar.activation(nmT[:, s, :], k.ps[0:heads, 7, 0:S], ACT.Copy).then_inc(s_nmT, 1)

            def high(b, s):
                act.wait_ge(s_o, b + 1)
                if isinstance(b, int):
                    wait(act, s_out, b - 1)
                nc.scalar.activation(oh[:, s], o[:, s], ACT.Copy).then_inc(s_oh, 1)

            def step(b, s):
                for u in range(UN):
                    wait(act, s_pv, UN * b + u - 1)
                    act.wait_ge(s_st, UN * b + u + 1)
                    nc.scalar.activation(pT[:, u % 2, :].rearrange("p (b c) -> p b c", b=2),
                                         k.ps[:, 2 + 2 * (u % 2):4 + 2 * (u % 2), :], ACT.Exp, scale=scale).then_inc(s_exp, 1)
                    if u == HALF and has(b, after=1):
                        turned(b + 1, 1 - s)
                    if u == 1 and has(b, before=2):
                        high(b - 2, s)

            turned(0, 0)
            over_batches(act, step)
            high(B - 2, 0)
            high(B - 1, 1)

        @block.vector
        def _(dve):
            def reduce(b, s, m):
                tc, hp = m // (heads // 2), m % (heads // 2)
                dve.wait_ge(s_mx, MU * b + m + 1)
                if m == 0 and has(b, before=2):
                    dve.wait_ge(s_turn, b - 1)
                nc.vector.tensor_reduce(nmx[:, s, tc, 2 * hp:2 * hp + 2],
                                        k.ps[:, m % 2, :].rearrange("p (e s) -> p e s", e=2), AX, ALU.max,
                                        negate=True).then_inc(s_red, 1)

            def collect(b, s, g):
                if g == 0:
                    wait(dve, s_o, b - 1)
                dve.wait_ge(s_pv, UN * b + 2 * g + 2)
                nc.vector.tensor_copy(sums[:, s, :, g * S:(g + 1) * S], k.ps[:, 6, 0:A.wide].rearrange("p (w s) -> p w s", s=S)).then_inc(s_sum, 1)

            def invert(b):
                dve.wait_ge(s_den, 16 * b + 16)
                wait(dve, s_recw, 16 * b)
                nc.vector.reciprocal(rec[:], den[:]).then_inc(s_rec, 1)

            def invert_last(g):
                cols = slice(g * S, (g + 1) * S)
                out, src = last_rec[:, cols], sums[:, (B - 1) % 2, A.wide // S - 1, cols]
                dve.wait_ge(s_sum, G * (B - 1) + g + 1)
                if dim < 32:
                    nc.vector.stream_shuffle(out, src, [dim + r % dim for r in range(32)]).then_inc(s_last, 1)
                    dve.wait_ge(s_last, 2 * g + 1)
                    nc.vector.reciprocal(out, out).then_inc(s_last, 1)
                else:
                    nc.vector.reciprocal(out, src).then_inc(s_last, 2)

            def divide(b, s):
                if has(b, after=1):
                    dve.wait_ge(s_recr, 16 * b + 16)
                else:
                    dve.wait_ge(s_last, 2 * G)
                nc.vector.tensor_tensor(o[:, s], sums[:, s, 0, :], recb[:] if has(b, after=1) else last_rec[:],
                                        ALU.mult).then_inc(s_o, 1)

            def residual(b):
                dve.wait_ge(s_out, b + 1)
                nc.vector.scalar_tensor_tensor(k.X[:, ds(2 * b, 2), :], k.ps[:, 7, :].rearrange("p (c d) -> p c d", c=2),
                                               1.0 / WS, k.X[:, ds(2 * b, 2), :], ALU.mult, ALU.add).then_inc(s_x, 1)
                dve.wait_ge(s_x, b + 1)
                for t in range(2):
                    tile_stats(nc, k, 2 * b + t).then_inc(s_stats, 1)

            def step(b, s):
                for u in range(UN):
                    if u < HALF and has(b, after=1):
                        for e in range(2):
                            reduce(b + 1, 1 - s, UN + 2 * u + e)
                    if u >= HALF and has(b, after=2):
                        for e in range(2):
                            reduce(b + 2, s, 2 * (u - HALF) + e)
                    if u == UN - 1 and has(b, before=2):
                        residual(b - 2)
                    if u % 2 == 1:
                        collect(b, s, u // 2)
                    if u % 2 == 1 and not has(b, after=1):
                        invert_last(u // 2)
                    if u == 0 and has(b, before=2):
                        divide(b - 2, s)
                    if u == HALF and has(b, before=1):
                        invert(b - 1)

            for m in range(MU):
                reduce(0, 0, m)
            for m in range(UN):
                reduce(1, 1, m)
            over_batches(dve, step)
            divide(B - 2, 0)
            divide(B - 1, 1)
            residual(B - 2)
            residual(B - 1)
def self_project(nc, k, A):
    with ExitStack() as ctx:
        sem = lambda n: ctx.enter_context(nc.semaphore("mp_" + n))
        qk_h = ctx.enter_context(nc.sbuf_tensor("mp_qk_h", [P, 4, BLK], F16))
        qk_l = ctx.enter_context(nc.sbuf_tensor("mp_qk_l", [P, 4, BLK], F16))
        s_qk, s_high, s_low, s_v, s_vout = (sem(n) for n in ("qk", "high", "low", "v", "vout"))
        s_fill = sem("fill")
        s_out = [sem(f"out{m}") for m in range(4)]
        block = ctx.enter_context(nc.Block())

        @block.tensor
        def _(pe):
            def one_block(i):
                for m, (name, c) in enumerate((("q", 0), ("q", 1), ("k", 0), ("k", 1))):
                    wait(pe, s_low, 4 * i)
                    for kc in range(KD):
                        mm = three_pass(nc, k.ps[:, m, :], lambda p: weight(k, name, kc, p)[:, c * P:(c + 1) * P],
                                        lambda p: k.nT[p][:, kc, ds(i * BLK, BLK)], kc == 0, kc == KD - 1)
                    mm.then_inc(s_qk, 1)
                for j in range(TB):
                    wait(pe, s_vout, TB * i)
                    for kc in range(KD):
                        mm = three_pass(nc, k.ps[:, 4 + j, 0:D], lambda p: k.nT[p][:, kc, ds(i * BLK + j * P, P)],
                                        lambda p: weight(k, "v", kc, p), kc == 0, kc == KD - 1)
                    mm.then_inc(s_v, 1)

            peeled(pe, NB, one_block)

        @block.scalar
        def _(act):
            def one_block(i):
                for m in range(4):
                    act.wait_ge(s_qk, 4 * i + m + 1)
                    wait(act, s_out[m], 32 * i)
                    nc.scalar.activation(qk_h[:, m, :], k.ps[:, m, :], ACT.Copy, scale=1.0 / WS).then_inc(s_high, 1)
                for j in range(TB):
                    act.wait_ge(s_v, TB * i + j + 1)
                    nc.scalar.activation(k.V[:, ds(i * TB + j, 1), :], k.ps[:, 4 + j, 0:D], ACT.Copy,
                                         scale=1.0 / WS).then_inc(s_vout, 1)

            peeled(act, NB, one_block)

        @block.vector
        def _(dve):
            with dve.Fori(0, NB) as i:
                for m in range(4):
                    dve.wait_ge(s_high, 4 * i + m + 1)
                    nc.vector.scalar_tensor_tensor(qk_l[:, m, :], k.ps[:, m, :], 1.0 / WS, qk_h[:, m, :],
                                                   ALU.mult, ALU.subtract).then_inc(s_low, 1)

        @block.gpsimd
        def _(pool):
            A.fill(nc, pool, s_fill)

        @block.sync
        def _(sp):
            with sp.Fori(0, NB) as i:
                for m in range(4):
                    sp.wait_ge(s_low, 4 * i + m + 1)
                    for p, part in enumerate((qk_h, qk_l)):
                        sp.dma_start(A.rows_of(k.mqk, m, p)[:, :, ds(i * BLK, BLK)], part[:, m, :]).then_inc(s_out[m], 16)
            for m in range(4):
                sp.wait_ge(s_out[m], 32 * NB)


def route(nc, k):
    with ExitStack() as ctx:
        sb = lambda n, s, d=F32: ctx.enter_context(nc.sbuf_tensor("rt_" + n, s, d))
        sem = lambda n: ctx.enter_context(nc.semaphore("rt_" + n))
        L, m1, d, ex = sb("L", [P, NT, E]), sb("m1", [P, NT]), sb("d", [P, NT, E]), sb("ex", [P, NT, E])
        gt, eq, rank = sb("gt", [P, NT, E, E]), sb("eq", [P, NT, E, E]), sb("rank", [P, NT, E])
        before = sb("before", [P, E, E])
        s_l, s_step, s_ex, s_before = sem("logits"), sem("step"), sem("ex"), sem("before")
        block = ctx.enter_context(nc.Block())

        @block.gpsimd
        def _(pool):
            nc.gpsimd.memset(before[:], 1.0).then_inc(s_before, 1)
            pool.wait_ge(s_before, 1)
            nc.gpsimd.affine_select(out=before[:], in_=before[:], compare_op=ALU.is_gt, fill=0.0, base=0,
                                    pattern=[[1, E], [-1, E]], channel_multiplier=0).then_inc(s_before, 1)

        @block.tensor
        def _(pe):
            for t in range(NT):
                for kc in range(KD):
                    mm = three_pass(nc, k.ps[:, 0, t * E:(t + 1) * E], lambda p: k.nT[p][:, kc, t * P:(t + 1) * P],
                                    lambda p: weight(k, "g", kc, p), kc == 0, kc == KD - 1)
            mm.then_inc(s_l, 1)

        @block.scalar
        def _(act):
            act.wait_ge(s_step, 3)
            nc.scalar.activation(ex[:], d[:], ACT.Exp).then_inc(s_ex, 1)

        @block.vector
        def _(dve):
            step = [0]

            def then(ins):
                step[0] += 1
                ins.then_inc(s_step, 1)
                dve.wait_ge(s_step, step[0])

            def of(x, kind):
                v = x.rearrange("p t (e o) -> p t e o", o=1) if kind == "e" else x.rearrange("p t (o j) -> p t o j", o=1)
                return v.to_broadcast([P, NT, E, E])

            dve.wait_ge(s_l, 1)
            then(nc.vector.tensor_scalar(L[:], k.ps[:, 0, 0:NT * E].rearrange("p (t e) -> p t e", e=E), 1.0 / WS, None, ALU.mult))
            then(nc.vector.tensor_reduce(m1[:], L[:], AX, ALU.max))
            then(nc.vector.tensor_tensor(d[:], L[:], m1[:].rearrange("p (t o) -> p t o", o=1).to_broadcast([P, NT, E]), ALU.subtract))
            then(nc.vector.tensor_tensor(gt[:], of(L[:], "j"), of(L[:], "e"), ALU.is_gt))
            then(nc.vector.tensor_tensor(eq[:], of(L[:], "j"), of(L[:], "e"), ALU.is_equal))
            dve.wait_ge(s_before, 2)
            bb = before[:].rearrange("p (o e) j -> p o e j", o=1).to_broadcast([P, NT, E, E])
            then(nc.vector.tensor_tensor(eq[:], eq[:], bb, ALU.mult))
            then(nc.vector.tensor_tensor(gt[:], gt[:], eq[:], ALU.add))
            then(nc.vector.tensor_reduce(rank[:], gt[:], AX, ALU.add))
            then(nc.vector.tensor_scalar(rank[:], rank[:], 1.5, 1.0 / (WS * WS), ALU.is_lt, ALU.mult))
            dve.wait_ge(s_ex, 1)
            then(nc.vector.tensor_tensor(d[:], ex[:], rank[:], ALU.mult))
            then(nc.vector.tensor_reduce(m1[:], d[:], AX, ALU.add))
            then(nc.vector.tensor_scalar(m1[:], m1[:], WS * WS, None, ALU.mult))
            then(nc.vector.reciprocal(m1[:], m1[:]))
            then(nc.vector.tensor_tensor(k.wexp[:, :, 0:E], d[:], m1[:].rearrange("p (t o) -> p t o", o=1).to_broadcast([P, NT, E]), ALU.mult))
            then(nc.vector.memset(k.wexp[:, :, E:EA], 1.0 / (WS * WS)))


def expert_ffn(nc, k, a):
    NS = NB * EA
    with ExitStack() as ctx:
        sb = lambda n, s, d=F32: ctx.enter_context(nc.sbuf_tensor("ex_" + n, s, d))
        sem = lambda n: ctx.enter_context(nc.semaphore("ex_" + n))
        stage = sb("stage", [P, 2, NEW])
        wh, wl = sb("wh", [P, 2 * NEW], F16), sb("wl", [P, 2 * NEW], F16)
        gate, hid = sb("gate", [P, 2, BLK]), sb("hid", [P, 2, BLK])
        hh, hl = sb("hh", [P, 2, NHC, BLK], F16), sb("hl", [P, 2, NHC, BLK], F16)
        s_gu, s_gate, s_hid, s_high, s_low, s_y, s_x = (sem(n) for n in ("gu", "gate", "hid", "high", "low", "y", "x"))
        s_stats = sem("stats")
        s_win, s_wh, s_wl = [sem("win0"), sem("win1")], sem("wh"), sem("wl")
        block = ctx.enter_context(nc.Block())

        @block.sync
        def _(sp):
            def load(e, s):
                sp.dma_start(stage[:, s, :], a["mw"][:, ds(e * NEW, NEW)]).then_inc(s_win[s], 16)

            load(0, 0)
            load(1, 1)
            with sp.Fori(1, EA // 2) as i:
                for s in range(2):
                    sp.wait_ge(s_wl, 2 * i + s - 1)
                    load(2 * i + s, s)

        @block.tensor
        def _(pe):
            def gate_up(n, s):
                e, cols = n // NB, (n % NB) * BLK
                slot = (e % 2) * NEW
                if not isinstance(n, int):
                    e, cols, slot = pe.snap(e), pe.snap(cols), pe.snap(slot)
                pe.wait_ge(s_wl, e + 1)
                for c, (lo, w) in enumerate(HCH):
                    wait(pe, s_hid, NHC * n + c - 1)
                    for g in range(2):
                        for kc in range(KD):
                            mm = three_pass(nc, k.ps[0:w, 2 * ((s + c) % 2) + g, :],
                                            lambda p: (wh, wl)[p][:, ds(slot + ((g * KD + kc) * H + lo), w)],
                                            lambda p: k.nT[p][:, kc, ds(cols, BLK)], kc == 0, kc == KD - 1)
                    mm.then_inc(s_gu, 1)

            def down(n, s):
                slot = ((n // NB) % 2) * NEW
                if not isinstance(n, int):
                    slot = pe.snap(slot)
                pe.wait_ge(s_low, NHC * n + NHC)
                for j in range(TB):
                    wait(pe, s_x, TB * n - TB + j + 1)
                    for c, (_, w) in enumerate(HCH):
                        mm = three_pass(nc, k.ps[:, 4 + j, 0:D], lambda p: (hh, hl)[p][0:w, s, c, j * P:(j + 1) * P],
                                        lambda p: (wh, wl)[p][0:w, ds(slot + (2 * KD * H + c * D), D)], c == 0, c == NHC - 1)
                    mm.then_inc(s_y, 1)

            gate_up(0, 0)
            gate_up(1, 1)
            down(0, 0)
            with pe.Fori(0, NS // 2 - 1) as i:
                gate_up(2 * i + 2, 0)
                down(2 * i + 1, 1)
                gate_up(2 * i + 3, 1)
                down(2 * i + 2, 0)
            down(NS - 1, 1)

        @block.scalar
        def _(act):
            def split(e, s):
                if isinstance(e, int):
                    act.wait_ge(s_win[s], 16)
                else:
                    act.wait_ge(s_win[s], 8 * e + 16 - 8 * s)
                    act.wait_ge(s_y, TB * NB * e - TB * NB)
                nc.scalar.activation(wh[:, s * NEW:(s + 1) * NEW], stage[:, s, :], ACT.Copy, scale=WS).then_inc(s_wh, 1)

            def one_step(n, s, first):
                for c, (_, w) in enumerate(HCH):
                    m, q = NHC * n + c, (s + c) % 2
                    act.wait_ge(s_gu, m + 1)
                    nc.scalar.activation(gate[0:w, q, :], k.ps[0:w, 2 * q, :], ACT.Silu, scale=1.0 / WS).then_inc(s_gate, 1)
                    act.wait_ge(s_hid, m + 1)
                    if not first:
                        act.wait_ge(s_y, TB * n - TB)
                    nc.scalar.activation(hh[0:w, s, c, :], hid[0:w, q, :], ACT.Copy).then_inc(s_high, 1)

            def expert(e, s, last=False):
                for b in range(NB):
                    one_step(NB * e + b, b % 2, isinstance(e, int) and e == 0 and b < 2)
                    if b == 1 and not last:
                        split(e + 1, 1 - s)

            split(0, 0)
            expert(0, 0)
            with act.Fori(0, EA // 2 - 1) as i:
                expert(2 * i + 1, 1)
                expert(2 * i + 2, 0)
            expert(EA - 1, 1, last=True)

        @block.gpsimd
        def _(pool):
            with pool.Fori(0, NS // 2) as i:
                for s in range(2):
                    for c, (_, w) in enumerate(HCH):
                        pool.wait_ge(s_high, 2 * NHC * i + NHC * s + c + 1)
                        nc.gpsimd.tensor_tensor(hl[0:w, s, c, :], hid[0:w, (s + c) % 2, :], hh[0:w, s, c, :],
                                                ALU.subtract).then_inc(s_low, 1)

        @block.vector
        def _(dve):
            def split(e, s):
                dve.wait_ge(s_wh, e + 1)
                nc.vector.scalar_tensor_tensor(wl[:, s * NEW:(s + 1) * NEW], stage[:, s, :], WS, wh[:, s * NEW:(s + 1) * NEW],
                                               ALU.mult, ALU.subtract).then_inc(s_wl, 1)

            def hidden(n, s):
                for c, (_, w) in enumerate(HCH):
                    q = (s + c) % 2
                    wait(dve, s_low, NHC * n + c - 1)
                    dve.wait_ge(s_gate, NHC * n + c + 1)
                    nc.vector.tensor_tensor(hid[0:w, q, :], k.ps[0:w, 2 * q + 1, :], gate[0:w, q, :], ALU.mult).then_inc(s_hid, 1)

            def add(n, e, b, last):
                for j in range(TB):
                    t = b * TB + j
                    dve.wait_ge(s_y, TB * n + j + 1)
                    nc.vector.scalar_tensor_tensor(k.X[:, t, :], k.ps[:, 4 + j, 0:D], k.wexp[:, t, ds(e, 1)],
                                                   k.X[:, t, :], ALU.mult, ALU.add).then_inc(s_x, 1)
                    if last:
                        dve.wait_ge(s_x, TB * n + j + 1)
                        tile_stats(nc, k, t).then_inc(s_stats, 1)

            def expert(e, s, last=False):
                for b in range(NB):
                    n = NB * e + b
                    if not (last and b == NB - 1):
                        hidden(n + 1, (b + 1) % 2)
                    add(n, e, b, last)
                    if b == 1 and not last:
                        split(e + 1, 1 - s)

            split(0, 0)
            hidden(0, 0)
            expert(0, 0)
            with dve.Fori(0, EA // 2 - 1) as i:
                expert(2 * i + 1, 1)
                expert(2 * i + 2, 0)
            expert(EA - 1, 1, last=True)


def cross_attention(nc, k, a):
    normalise(nc, k, "n1")
    with ExitStack() as ctx:
        A = Heads(nc, k, ctx, "xa", 8, 32, True)
        cross_project(nc, k, a, A)
        attention(nc, k, A, k.xqk, "o", KD, k.negmask)


def experts(nc, k, a):
    normalise(nc, k, "n2")
    route(nc, k)
    expert_ffn(nc, k, a)


def self_attention(nc, k, a):
    normalise(nc, k, "n3")
    with ExitStack() as ctx:
        A = Heads(nc, k, ctx, "ma", 16, 16, False)
        self_project(nc, k, A)
        attention(nc, k, A, k.mqk, "mo", 0, None)
def depool(nc, k, a):
    normalise(nc, k, "n4", second=True, w=V_GRES)
    with ExitStack() as ctx:
        sb = lambda n, s, d=F32: ctx.enter_context(nc.sbuf_tensor("dp_" + n, s, d))
        sem = lambda n: ctx.enter_context(nc.semaphore("dp_" + n))
        patch_i, patch = sb("patch_i", [B, S], I32), sb("patch", [B, S])
        ends, neg = sb("ends", [B, S]), sb("neg", [B, S])
        ones, iota = sb("ones", [P, S]), sb("iota", [P, S])
        endT, qcol = sb("endT", [P, KD, B]), sb("qcol", [P, KD])
        hit = sb("hit", [P, 2, 2, S], BF16)
        mark, plug = sb("mark", [P, S]), sb("plug", [P, S])
        dist, M = sb("dist", [P, 2, S]), sb("M", [P, 2, 2, S])
        cx, junk = sb("cx", [P, NT, CD]), sb("junk", [P, CD])
        ss, u = sb("ss", [P, NT]), sb("u", [P, NT, D])
        s_patch, s_cx, s_step, s_turn, s_ss, s_rs = (sem(n) for n in ("patch", "cx", "step", "turn", "ss", "rs"))
        s_hit, s_cnt, s_arg, s_M, s_u, s_y, s_x, s_bin, s_mark, s_stats = (sem(n) for n in ("hit", "cnt", "arg", "M", "u", "y", "x", "bin", "mark", "stats"))
        block = ctx.enter_context(nc.Block())

        @block.sync
        def _(sp):
            sp.dma_start(patch_i[:], a["patch"]).then_inc(s_patch, 16)
            sp.dma_start(cx[:], a["ctx"].rearrange("(n p) d -> p n d", p=P)).then_inc(s_cx, 16)

        @block.scalar
        def _(act):
            act.wait_ge(s_cx, 16)
            for t in range(NT):
                if t:
                    act.wait_ge(s_ss, t)
                nc.scalar.activation(junk[:], cx[:, t, :], ACT.Square, accum_out=ss[:, t:t + 1]).then_inc(s_ss, 1)
            for b in range(B):
                act.wait_ge(s_arg, b + 1)
                if b >= 2:
                    act.wait_ge(s_y, 2 * (b - 1))
                nc.scalar.activation(M[:, b % 2], dist[:], ACT.Exp, scale=-DT).then_inc(s_M, 1)

        @block.gpsimd
        def _(pool):
            step = [0]

            def then(ins):
                step[0] += 1
                ins.then_inc(s_rs, 1)
                pool.wait_ge(s_rs, step[0])

            for t in range(NT):
                nc.gpsimd.tensor_tensor(k.X[:, t, :], k.X[:, t, :], k.rows[:, R_BIN, :], ALU.add).then_inc(s_bin, 1)
            pool.wait_ge(s_ss, NT)
            then(nc.gpsimd.tensor_scalar(ss[:], ss[:], 1.0 / CD, EPS, ALU.mult, ALU.add))
            then(nc.gpsimd.tensor_tensor(ss[:], ss[:], k.half[:], ALU.pow))
            then(nc.gpsimd.tensor_scalar(ss[:], ss[:], float(np.exp(LOGP)), None, ALU.mult))

        @block.vector
        def _(dve):
            step = [0]

            def then(ins):
                step[0] += 1
                ins.then_inc(s_step, 1)
                dve.wait_ge(s_step, step[0])

            then(nc.vector.memset(ones[:], 1.0))
            then(nc.vector.tensor_tensor_scan(iota[:], ones[:], ones[:], -1.0, ALU.mult, ALU.add))
            dve.wait_ge(s_patch, 16)
            then(nc.vector.tensor_copy(patch[:], patch_i[:]))
            then(nc.vector.tensor_tensor_scan(ends[:], ones[0:B, :], patch[:], -1.0, ALU.mult, ALU.add))
            then(nc.vector.tensor_scalar(neg[:], ends[:], 0.0, float(S), ALU.is_lt, ALU.mult))
            then(nc.vector.tensor_tensor(ends[:], ends[:], neg[:], ALU.add))
            dve.wait_ge(s_turn, 1)
            then(nc.vector.tensor_copy(endT[:], k.ps[:, 7, 0:KD * B].rearrange("p (c b) -> p c b", c=KD)))
            for c in range(KD):
                then(nc.vector.tensor_scalar(qcol[:, c:c + 1], k.ps[:, 7, P:P + 1], float(c * P), None, ALU.add))

            def hits(b):
                if b >= 2:
                    dve.wait_ge(s_cnt, b - 1)
                for c in range(KD):
                    nc.vector.tensor_scalar(hit[:, b % 2, c, :], iota[:], endT[:, c, b:b + 1], None, ALU.is_equal).then_inc(s_hit, 1)

            def distances(b):
                dve.wait_ge(s_cnt, b + 1)
                if b:
                    dve.wait_ge(s_M, b)
                then(nc.vector.tensor_scalar(mark[:], k.ps[:, 6, 0:S], 1.0, None, ALU.min))
                then(nc.vector.tensor_tensor_scan(plug[:], ones[:], mark[:], -1.0, ALU.mult, ALU.add))
                then(nc.vector.tensor_scalar(mark[:], plug[:], 0.0, float(S - 1), ALU.max, ALU.min))
                for c in range(KD):
                    then(nc.vector.tensor_scalar(plug[:], mark[:], qcol[:, c:c + 1], None, ALU.subtract))
                    ins = nc.vector.scalar_tensor_tensor(dist[:, c, :], plug[:], -1000.0, plug[:], ALU.mult, ALU.max)
                    if c == KD - 1:
                        ins.then_inc(s_arg, 1)
                        dve.wait_ge(s_arg, b + 1)
                    else:
                        then(ins)

            hits(0)
            dve.wait_ge(s_rs, 3)
            for b in range(B):
                if b + 1 < B:
                    hits(b + 1)
                distances(b)
                for t in (2 * b, 2 * b + 1):
                    nc.vector.scalar_tensor_tensor(u[:, t, :], cx[:, t, 0:D], ss[:, t:t + 1], k.rows[:, R_GI, :],
                                                   ALU.mult, ALU.mult).then_inc(s_u, 1)
                if b:
                    add(nc, k, dve, b - 1, s_y, s_x, s_bin, s_stats)
            add(nc, k, dve, B - 1, s_y, s_x, s_bin, s_stats)

        @block.tensor
        def _(pe):
            pe.wait_ge(s_step, 6)
            for c in range(KD):
                nc.tensor.transpose(k.ps[:, 7, c * B:(c + 1) * B], ends[:, c * P:(c + 1) * P], k.ident[0:B, 0:B])
            nc.tensor.transpose(k.ps[:, 7, P:2 * P], iota[:, 0:P], k.ident[:]).then_inc(s_turn, 1)

            def count(b):
                pe.wait_ge(s_hit, KD * (b + 1))
                if b:
                    pe.wait_ge(s_arg, b)
                for c in range(KD):
                    mm = nc.tensor.matmul(k.ps[:, 6, 0:S], k.ones16[:], hit[:, b % 2, c, :], start=c == 0, stop=c == KD - 1)
                mm.then_inc(s_cnt, 1)

            count(0)
            for b in range(B):
                if b + 1 < B:
                    count(b + 1)
                for tc in range(2):
                    t = 2 * b + tc
                    if b:
                        pe.wait_ge(s_x, 2 * (t - 1))
                    for kc in range(KD):
                        three_pass(nc, k.ps[:, 2 * tc, 0:D], lambda p: k.nT[p][:, kc, t * P:(t + 1) * P],
                                   lambda p: weight(k, "in", kc, p), kc == 0, kc == KD - 1)
                    pe.wait_ge(s_M, b + 1)
                    pe.wait_ge(s_u, 2 * b + 2)
                    for c in range(KD):
                        mm = nc.tensor.matmul(k.ps[:, 2 * tc + 1, 0:D], M[:, b % 2, c, tc * P:(tc + 1) * P], u[:, 2 * b + c, :],
                                              start=c == 0, stop=c == KD - 1)
                    mm.then_inc(s_y, 1)


def add(nc, k, dve, b, s_y, s_x, s_bin, s_stats):
    for tc in range(2):
        t = 2 * b + tc
        dve.wait_ge(s_y, t + 1)
        dve.wait_ge(s_bin, t + 1)
        nc.vector.scalar_tensor_tensor(k.X[:, t, :], k.ps[:, 2 * tc, 0:D], 1.0 / WS, k.X[:, t, :], ALU.mult, ALU.add).then_inc(s_x, 1)
        dve.wait_ge(s_x, 2 * t + 1)
        nc.vector.tensor_tensor(k.X[:, t, :], k.ps[:, 2 * tc + 1, 0:D], k.X[:, t, :], ALU.add).then_inc(s_x, 1)
        dve.wait_ge(s_x, 2 * t + 2)
        tile_stats(nc, k, t).then_inc(s_stats, 1)


def quant_ffn(nc, k, a, out):
    NQ = len(QCH)
    RMAX = bass.bass_isa.ReduceOp.max
    with ExitStack() as outer:
        keep = lambda n, s, d=F32: outer.enter_context(nc.sbuf_tensor("q_" + n, s, d))
        xqT = keep("xqT", [P, KD, T], BF16)
        wguT = keep("wguT", [P, 2, KD, HS], BF16)
        wdT = keep("wdT", [P, NQ, D], BF16)
        wsc = keep("wsc", [P, 14])
        drow = keep("drow", [P, D])
        clip = keep("clip", [P, 2])
        gmax, sx, sinv = keep("gmax", [P, 2]), keep("sx", [P, 2]), keep("sinv", [P, 2])
        hF = keep("hF", [P, NQ, T])
        hmax = keep("hmax", [P, NQ * NB])
        with ExitStack() as ctx:
            sb = lambda n, s, d=F32: ctx.enter_context(nc.sbuf_tensor("q1_" + n, s, d))
            sem = lambda n: ctx.enter_context(nc.semaphore("q1_" + n))
            W = sb("W", [P, 2 * NQ * D + KD * HS])
            winv, pmax = sb("winv", [P, 14]), sb("pmax", [P, 1])
            dve_stats, pool_stats = layer_stats(nc, k, "n5", ctx, False)
            s_w, s_step, s_scale, s_row, s_pmax, s_gmax, s_sig = (sem(n) for n in ("w", "step", "scale", "row", "pmax", "gmax", "sig"))
            s_wq, s_xq, s_tw, s_evac, s_rowin = (sem(n) for n in ("wq", "xq", "tw", "evac", "rowin"))
            s_xevac, s_tx = sem("xevac"), sem("tx")
            PARTS = [(c * D, D, c) for c in range(2 * NQ)] + [(2 * NQ * D + c * HS, HS, 12 + c) for c in range(KD)]
            TURNS = [(m * NQ * D + c * D + kc * P, w, P, wguT[:, m, kc, lo:lo + w])
                     for m in range(2) for c, (lo, w) in enumerate(QCH) for kc in range(KD)]
            TURNS += [(2 * NQ * D + r * HS + lo, P, w, wdT[0:w, c, r * P:(r + 1) * P])
                      for r in range(KD) for c, (lo, w) in enumerate(QCH)]
            xn = sb("xn", [P, NT, D])
            block = ctx.enter_context(nc.Block())

            @block.sync
            def _(sp):
                sp.dma_start(W[:, 0:NQ * D], a["wgate"].rearrange("p c d -> p (c d)")).then_inc(s_w, 16)
                sp.dma_start(W[:, NQ * D:2 * NQ * D], a["wup"].rearrange("p c d -> p (c d)")).then_inc(s_w, 16)
                sp.dma_start(W[:, 2 * NQ * D:], a["wdown"].rearrange("p c d -> p (c d)")).then_inc(s_w, 16)
                sp.dma_start(clip[:], a["clip"].to_broadcast([P, 2])).then_inc(s_w, 16)
                sp.wait_ge(s_scale, 1)
                for c in range(KD):
                    sp.dma_start(k.wsc[0:1, c * P:(c + 1) * P].rearrange("o p -> p o"), wsc[:, 12 + c:13 + c]).then_inc(s_row, 16)
                sp.wait_ge(s_row, 16 * KD)
                sp.dma_start(drow[:], k.wsc[0:1, :].to_broadcast([P, D])).then_inc(s_rowin, 16)
                sp.wait_ge(s_rowin, 16)

            @block.gpsimd
            def _(pool):
                pool_stats(pool)
                pool.wait_ge(s_pmax, 1)
                nc.gpsimd.partition_all_reduce(gmax[:, 0:1], pmax[:], P, RMAX).then_inc(s_gmax, 1)

            @block.scalar
            def _(act):
                act.wait_ge(s_w, 64)
                nc.scalar.activation(clip[:], clip[:], ACT.Sigmoid).then_inc(s_sig, 1)
                for n, (_, w_in, w_out, dst) in enumerate(TURNS):
                    act.wait_ge(s_tw, n + 1)
                    nc.scalar.activation(dst, k.ps[0:w_out if n >= 4 * NQ else P, n % 4, 0:P if n >= 4 * NQ else w_in],
                                         ACT.Copy).then_inc(s_evac, 1)

            @block.tensor
            def _(pe):
                for n, (src, w_in, w_out, _) in enumerate(TURNS):
                    pe.wait_ge(s_wq, 1)
                    if n >= 4:
                        pe.wait_ge(s_evac, n - 3)
                    nc.tensor.transpose(k.ps[0:w_out, n % 4, 0:w_in], W[0:w_in, src:src + w_out], k.ident[0:w_in, 0:w_in]).then_inc(s_tw, 1)
                for i in range(NB):
                    pe.wait_ge(s_xq, i + 1)
                    for c in range(KD):
                        q = 2 * i + c
                        if q >= 4:
                            pe.wait_ge(s_xevac, q - 3)
                        for j in range(TB):
                            mm = nc.tensor.transpose(k.ps[:, 4 + q % 4, j * P:(j + 1) * P], xn[:, i * TB + j, c * P:(c + 1) * P], k.ident[:])
                        mm.then_inc(s_tx, 1)

            @block.vector
            def _(dve):
                step = [0]

                def then(ins):
                    step[0] += 1
                    ins.then_inc(s_step, 1)
                    dve.wait_ge(s_step, step[0])

                dve_stats(dve)
                dve.wait_ge(s_w, 64)
                nc.vector.tensor_reduce(wsc[:, 0:12], W[:, 0:2 * NQ * D].rearrange("p (c d) -> p c d", d=D), AX, ALU.max,
                                        apply_absolute_value=True).then_inc(s_step, 1)
                step[0] += 1
                then(nc.vector.tensor_reduce(wsc[:, 12:14], W[:, 2 * NQ * D:].rearrange("p (c d) -> p c d", d=HS), AX, ALU.max,
                                             apply_absolute_value=True))
                ins = nc.vector.tensor_scalar(wsc[:], wsc[:], 1e-30, 1.0 / QMAX, ALU.max, ALU.mult)
                ins.then_inc(s_scale, 1)
                dve.wait_ge(s_scale, 1)
                then(nc.vector.reciprocal(winv[:], wsc[:]))
                for lo, n, s in PARTS:
                    last = nc.vector.tensor_scalar(W[:, lo:lo + n], W[:, lo:lo + n], winv[:, s:s + 1], MAGIC, ALU.mult, ALU.add)
                    last.then_inc(s_step, 1)
                    step[0] += 1
                dve.wait_ge(s_step, step[0])
                then(nc.vector.tensor_scalar(W[:], W[:], MAGIC - QMAX - 1.0, MAGIC + QMAX, ALU.max, ALU.min))
                nc.vector.tensor_scalar(W[:], W[:], MAGIC, None, ALU.subtract).then_inc(s_wq, 1)
                dve.wait_ge(k.s_fac, 2)
                for t in range(NT):
                    nc.vector.tensor_scalar(xn[:, t, :], k.X[:, t, :], k.mv[:, t, 0:1], k.fac[:, t:t + 1],
                                            ALU.subtract, ALU.mult).then_inc(s_step, 1)
                    step[0] += 1
                dve.wait_ge(s_step, step[0])
                nc.vector.tensor_reduce(pmax[:], xn[:].rearrange("p t d -> p (t d)"), AX, ALU.max, apply_absolute_value=True).then_inc(s_pmax, 1)
                dve.wait_ge(s_gmax, 1)
                dve.wait_ge(s_sig, 1)
                then(nc.vector.scalar_tensor_tensor(sx[:, 0:1], gmax[:, 0:1], 1.0 / QMAX, clip[:, 0:1], ALU.mult, ALU.mult))
                then(nc.vector.reciprocal(sinv[:, 0:1], sx[:, 0:1]))
                then(nc.vector.tensor_scalar(wsc[:, 0:12], wsc[:, 0:12], sx[:, 0:1], None, ALU.mult))
                for i in range(NB):
                    v = xn[:, i * TB:(i + 1) * TB, :].rearrange("p t d -> p (t d)")
                    then(nc.vector.tensor_scalar(v, v, sinv[:, 0:1], MAGIC, ALU.mult, ALU.add))
                    then(nc.vector.tensor_scalar(v, v, MAGIC - QMAX - 1.0, MAGIC + QMAX, ALU.max, ALU.min))
                    nc.vector.tensor_scalar(v, v, MAGIC, None, ALU.subtract).then_inc(s_xq, 1)
                for q in range(KD * NB):
                    dve.wait_ge(s_tx, q + 1)
                    i, c = q // KD, q % KD
                    nc.vector.tensor_copy(xqT[:, c, i * BLK:(i + 1) * BLK], k.ps[:, 4 + q % 4, :]).then_inc(s_xevac, 1)

        with ExitStack() as ctx:
            sem = lambda n: ctx.enter_context(nc.semaphore("q2_" + n))
            gate = ctx.enter_context(nc.sbuf_tensor("q2_gate", [P, 2, BLK], F32))
            s_gu, s_gate, s_h, s_max = sem("gu"), sem("gate"), sem("h"), sem("max")
            block = ctx.enter_context(nc.Block())

            @block.tensor
            def _(pe):
                def one_block(i):
                    for c, (lo, w) in enumerate(QCH):
                        pair = 2 * (c % 2)
                        wait(pe, s_h, NQ * i + c - 1)
                        for m in range(2):
                            for kc in range(KD):
                                mm = nc.tensor.matmul(k.ps[0:w, pair + m, :], wguT[:, m, kc, lo:lo + w],
                                                      xqT[:, kc, ds(i * BLK, BLK)], start=kc == 0, stop=kc == KD - 1)
                        mm.then_inc(s_gu, 1)

                peeled(pe, NB, one_block)

            @block.scalar
            def _(act):
                def one_block(i):
                    for c, (lo, w) in enumerate(QCH):
                        act.wait_ge(s_gu, NQ * i + c + 1)
                        wait(act, s_h, NQ * i + c - 1)
                        nc.scalar.activation(gate[0:w, c % 2, :], k.ps[0:w, 2 * (c % 2), :], ACT.Silu,
                                             scale=wsc[0:w, c:c + 1]).then_inc(s_gate, 1)

                peeled(act, NB, one_block)

            @block.vector
            def _(dve):
                nc.vector.memset(hmax[:], 0.0).then_inc(s_max, 1)
                dve.wait_ge(s_max, 1)
                with dve.Fori(0, NB) as i:
                    for c, (lo, w) in enumerate(QCH):
                        dve.wait_ge(s_gate, NQ * i + c + 1)
                        nc.vector.scalar_tensor_tensor(hF[0:w, c, ds(i * BLK, BLK)], k.ps[0:w, 2 * (c % 2) + 1, :], wsc[0:w, NQ + c:NQ + c + 1],
                                                       gate[0:w, c % 2, :], ALU.mult, ALU.mult).then_inc(s_h, 1)
                        dve.wait_ge(s_h, NQ * i + c + 1)
                        nc.vector.tensor_reduce(hmax[0:w, ds(NQ * i + c, 1)], hF[0:w, c, ds(i * BLK, BLK)], AX, ALU.max,
                                                apply_absolute_value=True).then_inc(s_max, 1)

        with ExitStack() as ctx:
            sem = lambda n: ctx.enter_context(nc.semaphore("q3_" + n))
            pmax = ctx.enter_context(nc.sbuf_tensor("q3_pmax", [P, 1], F32))
            hq = ctx.enter_context(nc.sbuf_tensor("q3_hq", [P, NQ, T], BF16))
            y = ctx.enter_context(nc.sbuf_tensor("q3_y", [P, NT, D], F32))
            s_pmax, s_gmax, s_step, s_rnd, s_clip, s_hq, s_y, s_t, s_out = (sem(n) for n in ("pmax", "gmax", "step", "rnd", "clip", "hq", "y", "t", "out"))
            s_res = sem("res")
            block = ctx.enter_context(nc.Block())

            @block.gpsimd
            def _(pool):
                pool.wait_ge(s_pmax, 1)
                nc.gpsimd.partition_all_reduce(gmax[:, 1:2], pmax[:], P, RMAX).then_inc(s_gmax, 1)

            @block.vector
            def _(dve):
                nc.vector.tensor_reduce(pmax[:], hmax[:], AX, ALU.max).then_inc(s_pmax, 1)
                dve.wait_ge(s_gmax, 1)
                nc.vector.scalar_tensor_tensor(sx[:, 1:2], gmax[:, 1:2], 1.0 / QMAX, clip[:, 1:2], ALU.mult, ALU.mult).then_inc(s_step, 1)
                dve.wait_ge(s_step, 1)
                nc.vector.reciprocal(sinv[:, 1:2], sx[:, 1:2]).then_inc(s_step, 1)
                dve.wait_ge(s_step, 2)
                nc.vector.tensor_scalar(drow[:], drow[:], sx[:, 1:2], None, ALU.mult).then_inc(s_step, 1)
                for i in range(NB):
                    for c, (lo, w) in enumerate(QCH):
                        n = NQ * i + c
                        v = hF[0:w, c, i * BLK:(i + 1) * BLK]
                        nc.vector.tensor_scalar(v, v, sinv[0:w, 1:2], MAGIC, ALU.mult, ALU.add).then_inc(s_rnd, 1)
                    for c, (lo, w) in enumerate(QCH):
                        n = NQ * i + c
                        v = hF[0:w, c, i * BLK:(i + 1) * BLK]
                        dve.wait_ge(s_rnd, n + 1)
                        nc.vector.tensor_scalar(v, v, MAGIC - QMAX - 1.0, MAGIC + QMAX, ALU.max, ALU.min).then_inc(s_clip, 1)
                dve.wait_ge(s_step, 3)
                for t in range(NT):
                    dve.wait_ge(s_y, t + 1)
                    nc.vector.tensor_tensor(y[:, t, :], k.ps[:, t % 8, 0:D], drow[:], ALU.mult).then_inc(s_t, 1)
                    dve.wait_ge(s_t, t + 1)
                    nc.vector.tensor_tensor(y[:, t, :], y[:, t, :], k.X[:, t, :], ALU.add).then_inc(s_res, 1)

            @block.scalar
            def _(act):
                for i in range(NB):
                    for c, (lo, w) in enumerate(QCH):
                        act.wait_ge(s_clip, NQ * i + c + 1)
                        nc.scalar.activation(hq[0:w, c, i * BLK:(i + 1) * BLK], hF[0:w, c, i * BLK:(i + 1) * BLK], ACT.Copy,
                                             bias=-MAGIC).then_inc(s_hq, 1)

            @block.tensor
            def _(pe):
                for t in range(NT):
                    pe.wait_ge(s_hq, NQ * (t // TB + 1))
                    if t >= 8:
                        pe.wait_ge(s_t, t - 7)
                    for c, (lo, w) in enumerate(QCH):
                        mm = nc.tensor.matmul(k.ps[:, t % 8, 0:D], hq[0:w, c, t * P:(t + 1) * P], wdT[0:w, c, :],
                                              start=c == 0, stop=c == NQ - 1)
                    mm.then_inc(s_y, 1)

            @block.sync
            def _(sp):
                o = out.rearrange("(n p) d -> p n d", p=P)
                for i in range(NB):
                    sp.wait_ge(s_res, TB * (i + 1))
                    sp.dma_start(o[:, i * TB:(i + 1) * TB, :], y[:, i * TB:(i + 1) * TB, :]).then_inc(s_out, 16)
                sp.wait_ge(s_out, 16 * NB)
def build(nc, a, out, stop=None):
    with ExitStack() as ctx:
        def sb(name, shape, dt=F32):
            return ctx.enter_context(nc.sbuf_tensor(name, shape, dt))

        k = Shared()
        k.X = sb("X", [P, NT, D])
        k.nT = [sb("nT_high", [P, KD, T], F16), sb("nT_low", [P, KD, T], F16)]
        k.sw = [sb("sw_high", [P, NSW], F16), sb("sw_low", [P, NSW], F16)]
        k.ident, k.identb = sb("ident", [P, P]), sb("identb", [P, P], BF16)
        k.half, k.ones = sb("half", [P, NT]), sb("ones", [P, 32])
        k.ones16 = sb("ones16", [P, P], BF16)
        k.st, k.mv = sb("st", [P, NT, 6]), sb("mv", [P, NT, 2])
        k.r1, k.fac = sb("r1", [P, NT]), sb("fac", [P, NT])
        k.V = sb("V", [P, NT, D])
        k.mask_col, k.wexp = sb("mask_col", [P, NT]), sb("wexp", [P, NT, EA])
        dram = lambda n, s, d: nc.dram_tensor(n, s, d, kind="Internal").ap()
        k.xqk, k.mqk = dram("xqk", (2, 8, 2 * 32, T), F16), dram("mqk", (2, 16, 2 * 16, T), F16)
        k.negmask = dram("negmask", (B, S), F16)
        k.wsc = dram("wsc", (1, D), F32)
        k.vec = sb("vec", [P, 14])
        k.rows = sb("rows", [P, 6, D])
        k.ps = ctx.enter_context(nc.psum_tensor("ps", [P, 8, 512], F32))

        def clear_semaphores():
            with nc.Block() as block:
                @block.gpsimd
                def _(pool):
                    pool.sem_clear(range(first, 256))

        with nc.semaphore("first") as f:
            first = f.num
        stages = [
            ("prepare", lambda: prepare(nc, k, a)),
            ("ssm_norm", lambda: normalise(nc, k, "n0", second=True, w=V_LNW, b=V_LNB)),
            ("ssm", lambda: ssm(nc, k)),
            ("xat", lambda: cross_attention(nc, k, a)),
            ("moe", lambda: experts(nc, k, a)),
            ("mha", lambda: self_attention(nc, k, a)),
            ("clear", clear_semaphores),
            ("dep", lambda: depool(nc, k, a)),
            ("ffn", lambda: quant_ffn(nc, k, a, out)),
        ]
        for name, stage in stages:
            stage()
            if name == stop and name != "ffn":
                with nc.semaphore("dbg") as s, nc.Block() as block:
                    @block.sync
                    def _(sp):
                        sp.dma_start(out.rearrange("(n p) d -> p n d", p=P), k.X[:]).then_inc(s, 16)
                        sp.wait_ge(s, 16)
                return


def lay_out(i):
    g = {n: np.asarray(v) for n, v in i.items()}
    f = np.float32

    def chunks(w):
        kk, m = w.shape
        return w.reshape(kk // P, P, m).transpose(1, 0, 2).reshape(P, -1)

    heads = lambda w: w.transpose(1, 0, 2).reshape(D, D)
    mo = np.zeros((16, 32, D), f)
    mo[:, :16] = g["L1_attn_W_out"]
    sw = np.concatenate([chunks(w) for w in (
        g["L0_attn_W_alpha_w"].T, g["L0_attn_W_B_w"].T, g["L0_attn_W_C_w"].T,
        g["L0_xattn_W_src"].T, g["L0_xattn_W_tgt"].T, g["L0_xattn_W_out"].T,
        heads(g["L1_attn_W_query"]), heads(g["L1_attn_W_key"]), heads(g["L1_attn_W_val"]),
        mo.reshape(512, D), g["L1_xattn_W_in"].T, g["L0_ffn_Wg"])], axis=1)
    up = lambda w, s: np.concatenate([w, s.reshape(D, 2, H).transpose(1, 0, 2)])
    w1, w2 = up(g["L0_ffn_W1"], g["L0_ffn_Ws1"]), up(g["L0_ffn_W2"], g["L0_ffn_Ws2"])
    w3 = np.zeros((EA, NHC * P, D), f)
    w3[:E, :H] = g["L0_ffn_W3"]
    w3[E:, :H] = g["L0_ffn_Ws3"].reshape(2, H, D)
    mw = np.concatenate([chunks(m[e]) for e in range(EA) for m in (w1, w2, w3)], axis=1)
    vec = np.concatenate([g[n][:D].reshape(2, P).T for n in (
        "L0_attn_ln_w", "L0_attn_ln_b", "L0_attn_W_alpha_b", "L0_attn_W_B_b", "L0_xattn_b_tgt",
        "L0_xattn_b_src", "L1_xattn_g_res")], axis=1)
    rows = np.stack([g["L0_attn_W_C_b"], g["L0_attn_D_param"], g["L0_xattn_b_src"][D:], g["L0_xattn_b_out"],
                     g["L1_xattn_b_in"], g["L1_xattn_g_init"][:D]])

    def rowtiles(w):
        o = np.zeros((P, len(QCH), D), f)
        for c, (lo, n) in enumerate(QCH):
            o[:n, c] = w[lo:lo + n]
        return o

    return {k: np.ascontiguousarray(v) for k, v in {
        "x": g["x"].reshape(T, D), "sw": sw, "mw": mw, "vec": vec, "rows": rows,
        "ctxT": g["ctx_2048"].reshape(T, KC, P).transpose(2, 1, 0), "ctx": g["ctx_2048"].reshape(T, CD),
        "mask": g["mask_BxS2_fk1"], "maskT": g["mask_BxS2_fk1"].reshape(NT, P).T, "patch": g["mask_BxS2_if0"],
        "wgate": rowtiles(g["L1_ffn_w_gate"]), "wup": rowtiles(g["L1_ffn_w_up"]),
        "wdown": g["L1_ffn_w_down"].reshape(KD, P, HS).transpose(1, 0, 2),
        "clip": np.stack([g["L1_ffn_clip_x"], g["L1_ffn_clip_down"]], axis=1),
    }.items()}


def program(nc, arrays, stop=None):
    a = {n: nc.dram_tensor("in_" + n, v.shape, mybir.dt.from_np(v.dtype), kind="ExternalInput").ap() for n, v in arrays.items()}
    out = nc.dram_tensor("y", (T, D), F32, kind="ExternalOutput").ap()
    build(nc, a, out, stop)
    return nc


def kernel(**inputs):
    import concourse.bacc as _bacc
    from concourse.bass_utils import run_bass_kernel_spmd as _run

    arrays = lay_out(inputs)
    nc = _bacc.Bacc("TRN2", target_bir_lowering=False, num_devices=1)
    program(nc, arrays)
    r = _run(nc, [{"in_" + n: v for n, v in arrays.items()}], core_ids=[0])
    return r.results[0]["y"].reshape(B, S, D)
```

```python
from contextlib import ExitStack

import numpy as np
import concourse.bass as bass
from concourse import mybir

F32, F16, BF16, I32 = mybir.dt.float32, mybir.dt.float16, mybir.dt.bfloat16, mybir.dt.int32
ALU = mybir.AluOpType
ACT = mybir.ActivationFunctionType
AX = mybir.AxisListType.X
ds = bass.ds

P = 128
B, S, D, CD = 8, 256, 256, 512
T = B * S
NT = T // P
BLK = 512
NB = T // BLK
TB = BLK // P
KD, KC = D // P, CD // P
E, H = 8, 352
EA = E + 2
HCH = [(0, 128), (128, 128), (256, 96)]
NHC = len(HCH)
HS = 2 * H
QCH = [(0, 128), (128, 128), (256, 128), (384, 128), (512, 96), (608, 96)]
EPS = 1e-5
WS = 64.0
NEG = -60000.0
QMAX = 127.0
MAGIC = 1.5 * 2.0 ** 23

SW = {}
for _n, _k, _m in (("a", KD, D), ("b", KD, D), ("c", KD, D), ("src", KC, 2 * D), ("tgt", KD, D),
                   ("o", 2 * KD, D), ("q", KD, D), ("k", KD, D), ("v", KD, D), ("mo", 4, D),
                   ("in", KD, D), ("g", KD, E)):
    SW[_n] = (sum(k * m for _, k, m in SW.values()), _k, _m)
NSW = sum(k * m for _, k, m in SW.values())
NEW = 2 * KD * H + NHC * D

V_LNW, V_LNB, V_BA, V_BB, V_BTGT, V_BSRC, V_GRES = 0, 2, 4, 6, 8, 10, 12
R_BC, R_D, R_BV, R_BO, R_BIN, R_GI = range(6)

LOGP = np.float32(-0.001)
DT = float(-np.log(-np.expm1(LOGP)))


def weight(k, name, kc, part):
    off, _, m = SW[name]
    return k.sw[part][:, off + kc * m:off + (kc + 1) * m]


class Shared:
    pass


def wait(eng, sem, count):
    if not (isinstance(count, int) and count <= 0):
        eng.wait_ge(sem, count)


def peeled(eng, n, step):
    step(0)
    with eng.Fori(1, n) as i:
        step(i)


PASSES = ((0, 0), (0, 1), (1, 0))


SSM_CUT = SW["src"][0]
FIRST = [(SSM_CUT * i // 2, SSM_CUT * (i + 1) // 2) for i in range(2)]
OTHERS = [(SSM_CUT + (NSW - SSM_CUT) * i // 6, SSM_CUT + (NSW - SSM_CUT) * (i + 1) // 6) for i in range(6)]


def split_high(nc, k, stage, piece):
    lo, hi = piece
    return nc.scalar.activation(k.sw[0][:, lo:hi], stage[:, lo:hi], ACT.Copy, scale=WS)


def split_low(nc, k, stage, piece):
    lo, hi = piece
    return nc.vector.scalar_tensor_tensor(k.sw[1][:, lo:hi], stage[:, lo:hi], WS, k.sw[0][:, lo:hi], ALU.mult, ALU.subtract)


def prepare(nc, k, a, stage, others_in):
    with ExitStack() as ctx:
        sem = lambda n: ctx.enter_context(nc.semaphore(n))
        rest_in, stats, high, low, made = (sem(n) for n in ("rest_in", "stats", "w_high", "w_low", "const_made"))
        x_in = [sem(f"x_in{i}") for i in range(NB)]
        w_in = [sem(f"w_in{i}") for i in range(len(FIRST))]
        patch_in, ends_made, ends_turned = sem("patch_in"), sem("ends_made"), sem("ends_turned")
        patch_i, patch, ends, wrap = (ctx.enter_context(nc.sbuf_tensor(n, [B, S], d)) for n, d in
                                      (("patch_i", I32), ("patch", F32), ("ends", F32), ("wrap", F32)))
        ones = ctx.enter_context(nc.sbuf_tensor("pr_ones", [P, S], F32))
        aggregated = sem("aggregated")
        block = ctx.enter_context(nc.Block())

        @block.sync
        def _(sp):
            sp.dma_start(patch_i[:], a["patch"]).then_inc(patch_in, 16)
            x = a["x"].rearrange("(n p) d -> p n d", p=P)
            for i in range(NB):
                sp.dma_start(k.X[:, i * TB:(i + 1) * TB, :], x[:, i * TB:(i + 1) * TB, :]).then_inc(x_in[i], 16)
            for (lo, hi), piece_in in zip(FIRST, w_in):
                sp.dma_start(stage[:, lo:hi], a["sw"][:, lo:hi]).then_inc(piece_in, 16)
            sp.dma_start(k.vec[:], a["vec"]).then_inc(rest_in, 16)
            for r in range(6):
                sp.dma_start(k.rows[:, r, :], a["rows"][r:r + 1, :].to_broadcast([P, D])).then_inc(rest_in, 16)
            for (lo, hi), piece_in in zip(OTHERS, others_in):
                sp.dma_start(stage[:, lo:hi], a["sw"][:, lo:hi]).then_inc(piece_in, 16)
            sp.wait_ge(rest_in, 16 * 7)

        @block.scalar
        def _(act):
            for i, piece in enumerate(FIRST):
                act.wait_ge(w_in[i], 16)
                split_high(nc, k, stage, piece).then_inc(high, 1)

        @block.vector
        def _(dve):
            nc.vector.memset(k.ones[:], 1.0)
            nc.vector.memset(k.ones16[:], 1.0)
            step = [0]

            def then(ins):
                step[0] += 1
                ins.then_inc(ends_made, 1)
                dve.wait_ge(ends_made, step[0])

            then(nc.vector.memset(ones[:], 1.0))
            then(nc.vector.tensor_tensor_scan(k.iota[:], ones[:], ones[:], -1.0, ALU.mult, ALU.add))
            dve.wait_ge(patch_in, 16)
            then(nc.vector.tensor_copy(patch[:], patch_i[:]))
            then(nc.vector.tensor_tensor_scan(ends[:], ones[0:B, :], patch[:], -1.0, ALU.mult, ALU.add))
            then(nc.vector.tensor_scalar(wrap[:], ends[:], 0.0, float(S), ALU.is_lt, ALU.mult))
            then(nc.vector.tensor_tensor(ends[:], ends[:], wrap[:], ALU.add))
            dve.wait_ge(ends_turned, 1)
            then(nc.vector.tensor_copy(k.endT[:], k.ps[:, 7, 0:KD * B].rearrange("p (c b) -> p c b", c=KD)))
            for c in range(KD):
                then(nc.vector.tensor_scalar(k.qcol[:, c:c + 1], k.ps[:, 7, P:P + 1], float(c * P), None, ALU.add))
            for i in range(NB):
                dve.wait_ge(x_in[i], 16)
                for t in range(i * TB, (i + 1) * TB):
                    tile_stats(nc, k, t).then_inc(stats, 1)
            dve.wait_ge(stats, NT)
            aggregate(nc, k, aggregated)
            for i, piece in enumerate(FIRST):
                dve.wait_ge(high, i + 1)
                split_low(nc, k, stage, piece).then_inc(low, 1)

        @block.tensor
        def _(pe):
            pe.wait_ge(made, 3)
            pe.wait_ge(ends_made, 6)
            for c in range(KD):
                nc.tensor.transpose(k.ps[:, 7, c * B:(c + 1) * B], ends[:, c * P:(c + 1) * P], k.ident[0:B, 0:B])
            nc.tensor.transpose(k.ps[:, 7, P:2 * P], k.iota[:, 0:P], k.ident[:]).then_inc(ends_turned, 1)

        @block.gpsimd
        def _(pool):
            nc.gpsimd.memset(k.ident[:], 0.0).then_inc(made, 1)
            nc.gpsimd.memset(k.half[:], -0.5).then_inc(made, 1)
            pool.wait_ge(made, 1)
            nc.gpsimd.affine_select(out=k.ident[:], in_=k.ident[:], compare_op=ALU.not_equal, fill=1.0,
                                    base=0, pattern=[[-1, P]], channel_multiplier=1).then_inc(made, 1)
            pool.wait_ge(made, 3)
            nc.gpsimd.tensor_copy(k.identb[:], k.ident[:]).then_inc(made, 1)


def tile_stats(nc, k, t):
    return nc.vector.bn_stats(k.st[:, ds(t, 1), :], k.X[:, ds(t, 1), :])


def aggregate(nc, k, done):
    for t in range(NT):
        nc.vector.bn_aggr(k.mv[:, t, :], k.st[:, t, :]).then_inc(done, 1)


def layer_stats(nc, k, tag, ctx, second, aggregated=False):
    sem = lambda n: ctx.enter_context(nc.semaphore(f"{tag}_{n}"))
    s_aggr, k.s_rstd, k.s_fac = sem("aggr"), sem("rstd"), sem("fac")

    def dve_part(dve):
        if not aggregated:
            aggregate(nc, k, s_aggr)

    def pool_part(pool):
        step = [0]

        def then(ins):
            step[0] += 1
            ins.then_inc(k.s_rstd, 1)
            pool.wait_ge(k.s_rstd, step[0])

        for ts in (slice(i * TB, (i + 1) * TB) for i in range(NB)):
            r1, fac, var, half = k.r1[:, ts], k.fac[:, ts], k.mv[:, ts, 1], k.half[:, ts]
            if not aggregated:
                pool.wait_ge(s_aggr, ts.stop)
            then(nc.gpsimd.tensor_scalar(r1, var, EPS, None, ALU.add))
            then(nc.gpsimd.tensor_tensor(r1, r1, half, ALU.pow))
            if not second:
                nc.gpsimd.tensor_copy(fac, r1).then_inc(k.s_fac, 1)
                continue
            then(nc.gpsimd.tensor_tensor(fac, r1, r1, ALU.mult))
            then(nc.gpsimd.tensor_tensor(fac, fac, var, ALU.mult))
            then(nc.gpsimd.tensor_scalar(fac, fac, EPS, None, ALU.add))
            then(nc.gpsimd.tensor_tensor(fac, fac, half, ALU.pow))
            nc.gpsimd.tensor_tensor(fac, fac, r1, ALU.mult).then_inc(k.s_fac, 1)

    return dve_part, pool_part


def normalise(nc, k, tag, second=False, w=None, b=None, aggregated=False, loads=None):
    with ExitStack() as ctx:
        sem = lambda n: ctx.enter_context(nc.semaphore(f"{tag}_{n}"))
        xn = ctx.enter_context(nc.sbuf_tensor(f"{tag}_xn", [P, NT, D], F32))
        full = ctx.enter_context(nc.sbuf_tensor(f"{tag}_full", [P, 2, KD, BLK], F32)) if b is not None else None
        dve_stats, pool_stats = layer_stats(nc, k, tag, ctx, second, aggregated)
        s_xn, s_turned, s_full, s_high, s_low = sem("xn"), sem("turned"), sem("full"), sem("high"), sem("low")
        block = ctx.enter_context(nc.Block())
        high, low = ([part[:, :, i * BLK:(i + 1) * BLK] for i in range(NB)] for part in k.nT)

        if loads:
            @block.sync
            def _(sp):
                loads(sp)

        def banks(i):
            return k.ps[:, KD * i:KD * i + KD, :]

        @block.vector
        def _(dve):
            def scaled(i):
                dve.wait_ge(k.s_fac, i + 1)
                for t in range(i * TB, (i + 1) * TB):
                    nc.vector.tensor_scalar(xn[:, t, :], k.X[:, t, :], k.mv[:, t, 0:1], k.fac[:, t:t + 1],
                                            ALU.subtract, ALU.mult).then_inc(s_xn, 1)

            def low_part(i):
                dve.wait_ge(s_high, KD * (i + 1))
                if b is not None:
                    nc.vector.tensor_tensor(low[i], full[:, i % 2], high[i], ALU.subtract).then_inc(s_low, KD)
                elif w is not None:
                    for c in range(KD):
                        nc.vector.scalar_tensor_tensor(low[i][:, c], banks(i)[:, c], k.vec[:, w + c:w + c + 1], high[i][:, c],
                                                       ALU.mult, ALU.subtract).then_inc(s_low, 1)
                else:
                    nc.vector.tensor_tensor(low[i], banks(i), high[i], ALU.subtract).then_inc(s_low, KD)

            dve_stats(dve)
            for i in range(NB - 1):
                scaled(i)
            low_part(0)
            scaled(NB - 1)
            for i in range(1, NB):
                low_part(i)

        @block.gpsimd
        def _(pool):
            pool_stats(pool)

        @block.tensor
        def _(pe):
            for i in range(NB):
                pe.wait_ge(s_xn, TB * (i + 1))
                for c in range(KD):
                    for j in range(TB):
                        t = nc.tensor.transpose(k.ps[:, KD * i + c, j * P:(j + 1) * P],
                                                xn[:, i * TB + j, c * P:(c + 1) * P], k.ident[:])
                    t.then_inc(s_turned, 1)

        @block.scalar
        def _(act):
            for i in range(NB):
                act.wait_ge(s_turned, KD * (i + 1))
                if b is not None:
                    wait(act, s_low, KD * (i - 1))
                    for c in range(KD):
                        nc.scalar.activation(full[:, i % 2, c, :], banks(i)[:, c], ACT.Identity, scale=k.vec[:, w + c:w + c + 1],
                                             bias=k.vec[:, b + c:b + c + 1]).then_inc(s_full, 1)
                    act.wait_ge(s_full, KD * (i + 1))
                    nc.scalar.activation(high[i], full[:, i % 2], ACT.Copy).then_inc(s_high, KD)
                elif w is not None:
                    for c in range(KD):
                        nc.scalar.activation(high[i][:, c], banks(i)[:, c], ACT.Copy, scale=k.vec[:, w + c:w + c + 1]).then_inc(s_high, 1)
                else:
                    nc.scalar.activation(high[i], banks(i), ACT.Copy).then_inc(s_high, KD)


def ssm(nc, k, stage, others_in):
    with ExitStack() as ctx:
        sb = lambda n, s, d=F32: ctx.enter_context(nc.sbuf_tensor("ssm_" + n, s, d))
        sem = lambda n: ctx.enter_context(nc.semaphore("ssm_" + n))
        alpha, u, h = sb("alpha", [P, KD, T]), sb("u", [P, KD, T]), sb("h", [P, KD, T])
        h_split = [sb("hh", [P, KD, T], F16), sb("hl", [P, KD, T], F16)]
        xbc, res = sb("xbc", [P, NT, D]), sb("res", [P, 2, D])
        s_au, s_evac, s_scan, s_high, s_low = sem("au"), sem("evac"), sem("scan"), sem("high"), sem("low")
        s_y, s_x, s_res, s_st, s_bc = sem("y"), sem("x"), sem("res"), sem("st"), sem("bc")
        s_whigh, s_wlow = sem("whigh"), sem("wlow")
        block = ctx.enter_context(nc.Block())
        AU = (("a", V_BA, ACT.Sigmoid, alpha), ("b", V_BB, ACT.Identity, u))

        @block.tensor
        def _(pe):
            def alpha_u(i):
                wait(pe, s_evac, 4 * i)
                for m, (name, _, _, _) in enumerate(AU):
                    for c in range(KD):
                        n = 0
                        for kc in range(KD):
                            for pw, px in PASSES:
                                mm = nc.tensor.matmul(k.ps[:, 2 * m + c, :],
                                                      weight(k, name, kc, pw)[:, c * P:(c + 1) * P],
                                                      k.nT[px][:, kc, ds(i * BLK, BLK)],
                                                      start=n == 0, stop=n == 5)
                                n += 1
                        mm.then_inc(s_au, 1)

            def y(i):
                pe.wait_ge(s_low, i + 1)
                wait(pe, s_x, TB * i)
                for j in range(TB):
                    n = 0
                    for kc in range(KD):
                        for ph, pw in PASSES:
                            mm = nc.tensor.matmul(k.ps[:, 4 + j, 0:D], h_split[ph][:, kc, ds(i * BLK + j * P, P)],
                                                  weight(k, "c", kc, pw), start=n == 0, stop=n == 5)
                            n += 1
                    mm.then_inc(s_y, 1)

            alpha_u(0)
            alpha_u(1)
            y(0)
            with pe.Fori(2, NB) as i:
                alpha_u(i)
                y(i - 1)
            y(NB - 1)

        @block.scalar
        def _(act):
            for i, piece in enumerate(OTHERS):
                act.wait_ge(others_in[i], 16)
                split_high(nc, k, stage, piece).then_inc(s_whigh, 1)
            with act.Fori(0, NB) as i:
                for m, (_, bias, fn, dst) in enumerate(AU):
                    for c in range(KD):
                        act.wait_ge(s_au, 4 * i + 2 * m + c + 1)
                        nc.scalar.activation(dst[:, c, ds(i * BLK, BLK)], k.ps[:, 2 * m + c, :], fn,
                                             scale=1.0 / WS, bias=k.vec[:, bias + c:bias + c + 1]).then_inc(s_evac, 1)

        @block.gpsimd
        def _(pool):
            with pool.Fori(0, NT) as t:
                nc.gpsimd.tensor_tensor(xbc[:, ds(t, 1), :], k.X[:, ds(t, 1), :], k.rows[:, R_BC, :], ALU.add).then_inc(s_bc, 1)
            with pool.Fori(0, NB) as i:
                cols = ds(i * BLK, BLK)
                pool.wait_ge(s_scan, 4 * i + 4)
                nc.gpsimd.tensor_copy(h_split[0][:, :, cols], h[:, :, cols]).then_inc(s_high, 1)
                pool.wait_ge(s_high, i + 1)
                nc.gpsimd.tensor_tensor(h_split[1][:, :, cols], h[:, :, cols], h_split[0][:, :, cols],
                                        ALU.subtract).then_inc(s_low, 1)

        @block.vector
        def _(dve):
            def scans(i):
                dve.wait_ge(s_evac, 4 * i + 4)
                for c in range(KD):
                    for b in range(BLK // S):
                        cols = ds(i * BLK + b * S, S)
                        nc.vector.tensor_tensor_scan(h[:, c, cols], alpha[:, c, cols], u[:, c, cols], 0.0,
                                                     ALU.mult, ALU.add).then_inc(s_scan, 1)

            def residual(i):
                for j in range(TB):
                    n = i * TB + j
                    t = ds(n, 1)
                    nc.vector.scalar_tensor_tensor(res[:, 0, :], k.X[:, t, :], k.mv[:, t, 0], k.rows[:, R_D, :],
                                                   ALU.subtract, ALU.mult).then_inc(s_res, 1)
                    dve.wait_ge(s_res, 2 * n + 1)
                    dve.wait_ge(s_bc, n + 1)
                    nc.vector.scalar_tensor_tensor(res[:, 1, :], res[:, 0, :], k.r1[:, t], xbc[:, t, :],
                                                   ALU.mult, ALU.add).then_inc(s_res, 1)
                    dve.wait_ge(s_res, 2 * n + 2)
                    dve.wait_ge(s_y, n + 1)
                    nc.vector.scalar_tensor_tensor(k.X[:, t, :], k.ps[:, 4 + j, 0:D], 1.0 / WS, res[:, 1, :],
                                                   ALU.mult, ALU.add).then_inc(s_x, 1)
                    dve.wait_ge(s_x, n + 1)
                    tile_stats(nc, k, n).then_inc(s_st, 1)

            for i, piece in enumerate(OTHERS):
                dve.wait_ge(s_whigh, i + 1)
                split_low(nc, k, stage, piece).then_inc(s_wlow, 1)
            scans(0)
            with dve.Fori(1, NB) as i:
                scans(i)
                residual(i - 1)
            residual(NB - 1)




def ssm_layer(nc, k, a):
    with ExitStack() as ctx:
        stage = ctx.enter_context(nc.sbuf_tensor("stage", [P, NSW], F32))
        others_in = [ctx.enter_context(nc.semaphore(f"others_in{i}")) for i in range(len(OTHERS))]
        prepare(nc, k, a, stage, others_in)
        normalise(nc, k, "n0", second=True, w=V_LNW, b=V_LNB, aggregated=True)
        ssm(nc, k, stage, others_in)


def three_pass(nc, out, stationary, moving, first=True, last=True):
    for n, (ps, pm) in enumerate(PASSES):
        mm = nc.tensor.matmul(out, stationary(ps), moving(pm), start=first and n == 0,
                              stop=last and n == len(PASSES) - 1)
    return mm


class PatchSum:

    def __init__(self, nc, k, a, ctx):
        sb = lambda n, s, d=F32: ctx.enter_context(nc.sbuf_tensor("sum_" + n, s, d))
        sem = lambda n: ctx.enter_context(nc.semaphore("sum_" + n))
        self.nc, self.k, self.a = nc, k, a
        self.ones = k.ones[:, 0:1].to_broadcast([P, S])
        self.hit = sb("hit", [P, 2, 2, S], BF16)
        self.mark, self.plug, self.dist = sb("mark", [P, S]), sb("plug", [P, S]), sb("dist", [P, 2, S])
        self.M = sb("M", [P, 2, 2, S])
        self.cx, self.junk = sb("cx", [P, 2, 2, CD]), sb("junk", [P, CD], BF16)
        self.ss, self.u, self.total = sb("ss", [P, 2, 2]), sb("u", [P, 2, 2, D]), sb("total", [P, 2, 2, D])
        self.s_cx = [sem("cx0"), sem("cx1")]
        self.s_hit, self.s_count, self.s_mark, self.s_step = (sem(n) for n in ("hit", "count", "mark", "step"))
        self.s_dist, self.s_M, self.s_square, self.s_power, self.s_u = (sem(n) for n in ("dist", "M", "square", "power", "u"))
        self.s_product, self.s_total = sem("product"), sem("total")
        self.s_out = [sem("out0"), sem("out1")]

    def load(self, sp, b, s):
        wait(sp, self.s_u, 2 * (b - 1))
        rows = self.a["ctx"].rearrange("(n p) d -> p n d", p=P)
        sp.dma_start(self.cx[:, s], rows[:, 2 * b:2 * b + 2, :]).then_inc(self.s_cx[s], 16)

    def store(self, sp, b, s):
        sp.wait_ge(self.s_total, b + 1)
        sp.dma_start(self.k.patch_sum[:, 2 * b:2 * b + 2, :], self.total[:, s]).then_inc(self.s_out[s], 16)

    def hits(self, dve, b, s):
        wait(dve, self.s_count, b - 1)
        for c in range(KD):
            self.nc.vector.tensor_scalar(self.hit[:, s, c, :], self.k.iota[:], self.k.endT[:, c, b:b + 1], None,
                                         ALU.is_equal).then_inc(self.s_hit, 1)

    def count(self, pe, b, s):
        pe.wait_ge(self.s_hit, KD * b + KD)
        wait(pe, self.s_mark, b)
        for c in range(KD):
            mm = self.nc.tensor.matmul(self.k.ps[:, 6, 0:S], self.k.ones16[:], self.hit[:, s, c, :], start=c == 0, stop=c == KD - 1)
        mm.then_inc(self.s_count, 1)

    def distances(self, dve, b):
        v, n = self.nc.vector, 4 * b
        dve.wait_ge(self.s_count, b + 1)
        v.tensor_scalar(self.mark[:], self.k.ps[:, 6, 0:S], 1.0, None, ALU.min).then_inc(self.s_mark, 1)
        dve.wait_ge(self.s_mark, b + 1)
        v.tensor_tensor_scan(self.plug[:], self.ones, self.mark[:], -1.0, ALU.mult, ALU.add).then_inc(self.s_step, 1)
        dve.wait_ge(self.s_step, n + 1)
        v.tensor_scalar(self.mark[:], self.plug[:], 0.0, float(S - 1), ALU.max, ALU.min).then_inc(self.s_step, 1)
        dve.wait_ge(self.s_step, n + 2)
        wait(dve, self.s_M, b)
        for c in range(KD):
            v.tensor_scalar(self.plug[:], self.mark[:], self.k.qcol[:, c:c + 1], None, ALU.subtract).then_inc(self.s_step, 1)
            dve.wait_ge(self.s_step, n + 3 + c)
            v.scalar_tensor_tensor(self.dist[:, c, :], self.plug[:], -1000.0, self.plug[:], ALU.mult, ALU.max).then_inc(self.s_dist, 1)
            dve.wait_ge(self.s_dist, KD * b + c + 1)

    def decay(self, act, b, s):
        act.wait_ge(self.s_dist, KD * b + KD)
        wait(act, self.s_product, b - 1)
        self.nc.scalar.activation(self.M[:, s], self.dist[:], ACT.Exp, scale=-DT).then_inc(self.s_M, 1)

    def squares(self, act, b, s):
        act.wait_ge(self.s_cx[s], 8 * b + 16 - 8 * s)
        wait(act, self.s_u, 2 * (b - 1))
        for t in range(2):
            wait(act, self.s_square, 2 * b + t)
            self.nc.scalar.activation(self.junk[:], self.cx[:, s, t, :], ACT.Square,
                                      accum_out=self.ss[:, s, t:t + 1]).then_inc(self.s_square, 1)

    def power(self, pool, b, s):
        v, ss = self.nc.gpsimd, self.ss[:, s]
        pool.wait_ge(self.s_square, 2 * b + 2)
        v.tensor_scalar(ss, ss, 1.0 / CD, EPS, ALU.mult, ALU.add).then_inc(self.s_power, 1)
        pool.wait_ge(self.s_power, 3 * b + 1)
        v.tensor_tensor(ss, ss, self.k.half[:, 0:2], ALU.pow).then_inc(self.s_power, 1)
        pool.wait_ge(self.s_power, 3 * b + 2)
        v.tensor_scalar(ss, ss, float(np.exp(LOGP)), None, ALU.mult).then_inc(self.s_power, 1)

    def rows(self, dve, b, s):
        dve.wait_ge(self.s_power, 3 * b + 3)
        wait(dve, self.s_product, b - 1)
        for t in range(2):
            self.nc.vector.scalar_tensor_tensor(self.u[:, s, t, :], self.cx[:, s, t, 0:D], self.ss[:, s, t:t + 1],
                                                self.k.rows[:, R_GI, :], ALU.mult, ALU.mult).then_inc(self.s_u, 1)

    def product(self, pe, b, s):
        pe.wait_ge(self.s_M, b + 1)
        pe.wait_ge(self.s_u, 2 * b + 2)
        wait(pe, self.s_total, b)
        for tc in range(2):
            for c in range(KD):
                mm = self.nc.tensor.matmul(self.k.ps[:, 7, tc * D:(tc + 1) * D], self.M[:, s, c, tc * P:(tc + 1) * P],
                                           self.u[:, s, c, :], start=c == 0, stop=c == KD - 1)
        mm.then_inc(self.s_product, 1)

    def total_of(self, dve, b, s):
        dve.wait_ge(self.s_product, b + 1)
        wait(dve, self.s_out[s], 8 * b - 8 * s)
        self.nc.vector.tensor_tensor(self.total[:, s], self.k.ps[:, 7, :].rearrange("p (c d) -> p c d", c=2),
                                     self.k.rows[:, R_BIN:R_BIN + 1, :].to_broadcast([P, 2, D]), ALU.add).then_inc(self.s_total, 1)


def cross_project(nc, k, a, A):
    with ExitStack() as ctx:
        sb = lambda n, s, d=F32: ctx.enter_context(nc.sbuf_tensor("xp_" + n, s, d))
        sem = lambda n: ctx.enter_context(nc.semaphore("xp_" + n))
        ctx_in = sb("ctx_in", [P, 2, KC, BLK])
        ctx_h, ctx_l = sb("ctx_h", [P, 2, KC, BLK], F16), sb("ctx_l", [P, 2, KC, BLK], F16)
        mask_row = sb("mask_row", [P, 2, BLK])
        biased = sb("biased", [P, 2, BLK])
        masked = sb("masked", [P, 2, BLK])
        qk_h, qk_l = sb("qk_h", [P, 4, BLK], F16), sb("qk_l", [P, 4, BLK], F16)
        vtmp = sb("vtmp", [P, 2, D])
        negh = sb("negh", [B, S], F16)
        s_ctx = [sem("ctx0"), sem("ctx1")]
        s_mask, s_ch, s_cl, s_qk, s_biased, s_masked = sem("mask"), sem("ch"), sem("cl"), sem("qk"), sem("biased"), sem("masked")
        s_high, s_low, s_v, s_vt, s_vm, s_o, s_x = (sem(n) for n in ("high", "low", "v", "vt", "vm", "o", "x"))
        s_out = [sem(f"out{m}") for m in range(4)]
        s_neg, s_negout, s_xb, s_fill = sem("neg"), sem("negout"), sem("xb"), sem("fill")
        s_row = [sem("row0"), sem("row1")]
        patches = PatchSum(nc, k, a, ctx)
        negm = patches.dist[0:B, 0, :]
        block = ctx.enter_context(nc.Block())
        UNITS = (("tgt", 0, V_BTGT), ("tgt", 1, V_BTGT + 1), ("src", 0, V_BSRC), ("src", 1, V_BSRC + 1))

        @block.sync
        def _(sp):
            sp.dma_start(negm, a["mask"]).then_inc(s_mask, 16)
            sp.dma_start(k.mask_col[:], a["maskT"]).then_inc(s_mask, 16)
            mask = a["mask"].rearrange("(o b) s -> o (b s)", o=1)
            def context(i):
                wait(sp, s_cl, i - 1)
                sp.dma_start(ctx_in[:, i % 2], a["ctxT"][:, :, i * BLK:(i + 1) * BLK]).then_inc(s_ctx[i % 2], 16)

            def mask_for(i):
                wait(sp, s_masked, 4 * (i - 1))
                sp.dma_start(mask_row[:, i % 2, :], mask[:, i * BLK:(i + 1) * BLK].to_broadcast([P, BLK])).then_inc(s_row[i % 2], 16)

            for i in range(2):
                context(i)
                mask_for(i)
                patches.load(sp, i, i)
            sp.wait_ge(s_neg, 2)
            sp.dma_start(k.negmask, negh[:]).then_inc(s_negout, 16)
            for i in range(NB):
                for m in range(4):
                    sp.wait_ge(s_low, 4 * i + m + 1)
                    for p, part in enumerate((qk_h, qk_l)):
                        sp.dma_start(A.rows_of(k.xqk, m, p)[:, :, i * BLK:(i + 1) * BLK], part[:, m, :]).then_inc(s_out[m], 16)
                if i + 1 < NB:
                    patches.load(sp, 2 * i + 2, 0)
                if i + 2 < NB:
                    mask_for(i + 2)
                    context(i + 2)
                if i + 1 < NB:
                    patches.load(sp, 2 * i + 3, 1)
                for s in range(2 if i else 0):
                    patches.store(sp, 2 * i - 2 + s, s)
            for s in range(2):
                patches.store(sp, B - 2 + s, s)
            sp.wait_ge(s_negout, 16)
            for s in range(2):
                sp.wait_ge(patches.s_out[s], 8 * B)
            for m in range(4):
                sp.wait_ge(s_out[m], 32 * NB)

        @block.tensor
        def _(pe):
            def two_blocks(ii):
                for s in range(2):
                    i = 2 * ii + s
                    for m, (name, c, _) in enumerate(UNITS):
                        if m == 2:
                            pe.wait_ge(s_cl, i + 1)
                        if m < 2:
                            patches.count(pe, 2 * i + m, m)
                        wait(pe, s_biased, 4 * i + m - 1)
                        for kc in range(KD if name == "tgt" else KC):
                            src = (lambda p: k.nT[p][:, kc, ds(i * BLK, BLK)]) if name == "tgt" else \
                                  (lambda p: (ctx_h, ctx_l)[p][:, s, kc, :])
                            mm = three_pass(nc, k.ps[:, m % 2, :], lambda p: weight(k, name, kc, p)[:, c * P:(c + 1) * P],
                                            src, kc == 0, kc == (KD if name == "tgt" else KC) - 1)
                        mm.then_inc(s_qk, 1)
                    for j in range(TB):
                        wait(pe, s_vt, TB * i + j - 1)
                        for kc in range(KC):
                            mm = three_pass(nc, k.ps[:, 2 + j % 2, 0:D], lambda p: (ctx_h, ctx_l)[p][:, s, kc, j * P:(j + 1) * P],
                                            lambda p: weight(k, "src", kc, p)[:, D:2 * D], kc == 0, kc == KC - 1)
                        mm.then_inc(s_v, 1)
                        wait(pe, s_x, TB * i + j - 1)
                        for kc in range(KD):
                            mm = three_pass(nc, k.ps[:, 4 + j % 2, 0:D], lambda p: k.nT[p][:, kc, ds(i * BLK + j * P, P)],
                                            lambda p: weight(k, "o", kc, p), kc == 0, kc == KD - 1)
                        mm.then_inc(s_o, 1)
                        if j % 2 == 0 and (s or not isinstance(i, int) or i):
                            patches.product(pe, 2 * i - 2 + j // 2, j // 2)

            peeled(pe, NB // 2, two_blocks)
            for s in range(2):
                patches.product(pe, B - 2 + s, s)

        @block.scalar
        def _(act):
            def context(i):
                act.wait_ge(s_ctx[i % 2], 16 * (i // 2 + 1))
                wait(act, s_v, TB * (i - 1))
                nc.scalar.activation(ctx_h[:, i % 2], ctx_in[:, i % 2], ACT.Copy).then_inc(s_ch, 1)

            context(0)
            for i in range(NB):
                for m, (_, _, v) in enumerate(UNITS):
                    n = 4 * i + m
                    act.wait_ge(s_qk, n + 1)
                    if n >= 2:
                        act.wait_ge(s_masked, n - 1)
                    nc.scalar.activation(biased[:, n % 2, :], k.ps[:, m % 2, :], ACT.Identity, scale=1.0 / WS,
                                         bias=k.vec[:, v:v + 1]).then_inc(s_biased, 1)
                    act.wait_ge(s_masked, n + 1)
                    if n >= 4:
                        act.wait_ge(s_out[m], 32 * i)
                    nc.scalar.activation(qk_h[:, m, :], masked[:, n % 2, :], ACT.Copy).then_inc(s_high, 1)
                    if m < 2:
                        patches.squares(act, 2 * i + m, m)
                    elif m == 2:
                        patches.decay(act, 2 * i, 0)
                patches.decay(act, 2 * i + 1, 1)
                if i + 1 < NB:
                    context(i + 1)

        @block.vector
        def _(dve):
            for s in range(2):
                patches.hits(dve, s, s)
            dve.wait_ge(s_mask, 32)
            nc.vector.tensor_scalar(negm, negm, 0.0, NEG, ALU.is_equal, ALU.mult).then_inc(s_neg, 1)
            dve.wait_ge(s_neg, 1)
            nc.vector.tensor_copy(negh[:], negm).then_inc(s_neg, 1)
            for i in range(NB):
                dve.wait_ge(s_row[i % 2], 16 * (i // 2 + 1))
                for m in range(4):
                    n = 4 * i + m
                    if m % 2 == 1:
                        patches.distances(dve, 2 * i + m // 2)
                    dve.wait_ge(s_biased, n + 1)
                    if n >= 2:
                        dve.wait_ge(s_low, n - 1)
                    nc.vector.tensor_tensor(masked[:, n % 2, :], biased[:, n % 2, :], mask_row[:, i % 2, :],
                                            ALU.mult).then_inc(s_masked, 1)
                patches.rows(dve, 2 * i, 0)
                for j in range(TB):
                    n = TB * i + j
                    if j % 2 == 1 and i:
                        patches.total_of(dve, 2 * i - 2 + j // 2, j // 2)
                    if j == TB - 1:
                        patches.rows(dve, 2 * i + 1, 1)
                    dve.wait_ge(s_v, n + 1)
                    wait(dve, s_vm, n - 1)
                    nc.vector.scalar_tensor_tensor(vtmp[:, n % 2, :], k.ps[:, 2 + j % 2, 0:D], 1.0 / WS, k.rows[:, R_BV, :],
                                                   ALU.mult, ALU.add).then_inc(s_vt, 1)
                    dve.wait_ge(s_vt, n + 1)
                    nc.vector.tensor_scalar(k.V[:, n, :], vtmp[:, n % 2, :], k.mask_col[:, n:n + 1], None, ALU.mult).then_inc(s_vm, 1)
                    dve.wait_ge(s_xb, n + 1)
                    dve.wait_ge(s_o, n + 1)
                    nc.vector.scalar_tensor_tensor(k.X[:, n, :], k.ps[:, 4 + j % 2, 0:D], 1.0 / WS, k.X[:, n, :],
                                                   ALU.mult, ALU.add).then_inc(s_x, 1)
                if i + 1 < NB:
                    for s in range(2):
                        patches.hits(dve, 2 * i + 2 + s, s)
            for s in range(2):
                patches.total_of(dve, B - 2 + s, s)

        @block.gpsimd
        def _(pool):
            def context(i):
                pool.wait_ge(s_ch, i + 1)
                nc.gpsimd.tensor_tensor(ctx_l[:, i % 2], ctx_in[:, i % 2], ctx_h[:, i % 2], ALU.subtract).then_inc(s_cl, 1)

            context(0)
            for i in range(NB):
                for j in range(TB):
                    n = TB * i + j
                    nc.gpsimd.tensor_tensor(k.X[:, n, :], k.X[:, n, :], k.rows[:, R_BO, :], ALU.add).then_inc(s_xb, 1)
                for m in range(4):
                    n = 4 * i + m
                    pool.wait_ge(s_high, n + 1)
                    nc.gpsimd.tensor_tensor(qk_l[:, m, :], masked[:, n % 2, :], qk_h[:, m, :], ALU.subtract).then_inc(s_low, 1)
                    if 1 <= m <= 2:
                        patches.power(pool, 2 * i + m - 1, m - 1)
                if i + 1 < NB:
                    context(i + 1)
                if i == 0:
                    pool.wait_ge(s_cl, 2)
                    A.fill(nc, pool, s_fill)


class Heads:

    def __init__(self, nc, k, ctx, tag, heads, dim, masked):
        sb = lambda n, s, d=F32: ctx.enter_context(nc.sbuf_tensor(tag + n, s, d))
        self.tag, self.heads, self.dim, self.masked = tag, heads, dim, masked
        self.top = 96 if masked else 64
        self.shift = self.top + 1
        self.groups = heads // 4
        self.units = 2 * self.groups
        self.wide = S if dim < 32 else 2 * S
        self.Q, self.K = sb("Q", [P, NSLOT * heads, S], F16), sb("K", [P, NSLOT * heads, S], F16)
        self.V = sb("Vb", [P, 2, 2, heads * 32])

    def rows_of(self, qk, m, part):
        n = P // self.dim
        return qk[m // 2, (m % 2) * n:(m % 2 + 1) * n, part * self.dim:(part + 1) * self.dim, :]

    def fill(self, nc, pool, filled):
        two_ones = float(np.array([1.0, 1.0], np.float16).view(np.float32)[0])
        rows = [(self.Q[96:P], two_ones), (self.K[96:P], two_ones)] if self.masked else \
               [(self.Q[:], 0.0), (self.K[0:64], 0.0), (self.K[64:P], two_ones)]
        fills = [(where.bitcast(F32), value) for where, value in rows]
        if not self.masked:
            fills.append((self.V[:], 1.0))
        for n, (where, value) in enumerate(fills):
            nc.gpsimd.memset(where, value).then_inc(filled, 1)
            pool.wait_ge(filled, n + 1)


NSLOT = 4


def has(b, before=0, after=0):
    return not isinstance(b, int) or (b >= before and b + after < B)


def over_batches(eng, step):
    step(0, 0)
    step(1, 1)
    with eng.Fori(1, B // 2 - 1) as i:
        step(2 * i, 0)
        step(2 * i + 1, 1)
    step(B - 2, 0)
    step(B - 1, 1)


def attention(nc, k, A, qk, wname, wk0, negmask):
    tag, heads, dim, top, shift = A.tag, A.heads, A.dim, A.top, A.shift
    Q, K, V, G, UN = A.Q, A.K, A.V, A.groups, A.units
    MU = 2 * UN
    HALF = UN // 2
    NC = G * S
    scale = float(dim) ** -0.5
    loads = 5 if negmask is not None else 4
    den_row = 0 if dim == 32 else dim
    with ExitStack() as ctx:
        sb = lambda n, s, d=F32: ctx.enter_context(nc.sbuf_tensor(tag + n, s, d))
        sem = lambda n: ctx.enter_context(nc.semaphore(tag + n))
        pT = sb("pT", [P, 2, 4 * S])
        nmx = sb("nmx", [P, 2, 2, heads])
        nmT = sb("nmT", [heads, 2, S], F16)
        sums = sb("sums", [P, 2, A.wide // S, NC])
        den, rec = sb("den", [P, heads * S // P]), sb("rec", [P, heads * S // P])
        rec_d = nc.dram_tensor(tag + "rec_d", (4, NC), F32, kind="Internal").ap()
        recb = sb("recb", [P, NC])
        last_rec = k.nT[0][:, 0, :].bitcast(F32)
        o = sb("o", [P, 2, NC])
        oh, ol = sb("oh", [P, 2, NC], F16), sb("ol", [P, 2, NC], F16)
        s_load, s_nmin = [sem("load0"), sem("load1")], [sem("nmin0"), sem("nmin1")]
        s_v, s_mx, s_red, s_turn, s_nmT = (sem(n) for n in ("v", "mx", "red", "turn", "nmT"))
        s_st, s_exp, s_pv, s_sum, s_rec, s_o, s_oh, s_ol, s_out, s_x = (sem(n) for n in ("st", "exp", "pv", "sum", "rec", "o", "oh", "ol", "out", "x"))
        s_den, s_recw, s_recr, s_last, s_stats = (sem(n) for n in ("den", "recw", "recr", "last", "stats"))
        block = ctx.enter_context(nc.Block())

        @block.sync
        def _(sp):
            def load(b, s):
                sl = (b % NSLOT) * heads
                cols = b * S
                if not isinstance(b, int):
                    sl, cols = sp.snap(sl), sp.snap(cols)
                wait(sp, s_pv, UN * (b - NSLOT + 1))
                for dst, row, src, lo, hi in ((Q, 0, 0, 0, 2), (Q, 2 * dim, 0, 0, 1), (K, 0, 1, 0, 1), (K, dim, 1, 0, 2)):
                    sp.dma_start(dst[row:row + (hi - lo) * dim, ds(sl, heads), :],
                                 qk[src, :, lo * dim:hi * dim, ds(cols, S)].rearrange("h r t -> r h t")).then_inc(s_load[s], 16)
                if negmask is not None:
                    sp.dma_start(K[top:top + 1, ds(sl, heads), :],
                                 negmask[ds(b, 1), :].rearrange("o (h s) -> o h s", h=1).to_broadcast([1, heads, S])).then_inc(s_load[s], 16)

            def maxima(b, s):
                sl = (b % NSLOT) * heads
                if not isinstance(b, int):
                    sl = sp.snap(sl)
                sp.wait_ge(s_nmT, b + 1)
                sp.dma_start(Q[shift:shift + 1, ds(sl, heads), :], nmT[:, s, :]).then_inc(s_nmin[s], 16)

            def gather(b, s):
                sp.wait_ge(s_sum, G * b + G)
                sp.dma_start(den[:], sums[den_row:P:32, s, A.wide // S - 1, :].rearrange("j (a e) -> j a e", a=32)).then_inc(s_den, 16)

            def scatter(b):
                sp.wait_ge(s_rec, b + 1)
                wait(sp, s_o, b)
                sp.dma_start(rec_d.rearrange("j (a e) -> (j a) e", a=32), rec[:]).then_inc(s_recw, 16)
                sp.wait_ge(s_recw, 16 * b + 16)
                sp.dma_start(recb[:], rec_d.rearrange("j (o c) -> j o c", o=1).to_broadcast([4, 32, NC])).then_inc(s_recr, 16)

            def step(b, s):
                if has(b, after=2):
                    load(b + 2, s)
                if has(b, before=1):
                    gather(b - 1, 1 - s)
                if has(b, after=1):
                    maxima(b + 1, 1 - s)
                if has(b, before=1):
                    scatter(b - 1)
                    if not has(b, after=1):
                        sp.wait_ge(s_recr, 16 * b)

            load(0, 0)
            load(1, 1)
            maxima(0, 0)
            over_batches(sp, step)

        @block.gpsimd
        def _(pool):
            def values(b, s):
                wait(pool, s_pv, UN * (b - 1))
                nc.gpsimd.tensor_copy(V[:, s].rearrange("p c (h d) -> p c h d", d=32)[:, :, :, 0:dim],
                                      k.V[:, ds(2 * b, 2), :].rearrange("p c (h d) -> p c h d", d=dim)).then_inc(s_v, 1)

            def low(b, s):
                pool.wait_ge(s_oh, b + 1)
                nc.gpsimd.tensor_tensor(ol[:, s], o[:, s], oh[:, s], ALU.subtract).then_inc(s_ol, 1)

            def step(b, s):
                if has(b, after=1):
                    values(b + 1, 1 - s)
                if has(b, before=2):
                    low(b - 2, s)

            values(0, 0)
            over_batches(pool, step)
            low(B - 2, 0)
            low(B - 1, 1)

        @block.tensor
        def _(pe):
            slot_regs = [pe.alloc_register(f"{tag}slot{r}") for r in range(3)]

            def slot_of(b, r):
                sl = (b % NSLOT) * heads
                if isinstance(b, int):
                    return sl
                pe.reg_mov(slot_regs[r], sl)
                return pe.snap(slot_regs[r], min_val=0, max_val=(NSLOT - 1) * heads)

            def max_unit(b, sl, m):
                tc, hp = m // (heads // 2), m % (heads // 2)
                wait(pe, s_red, MU * b + m - 1)
                for e in range(2):
                    mm = nc.tensor.matmul(k.ps[:, m % 2, e * S:(e + 1) * S], Q[0:top + 1, ds(sl + (2 * hp + e), 1), tc * P:(tc + 1) * P],
                                          K[0:top + 1, ds(sl + (2 * hp + e), 1), :], start=True, stop=True)
                mm.then_inc(s_mx, 1)

            def turn(b, s):
                pe.wait_ge(s_red, MU * b + MU)
                wait(pe, s_x, b - 3)
                for tc in range(2):
                    mm = nc.tensor.transpose(k.ps[0:heads, 7, tc * P:(tc + 1) * P], nmx[:, s, tc, :], k.ident[:])
                mm.then_inc(s_turn, 1)

            def scores(b, sl, u):
                g, c = u // 2, u % 2
                wait(pe, s_exp, UN * b + u - 1)
                for j in range(4):
                    mm = nc.tensor.matmul(k.ps[:, 2 + 2 * (u % 2) + j // 2, (j % 2) * S:(j % 2 + 1) * S],
                                          K[0:shift + 1, ds(sl + (4 * g + j), 1), c * P:(c + 1) * P], Q[0:shift + 1, ds(sl + (4 * g + j), 1), :], start=True, stop=True)
                mm.then_inc(s_st, 1)

            def weigh(b, s, u):
                g, c = u // 2, u % 2
                pe.wait_ge(s_exp, UN * b + u + 1)
                if c == 0:
                    wait(pe, s_sum, G * b + g)
                for what in range(A.wide // S):
                    for j in range(4):
                        h = 4 * g + j
                        lhs = V[:, s, c, 32 * h:32 * h + 32] if what == 0 else k.ones[:, :]
                        mm = nc.tensor.matmul(k.ps[32 * j:32 * j + 32, 6, what * S:(what + 1) * S], lhs,
                                              pT[:, u % 2, j * S:(j + 1) * S], start=c == 0 and what == 0, stop=c == 1,
                                              skip_group_check=True)
                mm.then_inc(s_pv, 1)

            def output(b, s, part):
                if part == 0:
                    pe.wait_ge(s_ol, b + 1)
                    pe.wait_ge(s_nmT, min(b + 4, B) if isinstance(b, int) else b + 4)
                for piece in (2 * part, 2 * part + 1):
                    tc, g = piece // G, piece % G
                    mm = three_pass(nc, k.ps[:, 7, tc * D:(tc + 1) * D],
                                    lambda p: (oh, ol)[p][:, s, g * S + tc * P:g * S + (tc + 1) * P],
                                    lambda p: weight(k, wname, wk0 + g, p), g == 0, g == G - 1)
                if part == HALF - 1:
                    mm.then_inc(s_out, 1)

            def step(b, s):
                pe.wait_ge(s_nmin[s], 8 * b + 16 - 8 * s)
                pe.wait_ge(s_v, b + 1)
                sl, sl1, sl2 = slot_of(b, 0), slot_of(b + 1, 1), slot_of(b + 2, 2)
                scores(b, sl, 0)
                for u in range(UN):
                    if u + 1 < UN:
                        scores(b, sl, u + 1)
                    if u < HALF and has(b, after=1):
                        for e in range(2):
                            max_unit(b + 1, sl1, UN + 2 * u + e)
                    if u == HALF and has(b, after=1):
                        turn(b + 1, 1 - s)
                    if u == HALF and has(b, after=2):
                        pe.wait_ge(s_load[s], loads * (8 * b + 32 - 8 * s))
                    if u >= HALF and has(b, after=2):
                        for e in range(2):
                            max_unit(b + 2, sl2, 2 * (u - HALF) + e)
                    if u >= HALF and has(b, before=2):
                        output(b - 2, s, u - HALF)
                    weigh(b, s, u)

            pe.wait_ge(s_load[0], 16 * loads)
            for m in range(MU):
                max_unit(0, 0, m)
            turn(0, 0)
            pe.wait_ge(s_load[1], 16 * loads)
            for m in range(UN):
                max_unit(1, heads, m)
            over_batches(pe, step)
            for b in (B - 2, B - 1):
                if b == B - 1:
                    pe.wait_ge(s_x, B - 1)
                for part in range(HALF):
                    output(b, b % 2, part)

        @block.scalar
        def _(act):
            def turned(b, s):
                act.wait_ge(s_turn, b + 1)
                if has(b, before=2):
                    act.wait_ge(s_nmin[s], 8 * b - 8 * s)
                nc.scalar.activation(nmT[:, s, :], k.ps[0:heads, 7, 0:S], ACT.Copy).then_inc(s_nmT, 1)

            def high(b, s):
                act.wait_ge(s_o, b + 1)
                if isinstance(b, int):
                    wait(act, s_out, b - 1)
                nc.scalar.activation(oh[:, s], o[:, s], ACT.Copy).then_inc(s_oh, 1)

            def step(b, s):
                for u in range(UN):
                    wait(act, s_pv, UN * b + u - 1)
                    act.wait_ge(s_st, UN * b + u + 1)
                    nc.scalar.activation(pT[:, u % 2, :].rearrange("p (b c) -> p b c", b=2),
                                         k.ps[:, 2 + 2 * (u % 2):4 + 2 * (u % 2), :], ACT.Exp, scale=scale).then_inc(s_exp, 1)
                    if u == HALF and has(b, after=1):
                        turned(b + 1, 1 - s)
                    if u == 1 and has(b, before=2):
                        high(b - 2, s)

            turned(0, 0)
            over_batches(act, step)
            high(B - 2, 0)
            high(B - 1, 1)

        @block.vector
        def _(dve):
            def reduce(b, s, m):
                tc, hp = m // (heads // 2), m % (heads // 2)
                dve.wait_ge(s_mx, MU * b + m + 1)
                if m == 0 and has(b, before=2):
                    dve.wait_ge(s_turn, b - 1)
                nc.vector.tensor_reduce(nmx[:, s, tc, 2 * hp:2 * hp + 2],
                                        k.ps[:, m % 2, :].rearrange("p (e s) -> p e s", e=2), AX, ALU.max,
                                        negate=True).then_inc(s_red, 1)

            def collect(b, s, g):
                if g == 0:
                    wait(dve, s_o, b - 1)
                dve.wait_ge(s_pv, UN * b + 2 * g + 2)
                nc.vector.tensor_copy(sums[:, s, :, g * S:(g + 1) * S], k.ps[:, 6, 0:A.wide].rearrange("p (w s) -> p w s", s=S)).then_inc(s_sum, 1)

            def invert(b):
                dve.wait_ge(s_den, 16 * b + 16)
                wait(dve, s_recw, 16 * b)
                nc.vector.reciprocal(rec[:], den[:]).then_inc(s_rec, 1)

            def invert_last(g):
                cols = slice(g * S, (g + 1) * S)
                out, src = last_rec[:, cols], sums[:, (B - 1) % 2, A.wide // S - 1, cols]
                dve.wait_ge(s_sum, G * (B - 1) + g + 1)
                if dim < 32:
                    nc.vector.stream_shuffle(out, src, [dim + r % dim for r in range(32)]).then_inc(s_last, 1)
                    dve.wait_ge(s_last, 2 * g + 1)
                    nc.vector.reciprocal(out, out).then_inc(s_last, 1)
                else:
                    nc.vector.reciprocal(out, src).then_inc(s_last, 2)

            def divide(b, s):
                if has(b, after=1):
                    dve.wait_ge(s_recr, 16 * b + 16)
                else:
                    dve.wait_ge(s_last, 2 * G)
                nc.vector.tensor_tensor(o[:, s], sums[:, s, 0, :], recb[:] if has(b, after=1) else last_rec[:, 0:NC],
                                        ALU.mult).then_inc(s_o, 1)

            def residual(b):
                dve.wait_ge(s_out, b + 1)
                nc.vector.scalar_tensor_tensor(k.X[:, ds(2 * b, 2), :], k.ps[:, 7, :].rearrange("p (c d) -> p c d", c=2),
                                               1.0 / WS, k.X[:, ds(2 * b, 2), :], ALU.mult, ALU.add).then_inc(s_x, 1)
                dve.wait_ge(s_x, b + 1)
                for t in range(2):
                    tile_stats(nc, k, 2 * b + t).then_inc(s_stats, 1)

            def step(b, s):
                for u in range(UN):
                    if u < HALF and has(b, after=1):
                        for e in range(2):
                            reduce(b + 1, 1 - s, UN + 2 * u + e)
                    if u >= HALF and has(b, after=2):
                        for e in range(2):
                            reduce(b + 2, s, 2 * (u - HALF) + e)
                    if u == UN - 1 and has(b, before=2):
                        residual(b - 2)
                    if u % 2 == 1:
                        collect(b, s, u // 2)
                    if u % 2 == 1 and not has(b, after=1):
                        invert_last(u // 2)
                    if u == 0 and has(b, before=2):
                        divide(b - 2, s)
                    if u == HALF and has(b, before=1):
                        invert(b - 1)

            for m in range(MU):
                reduce(0, 0, m)
            for m in range(UN):
                reduce(1, 1, m)
            over_batches(dve, step)
            divide(B - 2, 0)
            divide(B - 1, 1)
            residual(B - 2)
            residual(B - 1)
def self_project(nc, k, a, A):
    with ExitStack() as ctx:
        sem = lambda n: ctx.enter_context(nc.semaphore("mp_" + n))
        qk_h = ctx.enter_context(nc.sbuf_tensor("mp_qk_h", [P, 4, BLK], F16))
        qk_l = ctx.enter_context(nc.sbuf_tensor("mp_qk_l", [P, 4, BLK], F16))
        s_qk, s_high, s_low, s_v, s_vout = (sem(n) for n in ("qk", "high", "low", "v", "vout"))
        s_fill = sem("fill")
        weights = QuantWeights(nc, k, a, ctx)
        s_out = [sem(f"out{m}") for m in range(4)]
        block = ctx.enter_context(nc.Block())

        @block.tensor
        def _(pe):
            def one_block(i):
                for m, (name, c) in enumerate((("q", 0), ("q", 1), ("k", 0), ("k", 1))):
                    wait(pe, s_low, 4 * i)
                    for kc in range(KD):
                        mm = three_pass(nc, k.ps[:, m, :], lambda p: weight(k, name, kc, p)[:, c * P:(c + 1) * P],
                                        lambda p: k.nT[p][:, kc, ds(i * BLK, BLK)], kc == 0, kc == KD - 1)
                    mm.then_inc(s_qk, 1)
                for j in range(TB):
                    wait(pe, s_vout, TB * i)
                    for kc in range(KD):
                        mm = three_pass(nc, k.ps[:, 4 + j, 0:D], lambda p: k.nT[p][:, kc, ds(i * BLK + j * P, P)],
                                        lambda p: weight(k, "v", kc, p), kc == 0, kc == KD - 1)
                    mm.then_inc(s_v, 1)

            peeled(pe, NB, one_block)

        @block.scalar
        def _(act):
            def one_block(i):
                for m in range(4):
                    act.wait_ge(s_qk, 4 * i + m + 1)
                    wait(act, s_out[m], 32 * i)
                    nc.scalar.activation(qk_h[:, m, :], k.ps[:, m, :], ACT.Copy, scale=1.0 / WS).then_inc(s_high, 1)
                for j in range(TB):
                    act.wait_ge(s_v, TB * i + j + 1)
                    nc.scalar.activation(k.V[:, ds(i * TB + j, 1), :], k.ps[:, 4 + j, 0:D], ACT.Copy,
                                         scale=1.0 / WS).then_inc(s_vout, 1)

            peeled(act, NB, one_block)

        @block.vector
        def _(dve):
            for i in range(NB):
                for m in range(4):
                    dve.wait_ge(s_high, 4 * i + m + 1)
                    nc.vector.scalar_tensor_tensor(qk_l[:, m, :], k.ps[:, m, :], 1.0 / WS, qk_h[:, m, :],
                                                   ALU.mult, ALU.subtract).then_inc(s_low, 1)
                if i < 3:
                    weights.piece(dve, i)

        @block.gpsimd
        def _(pool):
            A.fill(nc, pool, s_fill)
            weights.store(pool)

        @block.sync
        def _(sp):
            weights.load(sp)
            with sp.Fori(0, NB) as i:
                for m in range(4):
                    sp.wait_ge(s_low, 4 * i + m + 1)
                    for p, part in enumerate((qk_h, qk_l)):
                        sp.dma_start(A.rows_of(k.mqk, m, p)[:, :, ds(i * BLK, BLK)], part[:, m, :]).then_inc(s_out[m], 16)
            for m in range(4):
                sp.wait_ge(s_out[m], 32 * NB)


class ExpertWeights:

    def __init__(self, nc, k, a, ctx):
        sb = lambda n, s, d=F32: ctx.enter_context(nc.sbuf_tensor("ew_" + n, s, d))
        sem = lambda n: ctx.enter_context(nc.semaphore("ew_" + n))
        self.nc, self.a = nc, a
        self.stage = sb("stage", [P, 2, NEW])
        self.high, self.low = sb("high", [P, 2 * NEW], F16), sb("low", [P, 2 * NEW], F16)
        self.s_in, self.s_high, self.s_low = [sem("in0"), sem("in1")], sem("high"), sem("low")

    def load(self, sp, e, s):
        sp.dma_start(self.stage[:, s, :], self.a["mw"][:, ds(e * NEW, NEW)]).then_inc(self.s_in[s], 16)

    def split_high(self, s):
        self.nc.scalar.activation(self.high[:, s * NEW:(s + 1) * NEW], self.stage[:, s, :], ACT.Copy, scale=WS).then_inc(self.s_high, 1)

    def split_low(self, dve, e, s):
        dve.wait_ge(self.s_high, e + 1)
        self.nc.vector.scalar_tensor_tensor(self.low[:, s * NEW:(s + 1) * NEW], self.stage[:, s, :], WS,
                                            self.high[:, s * NEW:(s + 1) * NEW], ALU.mult, ALU.subtract).then_inc(self.s_low, 1)


def route(nc, k, weights):
    with ExitStack() as ctx:
        sb = lambda n, s, d=F32: ctx.enter_context(nc.sbuf_tensor("rt_" + n, s, d))
        sem = lambda n: ctx.enter_context(nc.semaphore("rt_" + n))
        L, m1, d, ex = sb("L", [P, NT, E]), sb("m1", [P, NT]), sb("d", [P, NT, E]), sb("ex", [P, NT, E])
        gt, eq, rank = sb("gt", [P, NT, E, E]), sb("eq", [P, NT, E, E]), sb("rank", [P, NT, E])
        before = sb("before", [P, E, E])
        s_l, s_step, s_ex, s_before = sem("logits"), sem("step"), sem("ex"), sem("before")
        block = ctx.enter_context(nc.Block())

        @block.gpsimd
        def _(pool):
            nc.gpsimd.memset(before[:], 1.0).then_inc(s_before, 1)
            pool.wait_ge(s_before, 1)
            nc.gpsimd.affine_select(out=before[:], in_=before[:], compare_op=ALU.is_gt, fill=0.0, base=0,
                                    pattern=[[1, E], [-1, E]], channel_multiplier=0).then_inc(s_before, 1)

        @block.tensor
        def _(pe):
            for t in range(NT):
                for kc in range(KD):
                    mm = three_pass(nc, k.ps[:, 0, t * E:(t + 1) * E], lambda p: k.nT[p][:, kc, t * P:(t + 1) * P],
                                    lambda p: weight(k, "g", kc, p), kc == 0, kc == KD - 1)
            mm.then_inc(s_l, 1)

        @block.scalar
        def _(act):
            act.wait_ge(weights.s_in[0], 16)
            weights.split_high(0)
            act.wait_ge(s_step, 3)
            nc.scalar.activation(ex[:], d[:], ACT.Exp).then_inc(s_ex, 1)

        @block.vector
        def _(dve):
            step = [0]

            def then(ins):
                step[0] += 1
                ins.then_inc(s_step, 1)
                dve.wait_ge(s_step, step[0])

            def of(x, kind):
                v = x.rearrange("p t (e o) -> p t e o", o=1) if kind == "e" else x.rearrange("p t (o j) -> p t o j", o=1)
                return v.to_broadcast([P, NT, E, E])

            dve.wait_ge(s_l, 1)
            then(nc.vector.tensor_scalar(L[:], k.ps[:, 0, 0:NT * E].rearrange("p (t e) -> p t e", e=E), 1.0 / WS, None, ALU.mult))
            then(nc.vector.tensor_reduce(m1[:], L[:], AX, ALU.max))
            then(nc.vector.tensor_tensor(d[:], L[:], m1[:].rearrange("p (t o) -> p t o", o=1).to_broadcast([P, NT, E]), ALU.subtract))
            then(nc.vector.tensor_tensor(gt[:], of(L[:], "j"), of(L[:], "e"), ALU.is_gt))
            then(nc.vector.tensor_tensor(eq[:], of(L[:], "j"), of(L[:], "e"), ALU.is_equal))
            dve.wait_ge(s_before, 2)
            bb = before[:].rearrange("p (o e) j -> p o e j", o=1).to_broadcast([P, NT, E, E])
            then(nc.vector.tensor_tensor(eq[:], eq[:], bb, ALU.mult))
            then(nc.vector.tensor_tensor(gt[:], gt[:], eq[:], ALU.add))
            then(nc.vector.tensor_reduce(rank[:], gt[:], AX, ALU.add))
            then(nc.vector.tensor_scalar(rank[:], rank[:], 1.5, 1.0 / (WS * WS), ALU.is_lt, ALU.mult))
            dve.wait_ge(s_ex, 1)
            then(nc.vector.tensor_tensor(d[:], ex[:], rank[:], ALU.mult))
            then(nc.vector.tensor_reduce(m1[:], d[:], AX, ALU.add))
            then(nc.vector.tensor_scalar(m1[:], m1[:], WS * WS, None, ALU.mult))
            then(nc.vector.reciprocal(m1[:], m1[:]))
            then(nc.vector.tensor_tensor(k.wexp[:, :, 0:E], d[:], m1[:].rearrange("p (t o) -> p t o", o=1).to_broadcast([P, NT, E]), ALU.mult))
            then(nc.vector.memset(k.wexp[:, :, E:EA], 1.0 / (WS * WS)))
            weights.split_low(dve, 0, 0)


def expert_ffn(nc, k, weights):
    NS = NB * EA
    with ExitStack() as ctx:
        sb = lambda n, s, d=F32: ctx.enter_context(nc.sbuf_tensor("ex_" + n, s, d))
        sem = lambda n: ctx.enter_context(nc.semaphore("ex_" + n))
        wh, wl, s_win, s_wh, s_wl = weights.high, weights.low, weights.s_in, weights.s_high, weights.s_low
        gate, hid = sb("gate", [P, 2, BLK]), sb("hid", [P, 2, BLK])
        hh, hl = sb("hh", [P, 2, NHC, BLK], F16), sb("hl", [P, 2, NHC, BLK], F16)
        s_gu, s_gate, s_hid, s_high, s_low, s_y, s_x = (sem(n) for n in ("gu", "gate", "hid", "high", "low", "y", "x"))
        s_stats = sem("stats")
        block = ctx.enter_context(nc.Block())

        @block.sync
        def _(sp):
            with sp.Fori(1, EA // 2) as i:
                for s in range(2):
                    sp.wait_ge(s_wl, 2 * i + s - 1)
                    weights.load(sp, 2 * i + s, s)

        @block.tensor
        def _(pe):
            def gate_up(n, s):
                e, cols = n // NB, (n % NB) * BLK
                slot = (e % 2) * NEW
                if not isinstance(n, int):
                    e, cols, slot = pe.snap(e), pe.snap(cols), pe.snap(slot)
                pe.wait_ge(s_wl, e + 1)
                for c, (lo, w) in enumerate(HCH):
                    wait(pe, s_hid, NHC * n + c - 1)
                    for g in range(2):
                        for kc in range(KD):
                            mm = three_pass(nc, k.ps[0:w, 2 * ((s + c) % 2) + g, :],
                                            lambda p: (wh, wl)[p][:, ds(slot + ((g * KD + kc) * H + lo), w)],
                                            lambda p: k.nT[p][:, kc, ds(cols, BLK)], kc == 0, kc == KD - 1)
                    mm.then_inc(s_gu, 1)

            def down(n, s):
                slot = ((n // NB) % 2) * NEW
                if not isinstance(n, int):
                    slot = pe.snap(slot)
                pe.wait_ge(s_low, NHC * n + NHC)
                for j in range(TB):
                    wait(pe, s_x, TB * n - TB + j + 1)
                    for c, (_, w) in enumerate(HCH):
                        mm = three_pass(nc, k.ps[:, 4 + j, 0:D], lambda p: (hh, hl)[p][0:w, s, c, j * P:(j + 1) * P],
                                        lambda p: (wh, wl)[p][0:w, ds(slot + (2 * KD * H + c * D), D)], c == 0, c == NHC - 1)
                    mm.then_inc(s_y, 1)

            gate_up(0, 0)
            gate_up(1, 1)
            down(0, 0)
            with pe.Fori(0, NS // 2 - 1) as i:
                gate_up(2 * i + 2, 0)
                down(2 * i + 1, 1)
                gate_up(2 * i + 3, 1)
                down(2 * i + 2, 0)
            down(NS - 1, 1)

        @block.scalar
        def _(act):
            def split(e, s):
                if isinstance(e, int):
                    act.wait_ge(s_win[s], 16)
                else:
                    act.wait_ge(s_win[s], 8 * e + 16 - 8 * s)
                    act.wait_ge(s_y, TB * NB * e - TB * NB)
                weights.split_high(s)

            def one_step(n, s, first):
                for c, (_, w) in enumerate(HCH):
                    m, q = NHC * n + c, (s + c) % 2
                    act.wait_ge(s_gu, m + 1)
                    nc.scalar.activation(gate[0:w, q, :], k.ps[0:w, 2 * q, :], ACT.Silu, scale=1.0 / WS).then_inc(s_gate, 1)
                    act.wait_ge(s_hid, m + 1)
                    if not first:
                        act.wait_ge(s_y, TB * n - TB)
                    nc.scalar.activation(hh[0:w, s, c, :], hid[0:w, q, :], ACT.Copy).then_inc(s_high, 1)

            def expert(e, s, last=False):
                for b in range(NB):
                    one_step(NB * e + b, b % 2, isinstance(e, int) and e == 0 and b < 2)
                    if b == 1 and not last:
                        split(e + 1, 1 - s)

            expert(0, 0)
            with act.Fori(0, EA // 2 - 1) as i:
                expert(2 * i + 1, 1)
                expert(2 * i + 2, 0)
            expert(EA - 1, 1, last=True)

        @block.gpsimd
        def _(pool):
            with pool.Fori(0, NS // 2) as i:
                for s in range(2):
                    for c, (_, w) in enumerate(HCH):
                        pool.wait_ge(s_high, 2 * NHC * i + NHC * s + c + 1)
                        nc.gpsimd.tensor_tensor(hl[0:w, s, c, :], hid[0:w, (s + c) % 2, :], hh[0:w, s, c, :],
                                                ALU.subtract).then_inc(s_low, 1)

        @block.vector
        def _(dve):
            def hidden(n, s):
                for c, (_, w) in enumerate(HCH):
                    q = (s + c) % 2
                    wait(dve, s_low, NHC * n + c - 1)
                    dve.wait_ge(s_gate, NHC * n + c + 1)
                    nc.vector.tensor_tensor(hid[0:w, q, :], k.ps[0:w, 2 * q + 1, :], gate[0:w, q, :], ALU.mult).then_inc(s_hid, 1)

            def add(n, e, b, last):
                for j in range(TB):
                    t = b * TB + j
                    dve.wait_ge(s_y, TB * n + j + 1)
                    nc.vector.scalar_tensor_tensor(k.X[:, t, :], k.ps[:, 4 + j, 0:D], k.wexp[:, t, ds(e, 1)],
                                                   k.X[:, t, :], ALU.mult, ALU.add).then_inc(s_x, 1)
                    if last:
                        dve.wait_ge(s_x, TB * n + j + 1)
                        tile_stats(nc, k, t).then_inc(s_stats, 1)

            def expert(e, s, last=False):
                for b in range(NB):
                    n = NB * e + b
                    if not (last and b == NB - 1):
                        hidden(n + 1, (b + 1) % 2)
                    add(n, e, b, last)
                    if b == 1 and not last:
                        weights.split_low(dve, e + 1, 1 - s)

            hidden(0, 0)
            expert(0, 0)
            with dve.Fori(0, EA // 2 - 1) as i:
                expert(2 * i + 1, 1)
                expert(2 * i + 2, 0)
            expert(EA - 1, 1, last=True)


def cross_attention(nc, k, a):
    normalise(nc, k, "n1")
    with ExitStack() as ctx:
        A = Heads(nc, k, ctx, "xa", 8, 32, True)
        cross_project(nc, k, a, A)
        attention(nc, k, A, k.xqk, "o", KD, k.negmask)


def experts(nc, k, a):
    with ExitStack() as ctx:
        weights = ExpertWeights(nc, k, a, ctx)

        def load_first(sp):
            weights.load(sp, 0, 0)
            weights.load(sp, 1, 1)

        normalise(nc, k, "n2", loads=load_first)
        route(nc, k, weights)
        expert_ffn(nc, k, weights)


def self_attention(nc, k, a):
    normalise(nc, k, "n3")
    with ExitStack() as ctx:
        A = Heads(nc, k, ctx, "ma", 16, 16, False)
        self_project(nc, k, a, A)
        attention(nc, k, A, k.mqk, "mo", 0, None)
def depool(nc, k, a):
    with ExitStack() as ctx:
        sums = ctx.enter_context(nc.sbuf_tensor("dp_sums", [P, NT, D], F32))
        s_in = [ctx.enter_context(nc.semaphore(f"dp_in{i}")) for i in range(NB)]
        s_y, s_first, s_x, s_stats = (ctx.enter_context(nc.semaphore("dp_" + n)) for n in ("y", "first", "x", "stats"))

        def load_sums(sp):
            for i in range(NB):
                sp.dma_start(sums[:, i * TB:(i + 1) * TB, :], k.patch_sum[:, i * TB:(i + 1) * TB, :]).then_inc(s_in[i], 16)

        normalise(nc, k, "n4", second=True, w=V_GRES, loads=load_sums)
        block = ctx.enter_context(nc.Block())

        @block.tensor
        def _(pe):
            def one_block(i):
                for j in range(TB):
                    wait(pe, s_first, TB * i - TB + j + 1)
                    for kc in range(KD):
                        mm = three_pass(nc, k.ps[:, j, 0:D], lambda p: k.nT[p][:, kc, ds(i * BLK + j * P, P)],
                                        lambda p: weight(k, "in", kc, p), kc == 0, kc == KD - 1)
                    mm.then_inc(s_y, 1)

            peeled(pe, NB, one_block)

        @block.vector
        def _(dve):
            for t in range(NT):
                dve.wait_ge(s_y, t + 1)
                nc.vector.scalar_tensor_tensor(k.X[:, t, :], k.ps[:, t % TB, 0:D], 1.0 / WS, k.X[:, t, :],
                                               ALU.mult, ALU.add).then_inc(s_first, 1)
                if t % TB == 0:
                    dve.wait_ge(s_in[t // TB], 16)
                dve.wait_ge(s_first, t + 1)
                nc.vector.tensor_tensor(k.X[:, t, :], k.X[:, t, :], sums[:, t, :], ALU.add).then_inc(s_x, 1)
                dve.wait_ge(s_x, t + 1)
                tile_stats(nc, k, t).then_inc(s_stats, 1)


NQ = len(QCH)
GU, NW = 2 * NQ * D, 2 * NQ * D + KD * HS
ROW_PARTS = [(c * D, D, c) for c in range(2 * NQ)] + [(GU + c * HS, HS, 2 * NQ + c) for c in range(KD)]


class QuantWeights:

    def __init__(self, nc, k, a, ctx):
        sb = lambda n, s, d=F32: ctx.enter_context(nc.sbuf_tensor("qw_" + n, s, d))
        self.nc, self.k, self.a = nc, k, a
        self.W, self.whole, self.inverse = sb("W", [P, NW]), sb("whole", [P, NW], BF16), sb("inverse", [P, 14])
        self.s_in, self.s_step, self.s_done, self.s_out = (ctx.enter_context(nc.semaphore("qw_" + n)) for n in ("in", "step", "done", "out"))

    def load(self, sp):
        flat = lambda n: self.a[n].rearrange("p c d -> p (c d)")
        sp.dma_start(self.W[:, 0:NQ * D], flat("wgate")).then_inc(self.s_in, 16)
        sp.dma_start(self.W[:, NQ * D:GU], flat("wup")).then_inc(self.s_in, 16)
        sp.dma_start(self.W[:, GU:NW], flat("wdown")).then_inc(self.s_in, 16)

    def store(self, pool):
        pool.wait_ge(self.s_done, 1)
        pool.dma_start(self.k.wq, self.whole[:]).then_inc(self.s_out, 16)
        pool.wait_ge(self.s_out, 16)

    def piece(self, dve, i):
        v, k, W = self.nc.vector, self.k, self.W

        def then(ins, n):
            ins.then_inc(self.s_step, 1)
            dve.wait_ge(self.s_step, n)

        if i == 0:
            dve.wait_ge(self.s_in, 48)
            v.tensor_reduce(k.wsc[:, 0:2 * NQ], W[:, 0:GU].rearrange("p (c d) -> p c d", d=D), AX, ALU.max,
                            apply_absolute_value=True).then_inc(self.s_step, 1)
            then(v.tensor_reduce(k.wsc[:, 2 * NQ:], W[:, GU:].rearrange("p (c d) -> p c d", d=HS), AX, ALU.max,
                                 apply_absolute_value=True), 2)
            then(v.tensor_scalar(k.wsc[:], k.wsc[:], 1e-30, 1.0 / QMAX, ALU.max, ALU.mult), 3)
            then(v.reciprocal(self.inverse[:], k.wsc[:]), 4)
        elif i == 1:
            for lo, n, s in ROW_PARTS:
                v.tensor_scalar(W[:, lo:lo + n], W[:, lo:lo + n], self.inverse[:, s:s + 1], MAGIC, ALU.mult, ALU.add).then_inc(self.s_step, 1)
        else:
            n = 4 + len(ROW_PARTS)
            dve.wait_ge(self.s_step, n)
            then(v.tensor_scalar(W[:], W[:], MAGIC - QMAX - 1.0, MAGIC + QMAX, ALU.max, ALU.min), n + 1)
            v.tensor_scalar(self.whole[:], W[:], MAGIC, None, ALU.subtract).then_inc(self.s_done, 1)


def quant_ffn(nc, k, a, out):
    RMAX = bass.bass_isa.ReduceOp.max
    with ExitStack() as outer:
        keep = lambda n, s, d=F32: outer.enter_context(nc.sbuf_tensor("q_" + n, s, d))
        xqT = keep("xqT", [P, KD, T], BF16)
        wguT = keep("wguT", [P, 2, KD, HS], BF16)
        wdT = keep("wdT", [P, NQ, D], BF16)
        wsc = k.wsc
        drow = keep("drow", [P, D])
        clip = keep("clip", [P, 2])
        gmax, sx, sinv = keep("gmax", [P, 2]), keep("sx", [P, 2]), keep("sinv", [P, 2])
        hF = keep("hF", [P, NQ, T])
        hmax = keep("hmax", [P, NQ * NB])
        with ExitStack() as ctx:
            sb = lambda n, s, d=F32: ctx.enter_context(nc.sbuf_tensor("q1_" + n, s, d))
            sem = lambda n: ctx.enter_context(nc.semaphore("q1_" + n))
            W, pmax = sb("W", [P, NW], BF16), sb("pmax", [P, 1])
            dve_stats, pool_stats = layer_stats(nc, k, "n5", ctx, False)
            s_w, s_clip, s_step, s_row, s_pmax, s_gmax, s_sig = (sem(n) for n in ("w", "clip", "step", "row", "pmax", "gmax", "sig"))
            s_xq, s_tw, s_evac, s_rowin = (sem(n) for n in ("xq", "tw", "evac", "rowin"))
            s_xevac, s_tx = sem("xevac"), sem("tx")
            TURNS = [(m * NQ * D + c * D + kc * P, w, P, wguT[:, m, kc, lo:lo + w])
                     for m in range(2) for c, (lo, w) in enumerate(QCH) for kc in range(KD)]
            TURNS += [(2 * NQ * D + r * HS + lo, P, w, wdT[0:w, c, r * P:(r + 1) * P])
                      for r in range(KD) for c, (lo, w) in enumerate(QCH)]
            xn = sb("xn", [P, NT, D])
            block = ctx.enter_context(nc.Block())

            @block.sync
            def _(sp):
                sp.dma_start(W[:], k.wq).then_inc(s_w, 16)
                sp.dma_start(clip[:], a["clip"].to_broadcast([P, 2])).then_inc(s_clip, 16)
                for c in range(KD):
                    sp.dma_start(k.wsc_row[0:1, c * P:(c + 1) * P].rearrange("o p -> p o"), wsc[:, 12 + c:13 + c]).then_inc(s_row, 16)
                sp.wait_ge(s_row, 16 * KD)
                sp.dma_start(drow[:], k.wsc_row[0:1, :].to_broadcast([P, D])).then_inc(s_rowin, 16)
                sp.wait_ge(s_rowin, 16)

            @block.gpsimd
            def _(pool):
                pool_stats(pool)
                pool.wait_ge(s_pmax, 1)
                nc.gpsimd.partition_all_reduce(gmax[:, 0:1], pmax[:], P, RMAX).then_inc(s_gmax, 1)

            @block.scalar
            def _(act):
                act.wait_ge(s_clip, 16)
                nc.scalar.activation(clip[:], clip[:], ACT.Sigmoid).then_inc(s_sig, 1)
                for n, (_, w_in, w_out, dst) in enumerate(TURNS):
                    act.wait_ge(s_tw, n + 1)
                    nc.scalar.activation(dst, k.ps[0:w_out if n >= 4 * NQ else P, n % 4, 0:P if n >= 4 * NQ else w_in],
                                         ACT.Copy).then_inc(s_evac, 1)
                for q in range(KD * NB):
                    act.wait_ge(s_tx, q + 1)
                    i, c = q // KD, q % KD
                    nc.scalar.activation(xqT[:, c, i * BLK:(i + 1) * BLK], k.ps[:, 4 + q % 4, :], ACT.Copy).then_inc(s_xevac, 1)

            @block.tensor
            def _(pe):
                pe.wait_ge(s_w, 16)
                for n, (src, w_in, w_out, _) in enumerate(TURNS):
                    if n >= 4:
                        pe.wait_ge(s_evac, n - 3)
                    nc.tensor.matmul(k.ps[0:w_out, n % 4, 0:w_in], W[0:w_in, src:src + w_out], k.identb[0:w_in, 0:w_in],
                                     start=True, stop=True).then_inc(s_tw, 1)
                for i in range(NB):
                    pe.wait_ge(s_xq, i + 1)
                    for c in range(KD):
                        q = 2 * i + c
                        if q >= 4:
                            pe.wait_ge(s_xevac, q - 3)
                        for j in range(TB):
                            mm = nc.tensor.transpose(k.ps[:, 4 + q % 4, j * P:(j + 1) * P], xn[:, i * TB + j, c * P:(c + 1) * P], k.ident[:])
                        mm.then_inc(s_tx, 1)

            @block.vector
            def _(dve):
                step = [0]

                def then(ins):
                    step[0] += 1
                    ins.then_inc(s_step, 1)
                    dve.wait_ge(s_step, step[0])

                dve_stats(dve)
                dve.wait_ge(k.s_fac, NB)
                for t in range(NT):
                    nc.vector.tensor_scalar(xn[:, t, :], k.X[:, t, :], k.mv[:, t, 0:1], k.fac[:, t:t + 1],
                                            ALU.subtract, ALU.mult).then_inc(s_step, 1)
                    step[0] += 1
                dve.wait_ge(s_step, step[0])
                nc.vector.tensor_reduce(pmax[:], xn[:].rearrange("p t d -> p (t d)"), AX, ALU.max, apply_absolute_value=True).then_inc(s_pmax, 1)
                dve.wait_ge(s_gmax, 1)
                dve.wait_ge(s_sig, 1)
                then(nc.vector.scalar_tensor_tensor(sx[:, 0:1], gmax[:, 0:1], 1.0 / QMAX, clip[:, 0:1], ALU.mult, ALU.mult))
                then(nc.vector.reciprocal(sinv[:, 0:1], sx[:, 0:1]))
                then(nc.vector.tensor_scalar(wsc[:, 0:12], wsc[:, 0:12], sx[:, 0:1], None, ALU.mult))
                for i in range(NB):
                    v = xn[:, i * TB:(i + 1) * TB, :].rearrange("p t d -> p (t d)")
                    then(nc.vector.tensor_scalar(v, v, sinv[:, 0:1], MAGIC, ALU.mult, ALU.add))
                    then(nc.vector.tensor_scalar(v, v, MAGIC - QMAX - 1.0, MAGIC + QMAX, ALU.max, ALU.min))
                    nc.vector.tensor_scalar(v, v, MAGIC, None, ALU.subtract).then_inc(s_xq, 1)

        with ExitStack() as ctx:
            sem = lambda n: ctx.enter_context(nc.semaphore("q2_" + n))
            gate = ctx.enter_context(nc.sbuf_tensor("q2_gate", [P, 3, BLK], F32))
            s_gu, s_gate, s_h, s_max = (sem(n) for n in ("gu", "gate", "h", "max"))
            block = ctx.enter_context(nc.Block())

            @block.tensor
            def _(pe):
                def one_block(i):
                    for c, (lo, w) in enumerate(QCH):
                        pair = 2 * (c % 3)
                        wait(pe, s_h, NQ * i + c - 2)
                        for m in range(2):
                            for kc in range(KD):
                                mm = nc.tensor.matmul(k.ps[0:w, pair + m, :], wguT[:, m, kc, lo:lo + w],
                                                      xqT[:, kc, ds(i * BLK, BLK)], start=kc == 0, stop=kc == KD - 1)
                        mm.then_inc(s_gu, 1)

                peeled(pe, NB, one_block)

            @block.scalar
            def _(act):
                def one_block(i):
                    for c, (lo, w) in enumerate(QCH):
                        act.wait_ge(s_gu, NQ * i + c + 1)
                        wait(act, s_h, NQ * i + c - 2)
                        nc.scalar.activation(gate[0:w, c % 3, :], k.ps[0:w, 2 * (c % 3), :], ACT.Silu,
                                             scale=wsc[0:w, c:c + 1]).then_inc(s_gate, 1)

                peeled(act, NB, one_block)

            @block.vector
            def _(dve):
                nc.vector.memset(hmax[:], 0.0).then_inc(s_max, 1)
                dve.wait_ge(s_max, 1)
                def largest(i, c):
                    w = QCH[c][1]
                    dve.wait_ge(s_h, NQ * i + c + 1)
                    nc.vector.tensor_reduce(hmax[0:w, ds(NQ * i + c, 1)], hF[0:w, c, ds(i * BLK, BLK)], AX, ALU.max,
                                            apply_absolute_value=True).then_inc(s_max, 1)

                with dve.Fori(0, NB) as i:
                    for c, (lo, w) in enumerate(QCH):
                        dve.wait_ge(s_gate, NQ * i + c + 1)
                        nc.vector.scalar_tensor_tensor(hF[0:w, c, ds(i * BLK, BLK)], k.ps[0:w, 2 * (c % 3) + 1, :], wsc[0:w, NQ + c:NQ + c + 1],
                                                       gate[0:w, c % 3, :], ALU.mult, ALU.mult).then_inc(s_h, 1)
                        if c:
                            largest(i, c - 1)
                    largest(i, NQ - 1)

        with ExitStack() as ctx:
            sem = lambda n: ctx.enter_context(nc.semaphore("q3_" + n))
            pmax = ctx.enter_context(nc.sbuf_tensor("q3_pmax", [P, 1], F32))
            hq = ctx.enter_context(nc.sbuf_tensor("q3_hq", [P, NQ, T], BF16))
            y = ctx.enter_context(nc.sbuf_tensor("q3_y", [P, NT, D], F32))
            s_pmax, s_gmax, s_step, s_rnd, s_clip, s_hq, s_y, s_t, s_out = (sem(n) for n in ("pmax", "gmax", "step", "rnd", "clip", "hq", "y", "t", "out"))
            s_res, s_last = sem("res"), sem("last")
            block = ctx.enter_context(nc.Block())

            @block.gpsimd
            def _(pool):
                pool.wait_ge(s_pmax, 1)
                nc.gpsimd.partition_all_reduce(gmax[:, 1:2], pmax[:], P, RMAX).then_inc(s_gmax, 1)
                pool.wait_ge(s_gmax, 1)
                with pool.Fori(0, NT - TB) as t:
                    pool.wait_ge(s_t, t + 1)
                    nc.gpsimd.tensor_tensor(y[:, ds(t, 1), :], y[:, ds(t, 1), :], k.X[:, ds(t, 1), :], ALU.add).then_inc(s_res, 1)

            @block.vector
            def _(dve):
                nc.vector.tensor_reduce(pmax[:], hmax[:], AX, ALU.max).then_inc(s_pmax, 1)
                dve.wait_ge(s_gmax, 1)
                nc.vector.scalar_tensor_tensor(sx[:, 1:2], gmax[:, 1:2], 1.0 / QMAX, clip[:, 1:2], ALU.mult, ALU.mult).then_inc(s_step, 1)
                dve.wait_ge(s_step, 1)
                nc.vector.reciprocal(sinv[:, 1:2], sx[:, 1:2]).then_inc(s_step, 1)
                dve.wait_ge(s_step, 2)
                nc.vector.tensor_scalar(drow[:], drow[:], sx[:, 1:2], None, ALU.mult).then_inc(s_step, 1)
                def scaled(i):
                    for c, (lo, w) in enumerate(QCH):
                        v = hF[0:w, c, i * BLK:(i + 1) * BLK]
                        nc.vector.tensor_scalar(v, v, sinv[0:w, 1:2], MAGIC, ALU.mult, ALU.add).then_inc(s_rnd, 1)
                    for c, (lo, w) in enumerate(QCH):
                        v = hF[0:w, c, i * BLK:(i + 1) * BLK]
                        dve.wait_ge(s_rnd, NQ * i + c + 1)
                        nc.vector.tensor_scalar(v, v, MAGIC - QMAX - 1.0, MAGIC + QMAX, ALU.max, ALU.min).then_inc(s_clip, 1)

                def products(i):
                    for t in range(i * TB, (i + 1) * TB):
                        dve.wait_ge(s_y, t + 1)
                        nc.vector.tensor_tensor(y[:, t, :], k.ps[:, t % 8, 0:D], drow[:], ALU.mult).then_inc(s_t, 1)
                        if i == NB - 1:
                            dve.wait_ge(s_t, t + 1)
                            nc.vector.tensor_tensor(y[:, t, :], y[:, t, :], k.X[:, t, :], ALU.add).then_inc(s_last, 1)

                scaled(0)
                scaled(1)
                dve.wait_ge(s_step, 3)
                for i in range(2, NB):
                    scaled(i)
                    products(i - 2)
                products(NB - 2)
                products(NB - 1)

            @block.scalar
            def _(act):
                for i in range(NB):
                    for c, (lo, w) in enumerate(QCH):
                        act.wait_ge(s_clip, NQ * i + c + 1)
                        nc.scalar.activation(hq[0:w, c, i * BLK:(i + 1) * BLK], hF[0:w, c, i * BLK:(i + 1) * BLK], ACT.Copy,
                                             bias=-MAGIC).then_inc(s_hq, 1)

            @block.tensor
            def _(pe):
                for t in range(NT):
                    pe.wait_ge(s_hq, NQ * (t // TB + 1))
                    if t >= 8:
                        pe.wait_ge(s_t, t - 7)
                    for c, (lo, w) in enumerate(QCH):
                        mm = nc.tensor.matmul(k.ps[:, t % 8, 0:D], hq[0:w, c, t * P:(t + 1) * P], wdT[0:w, c, :],
                                              start=c == 0, stop=c == NQ - 1)
                    mm.then_inc(s_y, 1)

            @block.sync
            def _(sp):
                o = out.rearrange("(n p) d -> p n d", p=P)
                for i in range(NB):
                    if i < NB - 1:
                        sp.wait_ge(s_res, TB * (i + 1))
                    else:
                        sp.wait_ge(s_last, TB)
                    sp.dma_start(o[:, i * TB:(i + 1) * TB, :], y[:, i * TB:(i + 1) * TB, :]).then_inc(s_out, 16)
                sp.wait_ge(s_out, 16 * NB)
def build(nc, a, out, stop=None):
    with ExitStack() as ctx:
        def sb(name, shape, dt=F32):
            return ctx.enter_context(nc.sbuf_tensor(name, shape, dt))

        k = Shared()
        k.X = sb("X", [P, NT, D])
        k.nT = [sb("nT_high", [P, KD, T], F16), sb("nT_low", [P, KD, T], F16)]
        k.sw = [sb("sw_high", [P, NSW], F16), sb("sw_low", [P, NSW], F16)]
        k.ident, k.identb, k.iota = sb("ident", [P, P]), sb("identb", [P, P], BF16), sb("iota", [P, S])
        k.endT, k.qcol = sb("endT", [P, KD, B]), sb("qcol", [P, KD])
        k.half, k.ones = sb("half", [P, NT]), sb("ones", [P, 32])
        k.ones16 = sb("ones16", [P, P], BF16)
        k.st, k.mv = sb("st", [P, NT, 6]), sb("mv", [P, NT, 2])
        k.r1, k.fac = sb("r1", [P, NT]), sb("fac", [P, NT])
        k.V = sb("V", [P, NT, D])
        k.mask_col, k.wexp = sb("mask_col", [P, NT]), sb("wexp", [P, NT, EA])
        dram = lambda n, s, d: nc.dram_tensor(n, s, d, kind="Internal").ap()
        k.xqk, k.mqk = dram("xqk", (2, 8, 2 * 32, T), F16), dram("mqk", (2, 16, 2 * 16, T), F16)
        k.negmask = dram("negmask", (B, S), F16)
        k.patch_sum = dram("patch_sum", (P, NT, D), F32)
        k.wq, k.wsc_row = dram("wq", (P, NW), BF16), dram("wsc_row", (1, D), F32)
        k.wsc = sb("wsc", [P, 14])
        k.vec = sb("vec", [P, 14])
        k.rows = sb("rows", [P, 6, D])
        k.ps = ctx.enter_context(nc.psum_tensor("ps", [P, 8, 512], F32))

        def clear_semaphores():
            with nc.Block() as block:
                @block.gpsimd
                def _(pool):
                    pool.sem_clear(range(first, 256))

        with nc.semaphore("first") as f:
            first = f.num
        stages = [
            ("ssm", lambda: ssm_layer(nc, k, a)),
            ("xat", lambda: cross_attention(nc, k, a)),
            ("moe", lambda: experts(nc, k, a)),
            ("clear", clear_semaphores),
            ("mha", lambda: self_attention(nc, k, a)),
            ("dep", lambda: depool(nc, k, a)),
            ("ffn", lambda: quant_ffn(nc, k, a, out)),
        ]
        for name, stage in stages:
            stage()
            if name == stop and name != "ffn":
                with nc.semaphore("dbg") as s, nc.Block() as block:
                    @block.sync
                    def _(sp):
                        sp.dma_start(out.rearrange("(n p) d -> p n d", p=P), k.X[:]).then_inc(s, 16)
                        sp.wait_ge(s, 16)
                return


def lay_out(i):
    g = {n: np.asarray(v) for n, v in i.items()}
    f = np.float32

    def chunks(w):
        kk, m = w.shape
        return w.reshape(kk // P, P, m).transpose(1, 0, 2).reshape(P, -1)

    heads = lambda w: w.transpose(1, 0, 2).reshape(D, D)
    mo = np.zeros((16, 32, D), f)
    mo[:, :16] = g["L1_attn_W_out"]
    sw = np.concatenate([chunks(w) for w in (
        g["L0_attn_W_alpha_w"].T, g["L0_attn_W_B_w"].T, g["L0_attn_W_C_w"].T,
        g["L0_xattn_W_src"].T, g["L0_xattn_W_tgt"].T, g["L0_xattn_W_out"].T,
        heads(g["L1_attn_W_query"]), heads(g["L1_attn_W_key"]), heads(g["L1_attn_W_val"]),
        mo.reshape(512, D), g["L1_xattn_W_in"].T, g["L0_ffn_Wg"])], axis=1)
    up = lambda w, s: np.concatenate([w, s.reshape(D, 2, H).transpose(1, 0, 2)])
    w1, w2 = up(g["L0_ffn_W1"], g["L0_ffn_Ws1"]), up(g["L0_ffn_W2"], g["L0_ffn_Ws2"])
    w3 = np.zeros((EA, NHC * P, D), f)
    w3[:E, :H] = g["L0_ffn_W3"]
    w3[E:, :H] = g["L0_ffn_Ws3"].reshape(2, H, D)
    mw = np.concatenate([chunks(m[e]) for e in range(EA) for m in (w1, w2, w3)], axis=1)
    vec = np.concatenate([g[n][:D].reshape(2, P).T for n in (
        "L0_attn_ln_w", "L0_attn_ln_b", "L0_attn_W_alpha_b", "L0_attn_W_B_b", "L0_xattn_b_tgt",
        "L0_xattn_b_src", "L1_xattn_g_res")], axis=1)
    rows = np.stack([g["L0_attn_W_C_b"], g["L0_attn_D_param"], g["L0_xattn_b_src"][D:], g["L0_xattn_b_out"],
                     g["L1_xattn_b_in"], g["L1_xattn_g_init"][:D]])

    def rowtiles(w):
        o = np.zeros((P, len(QCH), D), f)
        for c, (lo, n) in enumerate(QCH):
            o[:n, c] = w[lo:lo + n]
        return o

    return {k: np.ascontiguousarray(v) for k, v in {
        "x": g["x"].reshape(T, D), "sw": sw, "mw": mw, "vec": vec, "rows": rows,
        "ctxT": g["ctx_2048"].reshape(T, KC, P).transpose(2, 1, 0), "ctx": g["ctx_2048"].reshape(T, CD),
        "mask": g["mask_BxS2_fk1"], "maskT": g["mask_BxS2_fk1"].reshape(NT, P).T, "patch": g["mask_BxS2_if0"],
        "wgate": rowtiles(g["L1_ffn_w_gate"]), "wup": rowtiles(g["L1_ffn_w_up"]),
        "wdown": g["L1_ffn_w_down"].reshape(KD, P, HS).transpose(1, 0, 2),
        "clip": np.stack([g["L1_ffn_clip_x"], g["L1_ffn_clip_down"]], axis=1),
    }.items()}


def program(nc, arrays, stop=None):
    a = {n: nc.dram_tensor("in_" + n, v.shape, mybir.dt.from_np(v.dtype), kind="ExternalInput").ap() for n, v in arrays.items()}
    out = nc.dram_tensor("y", (T, D), F32, kind="ExternalOutput").ap()
    build(nc, a, out, stop)
    return nc


def kernel(**inputs):
    import concourse.bacc as _bacc
    from concourse.bass_utils import run_bass_kernel_spmd as _run

    arrays = lay_out(inputs)
    nc = _bacc.Bacc("TRN2", target_bir_lowering=False, num_devices=1)
    program(nc, arrays)
    r = _run(nc, [{"in_" + n: v for n, v in arrays.items()}], core_ids=[0])
    return r.results[0]["y"].reshape(B, S, D)
```
